# Optimizing a Trainium2 kernel written in Bass

```python
import numpy as np
import jax
import jax.numpy as jnp

def _softmax(x, axis=-1):
    return jax.nn.softmax(x, axis=axis)

def _gelu(x):
    return jax.nn.gelu(x, approximate=True)

def _silu(x):
    return jax.nn.silu(x)

def _sigmoid(x):
    return jax.nn.sigmoid(x)

def _layernorm(x, axis=-1, eps=1e-05):
    m = jnp.mean(x, axis=axis, keepdims=True)
    v = jnp.var(x, axis=axis, keepdims=True)
    return (x - m) / jnp.sqrt(v + eps)

def _scatter_add(tgt, idx, src, axis=0):
    return tgt.at[idx].add(src)

def _segment_sum(src, seg, n):
    return jax.ops.segment_sum(src, seg, n)
kernel_name = 'mk_adj_preln_d4_adj_r2_88bc3b'

def setup_inputs(seed: int=0):
    np.random.seed(seed)
    _w = jnp.asarray

    def _rec_inputs():
        import jax
        import jax.numpy as jnp
        _gk = jax.random.key(seed)
        x = 7.22e-05 + 1 * jax.random.normal(jax.random.fold_in(_gk, 1), (1354, 512), jnp.float32)
        _a = jax.random.bernoulli(jax.random.fold_in(_gk, 2), 0.0118168, (1354, 1354))
        _a = jnp.logical_or(_a, jnp.swapaxes(_a, -1, -2))
        _a = jnp.logical_or(_a, jnp.eye(1354, dtype=bool))
        _af = _a.astype(jnp.float32)
        _d = jnp.maximum(_af.sum(-1), 1.0) ** (-0.5)
        _af = _af * _d[..., :, None] * _d[..., None, :]
        adj = _af
        return (x, adj)
    x, adj = _rec_inputs()

    def _L0_gnn_setup():
        import jax, jax.numpy as jnp
        import numpy as np
        N = 4096
        D = 512

        def adjacent_mat(adj):
            adj = adj + jnp.eye(adj.shape[0], dtype=adj.dtype)
            deg = jnp.sum(adj, axis=1)
            dinv = jnp.where(deg > 0, deg ** (-0.5), 0.0).astype(adj.dtype)
            return dinv[:, None] * adj * dinv[None, :]
        key = jax.random.key(seed)
        k1, k2 = jax.random.split(key)
        x = jax.random.normal(k1, (N, D), dtype=jnp.float32)
        Coefficient2 = 1e-08 * jnp.ones((N, N), dtype=jnp.float32)
        A = jax.random.uniform(k2, (N, N), dtype=jnp.float32)
        return {'x': x, 'Coefficient2': Coefficient2, 'A': A}
    _L0_gnn_all = _L0_gnn_setup()
    _L0_gnn_in = {k: v for k, v in _L0_gnn_all.items() if k in ()}
    del _L0_gnn_all

    def _L1_gnn_setup():
        import jax, jax.numpy as jnp
        import numpy as np
        NBITS = 4
        N_NODES = 4096
        IN_F = 512
        OUT_F = 512

        def _act_quant(x, alpha, b):
            n = float(2 ** b - 1)
            xd = x / alpha
            xc = jnp.minimum(xd, 1.0)
            xq = jnp.round(xc * n) / n
            return xq * alpha

        def _weight_quant(w, alpha, b):
            n = float(2 ** b - 1)
            wd = w / alpha
            wc = jnp.clip(wd, -1.0, 1.0)
            wq = jnp.round(jnp.abs(wc) * n) / n * jnp.sign(wc)
            return wq * alpha
        key = jax.random.key(seed)
        k1, k2, k3 = jax.random.split(key, 3)
        stdv = 1.0 / np.sqrt(OUT_F)
        inp = {'input': jax.random.uniform(k1, (N_NODES, IN_F), dtype=jnp.float32), 'adj': jax.random.uniform(k2, (N_NODES, N_NODES), dtype=jnp.float32), 'adj_scaling_factor': jnp.float32(2.0), 'weight': jax.random.uniform(k3, (IN_F, OUT_F), minval=-stdv, maxval=stdv, dtype=jnp.float32), 'wgt_alpha': jnp.float32(3.0), 'act_alpha': jnp.float32(1.0), 'act_alpha2': jnp.float32(1.0)}
        return inp
    _L1_gnn_all = _L1_gnn_setup()
    _L1_gnn_in = {k: v for k, v in _L1_gnn_all.items() if k in ('adj_scaling_factor', 'weight', 'wgt_alpha', 'act_alpha', 'act_alpha2')}
    del _L1_gnn_all

    def _L2_gnn_setup():
        import jax, jax.numpy as jnp
        import numpy as np
        D_IN, D_ATTN, STEPS = (512, 64, 2)
        P_TOP, TAU, LN_EPS = (0.9, 1.0, 1e-05)
        N = 2048

        def _xavier(key, shape):
            fan_in, fan_out = (shape[0], shape[1])
            lim = jnp.sqrt(6.0 / (fan_in + fan_out))
            return jax.random.uniform(key, shape, jnp.float32, -lim, lim)

        def _adj_from_feats(Xa, W1, W2, W3):
            Q = Xa @ W1
            K = Xa @ W3
            logits = Q @ W2 @ K.T / TAU
            n = logits.shape[1]
            order = jnp.argsort(-logits, axis=1)
            vals = jnp.take_along_axis(logits, order, axis=1)
            probs = jax.nn.softmax(vals, axis=1)
            csum = jnp.cumsum(probs, axis=1)
            k_i = jnp.sum(csum < P_TOP, axis=1) + 1
            keep = jnp.arange(n)[None, :] < k_i[:, None]
            masked_sorted = jnp.where(keep, vals, -jnp.inf)
            rows = jnp.arange(n)[:, None]
            masked = jnp.full_like(logits, -jnp.inf).at[rows, order].set(masked_sorted)
            return jax.nn.softmax(masked, axis=1)
        key = jax.random.key(seed)
        ks = jax.random.split(key, 12)
        X = jax.random.normal(ks[0], (N, D_IN), jnp.float32)
        S = jax.random.uniform(ks[1], (N, N), jnp.float32)
        W1 = _xavier(ks[2], (D_IN, D_ATTN))
        W3 = _xavier(ks[3], (D_IN, D_ATTN))
        W2 = _xavier(ks[4], (D_ATTN, D_ATTN))
        U1_0 = _xavier(ks[5], (D_IN, D_IN))
        U1_1 = _xavier(ks[6], (D_IN, D_IN))
        U2_0 = _xavier(ks[7], (D_IN, D_IN))
        U2_1 = _xavier(ks[8], (D_IN, D_IN))
        gamma = jnp.ones((D_IN,), jnp.float32)
        beta = jnp.zeros((D_IN,), jnp.float32)
        return {'X': X, 'S': S, 'W1': W1, 'W2': W2, 'W3': W3, 'U1_0': U1_0, 'U1_1': U1_1, 'U2_0': U2_0, 'U2_1': U2_1, 'gamma': gamma, 'beta': beta}
    _L2_gnn_all = _L2_gnn_setup()
    _L2_gnn_in = {k: v for k, v in _L2_gnn_all.items() if k in ('W1', 'W2', 'W3', 'U1_0', 'U1_1', 'U2_0', 'U2_1', 'gamma', 'beta')}
    del _L2_gnn_all

    def _L3_gnn_setup():
        import jax, jax.numpy as jnp
        import numpy as np
        ALPHA = 0.2
        NEG = -9000000000000000.0
        N, NFEAT, NHID, NHEADS = (2048, 512, 64, 8)
        EMB = NHID * NHEADS
        key = jax.random.key(seed)
        ks = jax.random.split(key, 16)
        x = jax.random.normal(ks[0], (N, NFEAT), dtype=jnp.float32)
        adj = (jax.random.uniform(ks[1], (N, N)) < 0.01).astype(jnp.float32)
        adj = jnp.maximum(adj, jnp.eye(N, dtype=jnp.float32))
        s = 0.05
        W = jax.random.normal(ks[2], (NHEADS, NFEAT, NHID), dtype=jnp.float32) * s
        a1 = jax.random.normal(ks[3], (NHEADS, NHID), dtype=jnp.float32) * s
        a2 = jax.random.normal(ks[4], (NHEADS, NHID), dtype=jnp.float32) * s
        W1 = jax.random.normal(ks[5], (EMB // 2, EMB), dtype=jnp.float32) * s
        b1 = jnp.zeros((EMB // 2,), dtype=jnp.float32)
        W2 = jax.random.normal(ks[6], (NFEAT // 4, EMB // 2), dtype=jnp.float32) * s
        b2 = jnp.zeros((NFEAT // 4,), dtype=jnp.float32)
        W3 = jax.random.normal(ks[7], (NFEAT // 2, NFEAT // 4), dtype=jnp.float32) * s
        b3 = jnp.zeros((NFEAT // 2,), dtype=jnp.float32)
        W4 = jax.random.normal(ks[8], (NFEAT, NFEAT // 2), dtype=jnp.float32) * s
        b4 = jnp.zeros((NFEAT,), dtype=jnp.float32)
        return {'x': x, 'adj': adj, 'W': W, 'a1': a1, 'a2': a2, 'W1': W1, 'b1': b1, 'W2': W2, 'b2': b2, 'W3': W3, 'b3': b3, 'W4': W4, 'b4': b4}
    _L3_gnn_all = _L3_gnn_setup()
    _L3_gnn_in = {k: v for k, v in _L3_gnn_all.items() if k in ('W', 'a1', 'a2', 'W1', 'b1', 'W2', 'b2', 'W3', 'b3', 'W4', 'b4')}
    del _L3_gnn_all
    return {'x': x, 'adj': adj, 'L1_gnn_adj_scaling_factor': _L1_gnn_in['adj_scaling_factor'], 'L1_gnn_weight': _L1_gnn_in['weight'], 'L1_gnn_wgt_alpha': _L1_gnn_in['wgt_alpha'], 'L1_gnn_act_alpha': _L1_gnn_in['act_alpha'], 'L1_gnn_act_alpha2': _L1_gnn_in['act_alpha2'], 'L2_gnn_W1': _L2_gnn_in['W1'], 'L2_gnn_W2': _L2_gnn_in['W2'], 'L2_gnn_W3': _L2_gnn_in['W3'], 'L2_gnn_U1_0': _L2_gnn_in['U1_0'], 'L2_gnn_U1_1': _L2_gnn_in['U1_1'], 'L2_gnn_U2_0': _L2_gnn_in['U2_0'], 'L2_gnn_U2_1': _L2_gnn_in['U2_1'], 'L2_gnn_gamma': _L2_gnn_in['gamma'], 'L2_gnn_beta': _L2_gnn_in['beta'], 'L3_gnn_W': _L3_gnn_in['W'], 'L3_gnn_a1': _L3_gnn_in['a1'], 'L3_gnn_a2': _L3_gnn_in['a2'], 'L3_gnn_W1': _L3_gnn_in['W1'], 'L3_gnn_b1': _L3_gnn_in['b1'], 'L3_gnn_W2': _L3_gnn_in['W2'], 'L3_gnn_b2': _L3_gnn_in['b2'], 'L3_gnn_W3': _L3_gnn_in['W3'], 'L3_gnn_b3': _L3_gnn_in['b3'], 'L3_gnn_W4': _L3_gnn_in['W4'], 'L3_gnn_b4': _L3_gnn_in['b4']}

def reference(x, adj, L1_gnn_adj_scaling_factor, L1_gnn_weight, L1_gnn_wgt_alpha, L1_gnn_act_alpha, L1_gnn_act_alpha2, L2_gnn_W1, L2_gnn_W2, L2_gnn_W3, L2_gnn_U1_0, L2_gnn_U1_1, L2_gnn_U2_0, L2_gnn_U2_1, L2_gnn_gamma, L2_gnn_beta, L3_gnn_W, L3_gnn_a1, L3_gnn_a2, L3_gnn_W1, L3_gnn_b1, L3_gnn_W2, L3_gnn_b2, L3_gnn_W3, L3_gnn_b3, L3_gnn_W4, L3_gnn_b4):
    import jax
    import jax.numpy as jnp

    def _L0_gnn_ref(x, Coefficient2, A):
        import jax, jax.numpy as jnp
        import numpy as np
        N = 4096
        D = 512

        def adjacent_mat(adj):
            adj = adj + jnp.eye(adj.shape[0], dtype=adj.dtype)
            deg = jnp.sum(adj, axis=1)
            dinv = jnp.where(deg > 0, deg ** (-0.5), 0.0).astype(adj.dtype)
            return dinv[:, None] * adj * dinv[None, :]
        A_c = jax.lax.stop_gradient(A)
        adj = adjacent_mat((A_c + A_c.T) * 0.5)
        y = Coefficient2 @ adj
        y = y @ x
        return y

    def _L1_gnn_ref(input, adj, adj_scaling_factor, weight, wgt_alpha, act_alpha, act_alpha2):
        import jax, jax.numpy as jnp
        import numpy as np
        NBITS = 4
        N_NODES = 4096
        IN_F = 512
        OUT_F = 512

        def _act_quant(x, alpha, b):
            n = float(2 ** b - 1)
            xd = x / alpha
            xc = jnp.minimum(xd, 1.0)
            xq = jnp.round(xc * n) / n
            return xq * alpha

        def _weight_quant(w, alpha, b):
            n = float(2 ** b - 1)
            wd = w / alpha
            wc = jnp.clip(wd, -1.0, 1.0)
            wq = jnp.round(jnp.abs(wc) * n) / n * jnp.sign(wc)
            return wq * alpha
        bit = NBITS
        wb = bit - 1
        mean = jax.lax.stop_gradient(jnp.mean(weight))
        std = jax.lax.stop_gradient(jnp.std(weight, ddof=1))
        w_norm = (weight - mean) / std
        weight_q = _weight_quant(w_norm, wgt_alpha, wb)
        x = _act_quant(input, act_alpha, bit)
        wgt_delta = wgt_alpha / (2 ** (bit - 1) - 1)
        act_delta = act_alpha / (2 ** bit - 1)
        support = jnp.matmul(x / act_delta, weight_q / wgt_delta)
        support = support * act_delta * wgt_delta
        support = jax.nn.relu(support)
        support_q = _act_quant(support, act_alpha2, bit)
        support_delta = act_alpha2 / (2 ** bit - 1)
        output = jnp.matmul(adj / adj_scaling_factor, support_q / support_delta)
        return output * adj_scaling_factor * support_delta

    def _L2_gnn_ref(X, S, W1, W2, W3, U1_0, U1_1, U2_0, U2_1, gamma, beta):
        import jax, jax.numpy as jnp
        import numpy as np
        D_IN, D_ATTN, STEPS = (512, 64, 2)
        P_TOP, TAU, LN_EPS = (0.9, 1.0, 1e-05)
        N = 2048

        def _xavier(key, shape):
            fan_in, fan_out = (shape[0], shape[1])
            lim = jnp.sqrt(6.0 / (fan_in + fan_out))
            return jax.random.uniform(key, shape, jnp.float32, -lim, lim)

        def _adj_from_feats(Xa, W1, W2, W3):
            Q = Xa @ W1
            K = Xa @ W3
            logits = Q @ W2 @ K.T / TAU
            n = logits.shape[1]
            order = jnp.argsort(-logits, axis=1)
            vals = jnp.take_along_axis(logits, order, axis=1)
            probs = jax.nn.softmax(vals, axis=1)
            csum = jnp.cumsum(probs, axis=1)
            k_i = jnp.sum(csum < P_TOP, axis=1) + 1
            keep = jnp.arange(n)[None, :] < k_i[:, None]
            masked_sorted = jnp.where(keep, vals, -jnp.inf)
            rows = jnp.arange(n)[:, None]
            masked = jnp.full_like(logits, -jnp.inf).at[rows, order].set(masked_sorted)
            return jax.nn.softmax(masked, axis=1)
        n = X.shape[0]
        S = S + jnp.eye(n, dtype=X.dtype)
        R = S / jnp.clip(S.sum(axis=1, keepdims=True), 1e-12)
        Z = jnp.zeros_like(X)
        Xf, Xa = (X, X)
        U1s, U2s = ((U1_0, U1_1), (U2_0, U2_1))
        for s in range(STEPS):
            A = _adj_from_feats(Xa, W1, W2, W3)
            Xf = R @ Xf
            Xa = A @ Xa
            Z = Z + (Xf @ U1s[s] + Xa @ U2s[s])
        Y = X + Z
        mu = Y.mean(axis=-1, keepdims=True)
        var = Y.var(axis=-1, keepdims=True)
        return (Y - mu) * jax.lax.rsqrt(var + LN_EPS) * gamma + beta

    def _L3_gnn_ref(x, adj, W, a1, a2, W1, b1, W2, b2, W3, b3, W4, b4):
        import jax, jax.numpy as jnp
        import numpy as np
        ALPHA = 0.2
        NEG = -9000000000000000.0
        N, NFEAT, NHID, NHEADS = (2048, 512, 64, 8)
        EMB = NHID * NHEADS
        Wh = jnp.einsum('nf,hfd->hnd', x, W)
        e_src = jnp.einsum('hnd,hd->hn', Wh, a1)
        e_dst = jnp.einsum('hnd,hd->hn', Wh, a2)
        e = jax.nn.leaky_relu(e_src[:, :, None] + e_dst[:, None, :], ALPHA)
        e = jnp.where(adj[None] > 0, e, NEG)
        att = jax.nn.softmax(e, axis=-1)
        h = jnp.einsum('hnm,hmd->hnd', att, Wh)
        h = jax.nn.elu(h)
        enc = jnp.transpose(h, (1, 0, 2)).reshape(x.shape[0], -1)
        out = jax.nn.relu(enc @ W1.T + b1)
        out = jax.nn.relu(out @ W2.T + b2)
        out = jax.nn.relu(out @ W3.T + b3)
        out = out @ W4.T + b4
        return out
    h = jnp.maximum(_layernorm(x, axis=-1), 0.0)
    x = x + _L0_gnn_ref(h, adj, adj)
    h = jnp.maximum(_layernorm(x, axis=-1), 0.0)
    x = x + _L1_gnn_ref(h, adj, L1_gnn_adj_scaling_factor, L1_gnn_weight, L1_gnn_wgt_alpha, L1_gnn_act_alpha, L1_gnn_act_alpha2)
    h = jnp.maximum(_layernorm(x, axis=-1), 0.0)
    x = x + _L2_gnn_ref(h, adj, L2_gnn_W1, L2_gnn_W2, L2_gnn_W3, L2_gnn_U1_0, L2_gnn_U1_1, L2_gnn_U2_0, L2_gnn_U2_1, L2_gnn_gamma, L2_gnn_beta)
    h = jnp.maximum(_layernorm(x, axis=-1), 0.0)
    x = x + _L3_gnn_ref(h, adj, L3_gnn_W, L3_gnn_a1, L3_gnn_a2, L3_gnn_W1, L3_gnn_b1, L3_gnn_W2, L3_gnn_b2, L3_gnn_W3, L3_gnn_b3, L3_gnn_W4, L3_gnn_b4)
    return x

_drawn_inputs = setup_inputs


def setup_inputs(seed=0):
    import zlib

    import numpy as np

    out = dict(_drawn_inputs(seed))
    spreads = {'L2_gnn_gamma': (1.0, 0.2),
     'L2_gnn_beta': (0.0, 0.1),
     'L3_gnn_b1': (0.0, 0.8),
     'L3_gnn_b2': (0.0, 0.719),
     'L3_gnn_b3': (0.0, 0.295),
     'L3_gnn_b4': (0.0, 0.1)}
    factors = {'L3_gnn_W': 2.669, 'L3_gnn_a1': 49.212, 'L3_gnn_a2': 8.0}
    for name, (base, spread) in spreads.items():
        noise = np.random.default_rng([zlib.crc32(name.encode()), seed]).standard_normal(out[name].shape)
        drawn = base * np.exp(spread * noise) if base else spread * noise
        out[name] = jnp.asarray(drawn.astype(out[name].dtype))
    for name, factor in factors.items():
        out[name] = (out[name] * factor).astype(out[name].dtype)
    return out
```

```python
import concourse.bass as bass
from concourse import mybir

F32 = mybir.dt.float32
BF16 = mybir.dt.bfloat16
ALU = mybir.AluOpType
ACT = mybir.ActivationFunctionType
AX_X = mybir.AxisListType.X

N, D, P = 1354, 512, 128
NT = -(-N // P)
NP = NT * P
DC = D // P
HEADS, HD, ATTN = 8, 64, 64
CHUNKS = [(0, 512), (512, 1024), (1024, N)]
MAGIC = 1.5 * 2.0 ** 23
ACT_LEVELS = 15.0
WGT_LEVELS = 7.0
ROUNDS = 24
P_TOP = 0.9
EPS = 1e-5
FAR = -1.0e30
ALPHA = 0.2


def build(nc, ins, out, spill, rows_dram):
    sem_names = """
        const_id0 const_ready x_in scal_in w_in attn_w_in wsum_ready wtot_done wsq_ready wtot2_done w12_done w12_copied sqrt_in sqrt_out link row0_in row1_in deg_done rsum_done l0_staged l0_product l0_scaled l0_half at0_in at1_in p1_product p1_added p2_product p2_added p3_product p3_scaled p3_added p4_product p4_scaled p4_added q_a q_b xi_ready xi_turned xi_copied sup_done sup_a sup_b sup_c q_ready q_staged logits nmax exp_done pt_turned pt_copied att_done ln_stats ln_affine h3_ready h3_kept h3_turned h3_copied g0_done g1_done qk_done g0_kept g1_kept xa_ready0 xa_turned0 xa_copied0 xu_done0 xu_added0 g2_done0 g2_kept0 qk2_done0 qk2_kept0 qk_kept u_in pt_zero x_spilled pick0 pick1 pick2 pick3 pick4 keep_ready gam_in y_ready y_a y_b x3_ready x_back h4_ready h4_turned h4_copied wh_done wh_kept wh_prod wh_es ed_kept ed_turned ed_row wcat_in maskrow0_in maskrow1_in mask_done rows_out db0_in db1_in dmax_step dmax_kept ab_ready ab_turned ab_rows ab_out ab0_in ab1_in wh_staged t_ready p_exp t_masked p_used h0_ready h1_ready ev_a ev_b ev_c ev_exp enc_ready enc_zero mlp_in o1_done o1_kept o2_done o2_kept o3_done o3_kept y4_done out_a out_ready out_stored
    """.split()
    S = {n: nc.alloc_semaphore(n) for n in sem_names}
    for s in range(2):
        for n in ("search_e", "search_s"):
            S[f"{n}{s}"] = nc.alloc_semaphore(f"{n}{s}")
    STAGES = 16
    stage = [nc.alloc_semaphore(f"stage{i}_ended") for i in range(STAGES)]

    WORDS = 53200
    arena = nc.alloc_sbuf_tensor("arena", [P, WORDS], F32)
    at = [0]

    def region(words):
        at[0] += words
        assert at[0] <= WORDS, at[0]
        return at[0] - words

    def view(off, words):
        return arena[:, off:off + words]

    def nodes(off):
        return view(off, NT * D).rearrange("p (t d) -> p t d", d=D)

    oF = [region(NT * D) for _ in range(4)]
    F = [nodes(o) for o in oF]
    oE = region(NT * NP)
    Smat = view(oE, NT * NP).rearrange("p (t n) -> p t n", n=NP)
    E = view(oE, NT * N).rearrange("p (t n) -> p t n", n=N)
    oU = region(4224)
    U = view(oU, 2 * DC * D).rearrange("p (u c d) -> p u c d", u=2, c=DC)
    oST = region(2 * NP)
    ST = [view(oST + b * NP, NP) for b in range(2)]
    STk = [s.rearrange("p (k n) -> p k n", n=P) for s in ST]
    oPT = region(2 * NP)
    PT = [view(oPT + b * NP, NP) for b in range(2)]
    QKT = view(region(NP), NP)
    oHT = region(2 * D)
    HT = [view(oHT + b * D, D) for b in range(2)]
    HTc = [h.rearrange("p (c n) -> p c n", n=P) for h in HT]
    oXA = region(2 * D)
    XA = [view(oXA + b * D, D) for b in range(2)]
    ident = view(region(P), P)
    identb = view(region(P // 2), P // 2).bitcast(BF16)
    ones = view(region(P), P)
    WQK = view(region(DC * P), DC * P).rearrange("p (c m) -> p c m", m=P)
    oQS = region(2 * P)
    QS = [view(oQS + b * P, P) for b in range(2)]
    scal = view(region(8), 8)
    cols = [view(region(NT), NT) for _ in range(18)]
    (deg, dinv, rsum, rinv, lna, lnb, rad, root, nmax, Zs, tau, lo, hi, Fm, mid, ge, kept, rk) = cols
    width = view(region(1), 1)
    small = view(region(16), 16)
    Dst = [view(region(NT), NT) for _ in range(2)]
    Rem = [view(region(1), 1) for _ in range(2)]

    ps = nc.alloc_psum_tensor("ps", [P, 8 * 512], F32)

    def bank(i, w=512):
        return ps[:, i * 512:i * 512 + w]

    wq = view(oF[3], 1024).bitcast(BF16).rearrange("p (c d) -> p c d", d=D)
    XI = [view(oF[3] + 1024 + b * 256, 256).bitcast(BF16) for b in range(2)]
    XIT = [view(oF[3] + 1536 + b * 256, 256).bitcast(BF16) for b in range(2)]
    QT = [view(oF[3] + 2048 + b * 512, 512) for b in range(2)]
    SQ = [view(oF[3] + 3072 + b * 512, 512) for b in range(2)]
    w_raw = view(oU, 2048)
    w_cen = view(oU + 2048, 2048)
    w1t = view(oPT, D)[0:ATTN, :]
    w2 = view(oPT + D, ATTN)[0:ATTN, :]
    stats = view(oQS, 6 * NT).rearrange("p (t s) -> p t s", s=6)
    lt = [view(oQS + 80 + i * NT, NT) for i in range(4)]

    mneg = view(oE, NT * NP // 2).bitcast(BF16).rearrange("p (t n) -> p t n", n=NP)
    maskT = view(oE + NT * NP // 2, NT * NP // 2).bitcast(BF16).rearrange("p (t n) -> p t n", n=NP)
    gamma_b = view(oE, D)
    beta_b = view(oE + D, D)
    Wcat = view(oU, 2048).rearrange("p (c d) -> p c d", d=D)
    a1b = view(oU + 2048, D)
    a2b = view(oU + 2560, D)
    Wh = F[1]
    prod = view(oU + 3072, D)
    encT = view(oF[2], DC * NP).rearrange("p (c n) -> p c n", n=NP)
    AB = [[view(oF[3] + (2 * b + i) * NP, N) for i in range(2)] for b in range(2)]
    DB = [view(oF[3] + b * NP, N) for b in range(2)]
    WS = [view(oU + b * NP, NP).rearrange("p (k m) -> p k m", m=P) for b in range(2)]
    oC = oF[2]
    junk = [view(o + i * 704, N // 2).bitcast(BF16) for o, m in ((oST, 8), (oF[3] + 2 * NP, 4)) for i in range(m)]
    TP = [view(oST + b * NP, N) for b in range(2)]
    PP = [view(oPT + b * NP, N) for b in range(2)]
    evA = QKT[0:HD, 0:N]
    evB = view(oHT, 2 * D + 2 * D)[0:HD, 0:N]
    es = view(oC, NT * HEADS).rearrange("p (t h) -> p t h", h=HEADS)
    edst = [view(oC + 100 + 8 * b, 8) for b in range(2)]
    oL = region(3 * NT * HEADS)
    ed = view(oL, NT * HEADS).rearrange("p (t h) -> p t h", h=HEADS)
    ed8 = view(oL + 88, NT * HEADS).rearrange("p (t h) -> p t h", h=HEADS)
    ed2 = view(oL + 176, NT * HEADS).rearrange("p (t h) -> p t h", h=HEADS)
    Dm = view(oC + 200, NT * HEADS).rearrange("p (t h) -> p t h", h=HEADS)
    c1 = view(oC + 300, NT * HEADS).rearrange("p (t h) -> p t h", h=HEADS)
    c2 = view(oC + 400, NT * HEADS).rearrange("p (t h) -> p t h", h=HEADS)
    abc = view(oC + 500, NT * 16).rearrange("p (t j) -> p t j", j=16)
    o1T = view(oE, 2 * NP).rearrange("p (m n) -> p m n", n=NP)
    o2T = view(oE + 2 * NP, NP)
    o3T = view(oE + 3 * NP, 2 * NP).rearrange("p (m n) -> p m n", n=NP)
    m1 = view(oF[3], 1024).rearrange("p (c m) -> p c m", m=256)
    m2 = view(oF[3] + 1024, 256).rearrange("p (c m) -> p c m", m=128)
    m3 = view(oF[3] + 1280, 256)
    m4 = view(oF[3] + 1536, 1024).rearrange("p (c m) -> p c m", m=512)
    b4b = view(oF[3] + 2560, 512)
    bcols = view(oF[3] + 3072, 8)

    def tiles(body):
        def run(e):
            body(0, 0, 0)
            body(1, 1, 0)
            with e.Fori(1, NT // 2) as p:
                body(2 * p, 0, p)
                body(2 * p + 1, 1, p)
            body(NT - 1, 0, NT // 2)
        return run

    def two_back(e, sem, t, base=0):
        if not isinstance(t, int) or t >= 2:
            e.wait_ge(sem, t + (base - 1))

    def col(c, t):
        return c[:, bass.ds(t, 1)]

    def end_stage(e, i):
        e.drain().then_inc(stage[i], 1)
        e.wait_ge(stage[i], 5)

    block = nc.Block()
    with block:
        @block.sync
        def _(e):
            def load_at_blocks(product):
                def body(t, b, p):
                    two_back(e, S[product], t)
                    e.dma_start(ST[b], ins["adjT_blocks"][bass.ds(t, 1), :, :].rearrange("o p n -> (o p) n")).then_inc(S[f"at{b}_in"], 16)
                tiles(body)(e)

            e.dma_start(F[0], ins["x"].rearrange("(t p) d -> p t d", p=P)).then_inc(S["x_in"], 16)
            e.dma_start(scal[:, 0:5], ins["scalars"]).then_inc(S["scal_in"], 16)
            e.dma_start(w_raw.rearrange("p (c d) -> p c d", d=D), ins["L1_gnn_weight"].rearrange("(c p) d -> p c d", p=P)).then_inc(S["w_in"], 16)
            e.dma_start(w1t, ins["W1T"]).then_inc(S["attn_w_in"], 16)
            e.dma_start(w2, ins["L2_gnn_W2"]).then_inc(S["attn_w_in"], 16)
            e.dma_start(WQK[:, :, ATTN:], ins["L2_gnn_W3"].rearrange("(c p) m -> p c m", p=P)).then_inc(S["attn_w_in"], 16)
            end_stage(e, 0)

            def rows(t, b, p):
                two_back(e, S["deg_done"], t)
                two_back(e, S["rsum_done"], t)
                e.dma_start(ST[b], ins["adj_rows"][bass.ds(t * P, P), :]).then_inc(S[f"row{b}_in"], 16)
                e.dma_start(PT[b], ins["adjT_rows"][bass.ds(t * P, P), :]).then_inc(S[f"row{b}_in"], 16)
            tiles(rows)(e)
            end_stage(e, 1)
            end_stage(e, 2)
            load_at_blocks("p1_product")
            end_stage(e, 3)
            end_stage(e, 4)
            load_at_blocks("p2_product")
            end_stage(e, 5)
            e.dma_start(spill.rearrange("(t p) d -> p t d", p=P), F[0]).then_inc(S["x_spilled"], 16)
            e.dma_start(U[:, 0], ins["L2_gnn_U1_0"].rearrange("(c p) d -> p c d", p=P)).then_inc(S["u_in"], 16)
            e.dma_start(U[:, 1], ins["L2_gnn_U1_1"].rearrange("(c p) d -> p c d", p=P)).then_inc(S["u_in"], 16)
            e.wait_ge(S["x_spilled"], 16)
            end_stage(e, 6)
            e.dma_start(U[:, 0], ins["L2_gnn_U2_0"].rearrange("(c p) d -> p c d", p=P)).then_inc(S["u_in"], 16)
            e.dma_start(U[:, 1], ins["L2_gnn_U2_1"].rearrange("(c p) d -> p c d", p=P)).then_inc(S["u_in"], 16)
            load_at_blocks("p3_product")
            end_stage(e, 7)
            end_stage(e, 8)
            load_at_blocks("p4_product")
            end_stage(e, 9)
            end_stage(e, 10)
            e.dma_start(gamma_b, ins["gamma_b"]).then_inc(S["gam_in"], 16)
            e.dma_start(beta_b, ins["beta_b"]).then_inc(S["gam_in"], 16)
            e.dma_start(F[1], spill.rearrange("(t p) d -> p t d", p=P)).then_inc(S["x_back"], 16)
            e.dma_start(Wcat, ins["Wcat"].rearrange("(c p) m -> p c m", p=P)).then_inc(S["wcat_in"], 16)
            e.dma_start(a1b, ins["a1_b"]).then_inc(S["wcat_in"], 16)
            e.dma_start(a2b, ins["a2_b"]).then_inc(S["wcat_in"], 16)
            end_stage(e, 11)

            def mask_rows(t, b, p):
                two_back(e, S["mask_done"], t)
                e.dma_start(ST[b], ins["adj_rows"][bass.ds(t * P, P), :]).then_inc(S[f"maskrow{b}_in"], 16)
                e.dma_start(PT[b], ins["adjT_rows"][bass.ds(t * P, P), :]).then_inc(S[f"maskrow{b}_in"], 16)
            tiles(mask_rows)(e)
            end_stage(e, 12)
            end_stage(e, 13)
            e.dma_start(rows_dram[0:8, :], QKT[0:8, :]).then_inc(S["rows_out"], 16)
            e.wait_ge(S["rows_out"], 16)
            for b in range(2):
                e.dma_start(DB[b], rows_dram[b:b + 1, 0:N].to_broadcast([P, N])).then_inc(S[f"db{b}_in"], 16)
            with e.Fori(1, HEADS // 2) as p:
                for b in range(2):
                    e.wait_ge(S["dmax_kept"], 2 * p + b - 1)
                    e.dma_start(DB[b], rows_dram[bass.ds(2 * p + b, 1), 0:N].to_broadcast([P, N])).then_inc(S[f"db{b}_in"], 16)
            e.wait_ge(S["ab_rows"], 1)
            e.dma_start(rows_dram[8:24, :], QKT[0:16, :]).then_inc(S["ab_out"], 16)
            e.wait_ge(S["ab_out"], 16)
            end_stage(e, 14)

            def load_ab(h, b):
                for i in range(2):
                    e.dma_start(AB[b][i], rows_dram[bass.ds(h + 8 + 8 * i, 1), 0:N].to_broadcast([P, N])).then_inc(S[f"ab{b}_in"], 16)
            load_ab(0, 0)
            load_ab(1, 1)
            with e.Fori(1, HEADS // 2) as p:
                for b in range(2):
                    e.wait_ge(S["t_ready"], (2 * p + b - 1) * NT)
                    load_ab(2 * p + b, b)
            end_stage(e, 15)
            e.dma_start(m1, ins["M1"].rearrange("(c p) m -> p c m", p=P)).then_inc(S["mlp_in"], 16)
            e.dma_start(m2, ins["M2"].rearrange("(c p) m -> p c m", p=P)).then_inc(S["mlp_in"], 16)
            e.dma_start(m3, ins["M3"]).then_inc(S["mlp_in"], 16)
            e.dma_start(m4, ins["M4"].rearrange("(c p) m -> p c m", p=P)).then_inc(S["mlp_in"], 16)
            e.dma_start(b4b, ins["b4_b"]).then_inc(S["mlp_in"], 16)
            e.dma_start(bcols[:, 0:5], ins["bcols"]).then_inc(S["mlp_in"], 16)
            e.wait_ge(S["out_ready"], NT)
            e.dma_start(out[0:(NT - 1) * P, :].rearrange("(t p) d -> p t d", p=P), F[0][:, 0:NT - 1, :]).then_inc(S["out_stored"], 16)
            e.dma_start(out[(NT - 1) * P:N, :], F[0][0:N - (NT - 1) * P, NT - 1, :]).then_inc(S["out_stored"], 16)
            e.wait_ge(S["out_stored"], 32)

        @block.gpsimd
        def _(e):
            e.memset(ident, 0.0).then_inc(S["const_id0"], 1)
            e.memset(identb, 0.0).then_inc(S["const_id0"], 1)
            e.memset(ones, 1.0).then_inc(S["const_id0"], 1)
            e.wait_ge(S["const_id0"], 3)
            e.affine_select(out=ident, in_=ident, compare_op=ALU.not_equal, fill=1.0, base=0,
                            pattern=[[-1, P]], channel_multiplier=1).then_inc(S["const_ready"], 1)
            e.affine_select(out=identb, in_=identb, compare_op=ALU.not_equal, fill=1.0, base=0,
                            pattern=[[-1, P]], channel_multiplier=1).then_inc(S["const_ready"], 1)
            for i in range(6):
                end_stage(e, i)

            def keep_h3(t, b, p):
                e.wait_ge(S["h3_ready"], t + 1)
                e.tensor_copy(F[1][:, t, :], XA[b]).then_inc(S["h3_kept"], 1)
            tiles(keep_h3)(e)
            for b in range(2):
                e.memset(PT[b][:, N:NP], 0.0).then_inc(S["pt_zero"], 1)
            end_stage(e, 6)

            def add_g0(t, b, p):
                e.wait_ge(S["p3_scaled"], t + 1)
                e.tensor_tensor(out=F[2][:, t, :], in0=XA[b], in1=F[2][:, t, :], op=ALU.add).then_inc(S["p3_added"], 1)
            tiles(add_g0)(e)
            end_stage(e, 7)
            end_stage(e, 8)

            def add_z(t, b, p):
                e.wait_ge(S["p4_scaled"], t + 1)
                e.tensor_tensor(out=F[0][:, t, :], in0=XA[b], in1=F[0][:, t, :], op=ALU.add).then_inc(S["p4_added"], 1)
            tiles(add_z)(e)
            for i in range(9, 15):
                end_stage(e, i)
            e.memset(encT[:, :, N:NP], 0.0).then_inc(S["enc_zero"], 1)

            def mask_head(g0, first):
                for k in range(NT):
                    e.wait_ge(S["t_ready"], g0 + k + 1)
                    r = (k + first) % 2
                    e.tensor_tensor(out=TP[r], in0=TP[r], in1=maskT[:, k, 0:N], op=ALU.add).then_inc(S["t_masked"], 1)
            with e.Fori(0, HEADS // 2) as p:
                mask_head(2 * p * NT, 0)
                mask_head((2 * p + 1) * NT, 1)
            end_stage(e, 15)

        @block.scalar
        def _(e):
            roots = [0]

            def root_of(width_):
                roots[0] += 1
                e.wait_ge(S["sqrt_in"], roots[0])
                e.activation(root[:, 0:width_], rad[:, 0:width_], ACT.Sqrt).then_inc(S["sqrt_out"], 1)

            root_of(1)
            e.wait_ge(S["w12_done"], 1)
            e.activation(WQK[:, :, 0:ATTN], ps[:, 1024:1024 + DC * ATTN].rearrange("p (c m) -> p c m", m=ATTN), ACT.Copy).then_inc(S["w12_copied"], 1)
            end_stage(e, 0)

            def row_sum(t, b, p):
                e.wait_ge(S[f"row{b}_in"], 32 * (p + 1))
                if not isinstance(t, int) or t >= 1:
                    e.wait_ge(S["rsum_done"], t)
                e.activation(F[2][:, 0:3, :].rearrange("p t d -> p (t d)")[:, 0:NP], ST[b], ACT.Copy, accum_out=col(rsum, t)).then_inc(S["rsum_done"], 1)
            tiles(row_sum)(e)
            root_of(NT)
            end_stage(e, 1)

            def norm_relu(src, dst, aff, ready, i):
                e.wait_ge(S["ln_affine"], i + 1)

                def body(t, b, p):
                    o = dst(t, b)
                    e.activation(o, src[:, t, :], ACT.Relu, scale=col(lna, t), bias=col(lnb, t)).then_inc(S[ready], 1)
                return body

            root_of(NT)
            tiles(norm_relu(F[0], lambda t, b: F[1][:, t, :], 0, "h0_ready", 0))(e)

            def stage_s(t, b, p):
                two_back(e, S["l0_product"], t)
                e.activation(STk[b], Smat[:, :, bass.ds(t * P, P)], ACT.Copy).then_inc(S["l0_staged"], 1)
            tiles(stage_s)(e)
            end_stage(e, 2)
            end_stage(e, 3)
            root_of(NT)
            tiles(norm_relu(F[0], lambda t, b: F[1][:, t, :], 0, "h1_ready", 1))(e)

            def copy_xi(t, b, p):
                e.wait_ge(S["xi_turned"], t + 1)
                two_back(e, S["sup_done"], t)
                e.activation(XIT[b], bank(2 + b, 256).bitcast(BF16), ACT.Copy).then_inc(S["xi_copied"], 1)
            tiles(copy_xi)(e)
            end_stage(e, 4)
            end_stage(e, 5)
            root_of(NT)
            e.wait_ge(S["ln_affine"], 3)

            def h3(t, b, p):
                two_back(e, S["h3_turned"], t)
                two_back(e, S["h3_kept"], t)
                e.activation(XA[b], F[0][:, t, :], ACT.Relu, scale=col(lna, t), bias=col(lnb, t)).then_inc(S["h3_ready"], 1)
                e.wait_ge(S["g1_done"], t + 1)
                e.activation(F[3][:, t, :], bank(1), ACT.Copy).then_inc(S["g1_kept"], 1)
                e.wait_ge(S["qk_done"], t + 1)
                e.activation(QKT[:, bass.ds(t * P, P)], bank(4, P), ACT.Copy).then_inc(S["qk_kept"], 1)
            tiles(h3)(e)
            end_stage(e, 6)

            def softmax(s):
                def body(t, b, p):
                    two_back(e, S["logits"], t, NT * s)
                    e.activation(QS[b][ATTN:, :], QKT[0:ATTN, bass.ds(t * P, P)], ACT.Copy).then_inc(S["q_staged"], 1)
                    e.wait_ge(S["nmax"], NT * s + t + 1)
                    e.activation(E[:, t, :], ps[:, b * 1536:b * 1536 + N], ACT.Exp, bias=col(nmax, t), accum_out=col(Zs, t)).then_inc(S["exp_done"], 1)
                return body

            def scale_product(name):
                def body(t, b, p):
                    e.wait_ge(S[f"{name}_product"], t + 1)
                    two_back(e, S[f"{name}_added"], t)
                    e.activation(XA[b], bank(6 + b), ACT.Identity, scale=col(rinv, t)).then_inc(S[f"{name}_scaled"], 1)
                return body

            def attention(s):
                def body(t, b, p):
                    e.wait_ge(S["pt_turned"], NT * s + t + 1)
                    two_back(e, S["att_done"], t, NT * s)
                    e.activation(ST[b], ps[:, 0:NP], ACT.Copy).then_inc(S["pt_copied"], 1)
                    if s == 0:
                        e.wait_ge(S["xa_turned0"], t + 1)
                        e.activation(HT[0], bank(7), ACT.Copy).then_inc(S["xa_copied0"], 1)
                        e.wait_ge(S["g2_done0"], t + 1)
                        e.activation(F[3][:, t, :], bank(7), ACT.Copy).then_inc(S["g2_kept0"], 1)
                        e.wait_ge(S["qk2_done0"], t + 1)
                        e.activation(QKT[:, bass.ds(t * P, P)], bank(6, P), ACT.Copy).then_inc(S["qk2_kept0"], 1)
                return body

            for s in range(2):
                tiles(softmax(s))(e)
                tiles(scale_product(("p3", "p4")[s]))(e)
                end_stage(e, 7 + 2 * s)
                tiles(attention(s))(e)
                end_stage(e, 8 + 2 * s)
            root_of(NT)
            e.wait_ge(S["ln_affine"], 4)

            def y_norm(t, b, p):
                two_back(e, S["x3_ready"], t)
                e.activation(XA[b], F[0][:, t, :], ACT.Identity, scale=col(lna, t), bias=col(lnb, t)).then_inc(S["y_ready"], 1)
            tiles(y_norm)(e)
            end_stage(e, 11)
            end_stage(e, 12)
            root_of(NT)
            e.wait_ge(S["ln_affine"], 5)

            def h4(t, b, p):
                two_back(e, S["h4_turned"], t)
                e.activation(XA[b], F[0][:, t, :], ACT.Relu, scale=col(lna, t), bias=col(lnb, t)).then_inc(S["h4_ready"], 1)
                e.wait_ge(S["wh_done"], t + 1)
                e.activation(Wh[:, t, :], bank(0), ACT.Copy).then_inc(S["wh_kept"], 1)
                e.wait_ge(S["ed_turned"], t + 1)
                e.activation(QKT[0:8, bass.ds(t * P, P)], bank(5, P)[0:8, :], ACT.Copy).then_inc(S["ed_row"], 1)
            tiles(h4)(e)
            end_stage(e, 13)
            e.wait_ge(S["ab_turned"], 1)
            e.wait_ge(S["rows_out"], 16)
            e.activation(QKT[0:16, :], ps[0:16, 0:NP], ACT.Copy).then_inc(S["ab_rows"], 1)
            end_stage(e, 14)

            def head(h, b, g0, first, wait_two):
                if wait_two:
                    e.wait_ge(S["p_used"], NT * (h - 1))
                e.activation(WS[b][:, :, 0:HD], Wh[:, :, bass.ds(h * HD, HD)], ACT.Copy).then_inc(S["wh_staged"], 1)
                for k in range(NT):
                    r = (k + first) % 2
                    e.wait_ge(S["t_masked"], g0 + k + 1)
                    if not isinstance(h, int) or h > 0 or k >= 2:
                        e.wait_ge(S["p_used"], g0 + k - 1)
                    e.activation(PP[r], TP[r], ACT.Exp, bias=ed2[:, k, bass.ds(h, 1)]).then_inc(S["p_exp"], 1)

            def elu(h):
                e.wait_ge(S["ev_c"], h + 1)
                e.activation(evB, evB, ACT.Exp).then_inc(S["ev_exp"], 1)

            head(0, 0, 0, 0, False)
            head(1, 1, NT, 1, False)
            elu(0)
            with e.Fori(1, HEADS // 2) as p:
                head(2 * p, 0, 2 * p * NT, 0, True)
                elu(2 * p - 1)
                head(2 * p + 1, 1, (2 * p + 1) * NT, 1, True)
                elu(2 * p)
            elu(HEADS - 1)
            end_stage(e, 15)
            e.wait_ge(S["mlp_in"], 96)
            for m in range(2):
                e.wait_ge(S["o1_done"], m + 1)
                e.activation(o1T[:, m, :], ps[:, m * 1536:m * 1536 + NP], ACT.Relu, bias=bcols[:, m:m + 1]).then_inc(S["o1_kept"], 1)
            e.wait_ge(S["o2_done"], 1)
            e.activation(o2T, ps[:, 0:NP], ACT.Relu, bias=bcols[:, 2:3]).then_inc(S["o2_kept"], 1)
            for m in range(2):
                e.wait_ge(S["o3_done"], m + 1)
                off = (1 - m) * 1536
                e.activation(o3T[:, m, :], ps[:, off:off + NP], ACT.Relu, bias=bcols[:, 3 + m:4 + m]).then_inc(S["o3_kept"], 1)

        @block.vector
        def _(e):
            chain = [0]
            roots = [0]

            def link(ins_):
                chain[0] += 1
                ins_.then_inc(S["link"], 1)
                e.wait_ge(S["link"], chain[0])

            def ts(out_, in_, s1, s2, op0, op1=None):
                if op1 is None:
                    return e.tensor_scalar(out_, in_, s1, None, op0)
                return e.tensor_scalar(out_, in_, s1, s2, op0, op1)

            def inverse_root(w, dst):
                r, q = root[:, 0:w], rad[:, 0:w]
                roots[0] += 1
                e.wait_ge(S["sqrt_out"], roots[0])
                link(e.reciprocal(dst, r))
                link(e.tensor_tensor(out=dst, in0=dst, in1=q, op=ALU.mult))
                link(e.tensor_tensor(out=dst, in0=dst, in1=r, op=ALU.add))
                link(ts(dst, dst, 0.5, None, ALU.mult))
                link(e.reciprocal(dst, dst))

            def layer_norm_columns(src, i):
                def st(t, b, p):
                    e.bn_stats(out=stats[:, t, :], in_=src[:, t, :]).then_inc(S["ln_stats"], 1)
                tiles(st)(e)
                e.wait_ge(S["ln_stats"], NT * (i + 1))
                me, se, mo, so = (stats[:, :, j] for j in (1, 2, 4, 5))
                link(e.tensor_tensor(out=lt[0], in0=me, in1=mo, op=ALU.add))
                link(e.tensor_tensor(out=lt[1], in0=me, in1=mo, op=ALU.subtract))
                link(e.tensor_tensor(out=lt[1], in0=lt[1], in1=lt[1], op=ALU.mult))
                link(e.tensor_tensor(out=lt[2], in0=se, in1=so, op=ALU.add))
                link(ts(lt[2], lt[2], 1.0 / D, EPS, ALU.mult, ALU.add))
                e.scalar_tensor_tensor(out=rad, in0=lt[1], scalar=0.25, in1=lt[2], op0=ALU.mult, op1=ALU.add).then_inc(S["sqrt_in"], 1)
                inverse_root(NT, lna)
                e.scalar_tensor_tensor(out=lnb, in0=lt[0], scalar=-0.5, in1=lna, op0=ALU.mult, op1=ALU.mult).then_inc(S["ln_affine"], 1)

            e.wait_ge(S["w_in"], 16)
            e.tensor_reduce(out=small[:, 0:1], in_=w_raw, op=ALU.add, axis=AX_X).then_inc(S["wsum_ready"], 1)
            e.wait_ge(S["wtot_done"], 1)
            link(ts(small[:, 1:2], bank(0, 1), 1.0 / (D * D), None, ALU.mult))
            link(ts(w_cen, w_raw, small[:, 1:2], None, ALU.subtract))
            e.scalar_tensor_tensor(out=w_raw, in0=w_cen, scalar=1.0, in1=w_cen, op0=ALU.mult, op1=ALU.mult,
                                   accum_out=small[:, 2:3]).then_inc(S["wsq_ready"], 1)
            e.wait_ge(S["wtot2_done"], 1)
            ts(rad[:, 0:1], bank(1, 1), 1.0 / (D * D - 1), None, ALU.mult).then_inc(S["sqrt_in"], 1)
            inverse_root(1, small[:, 3:4])
            e.wait_ge(S["scal_in"], 16)
            link(e.reciprocal(small[:, 4:8], scal[:, 0:4]))
            link(ts(w_cen, w_cen, small[:, 3:4], small[:, 5:6], ALU.mult, ALU.mult))
            link(ts(w_cen, w_cen, -1.0, 1.0, ALU.max, ALU.min))
            link(ts(w_cen, w_cen, WGT_LEVELS, MAGIC, ALU.mult, ALU.add))
            link(ts(wq.rearrange("p c d -> p (c d)"), w_cen, MAGIC, None, ALU.subtract))
            link(e.tensor_tensor(out=small[:, 8:9], in0=scal[:, 1:2], in1=scal[:, 2:3], op=ALU.mult))
            link(ts(small[:, 8:9], small[:, 8:9], 1.0 / (ACT_LEVELS * WGT_LEVELS), None, ALU.mult))
            link(e.tensor_tensor(out=small[:, 9:10], in0=scal[:, 0:1], in1=small[:, 4:5], op=ALU.mult))
            link(e.tensor_tensor(out=small[:, 9:10], in0=small[:, 9:10], in1=scal[:, 3:4], op=ALU.mult))
            link(ts(small[:, 9:10], small[:, 9:10], 1.0 / ACT_LEVELS, None, ALU.mult))
            end_stage(e, 0)

            def degrees(t, b, p):
                e.wait_ge(S[f"row{b}_in"], 32 * (p + 1))
                e.scalar_tensor_tensor(out=Smat[:, t, :], in0=ST[b], scalar=0.0, in1=PT[b], op0=ALU.add, op1=ALU.add,
                                       accum_out=col(deg, t)).then_inc(S["deg_done"], 1)
            tiles(degrees)(e)
            e.wait_ge(S["deg_done"], NT)
            link(ts(deg, deg, 0.5, 1.0, ALU.mult, ALU.add))
            e.tensor_scalar(rad, deg, 1e-30, None, ALU.max).then_inc(S["sqrt_in"], 1)
            inverse_root(NT, dinv)
            link(e.scalar_tensor_tensor(out=dinv, in0=deg, scalar=0.0, in1=dinv, op0=ALU.is_gt, op1=ALU.mult))
            e.wait_ge(S["rsum_done"], NT)
            link(ts(rinv, rsum, 1.0, 1e-12, ALU.add, ALU.max))
            link(e.reciprocal(rinv, rinv))
            end_stage(e, 1)

            e.wait_ge(S["x_in"], 16)
            layer_norm_columns(F[0], 0)

            def scale_h(t, b, p):
                e.wait_ge(S["h0_ready"], t + 1)
                ts(F[1][:, t, :], F[1][:, t, :], col(dinv, t), None, ALU.mult).then_inc(S["l0_half"], 1)
            tiles(scale_h)(e)

            def l0_evacuate(t, b, p):
                e.wait_ge(S["l0_product"], t + 1)
                two_back(e, S["l0_scaled"], t)
                e.scalar_tensor_tensor(out=XA[b], in0=bank(b), scalar=0.5, in1=F[1][:, t, :], op0=ALU.mult, op1=ALU.add).then_inc(S["l0_half"], 1)
                e.wait_ge(S["l0_half"], NT + t + 1)
                ts(F[2][:, t, :], XA[b], col(dinv, t), None, ALU.mult).then_inc(S["l0_scaled"], 1)
            tiles(l0_evacuate)(e)
            end_stage(e, 2)

            def add_p1(t, b, p):
                e.wait_ge(S["p1_product"], t + 1)
                e.tensor_tensor(out=F[0][:, t, :], in0=bank(b), in1=F[0][:, t, :], op=ALU.add).then_inc(S["p1_added"], 1)
            tiles(add_p1)(e)
            e.wait_ge(S["p1_added"], NT)
            end_stage(e, 3)

            layer_norm_columns(F[0], 1)

            def quantise(t, b, p):
                e.wait_ge(S["h1_ready"], t + 1)
                ts(QT[b], F[1][:, t, :], small[:, 6:7], 1.0, ALU.mult, ALU.min).then_inc(S["q_a"], 1)
                e.wait_ge(S["q_a"], t + 1)
                ts(SQ[b], QT[b], ACT_LEVELS, MAGIC, ALU.mult, ALU.add).then_inc(S["q_b"], 1)
                e.wait_ge(S["q_b"], t + 1)
                two_back(e, S["xi_turned"], t)
                ts(XI[b], SQ[b], MAGIC, None, ALU.subtract).then_inc(S["xi_ready"], 1)
                e.wait_ge(S["sup_done"], t + 1)
                ts(QT[b], bank(b), small[:, 8:9], 0.0, ALU.mult, ALU.max).then_inc(S["sup_a"], 1)
                e.wait_ge(S["sup_a"], t + 1)
                ts(SQ[b], QT[b], small[:, 7:8], 1.0, ALU.mult, ALU.min).then_inc(S["sup_b"], 1)
                e.wait_ge(S["sup_b"], t + 1)
                ts(QT[b], SQ[b], ACT_LEVELS, MAGIC, ALU.mult, ALU.add).then_inc(S["sup_c"], 1)
                e.wait_ge(S["sup_c"], t + 1)
                ts(F[2][:, t, :], QT[b], MAGIC, None, ALU.subtract).then_inc(S["q_ready"], 1)
            tiles(quantise)(e)
            end_stage(e, 4)

            def add_p2(t, b, p):
                e.wait_ge(S["p2_product"], t + 1)
                e.scalar_tensor_tensor(out=F[0][:, t, :], in0=bank(b), scalar=small[:, 9:10], in1=F[0][:, t, :],
                                       op0=ALU.mult, op1=ALU.add).then_inc(S["p2_added"], 1)
            tiles(add_p2)(e)
            e.wait_ge(S["p2_added"], NT)
            end_stage(e, 5)

            layer_norm_columns(F[0], 2)

            def keep_g0(t, b, p):
                e.wait_ge(S["h3_turned"], t + 1)
                two_back(e, S["qk_done"], t)
                e.tensor_copy(HT[b], bank(2 + b)).then_inc(S["h3_copied"], 1)
                e.wait_ge(S["g0_done"], t + 1)
                e.tensor_copy(F[2][:, t, :], bank(0)).then_inc(S["g0_kept"], 1)
            tiles(keep_g0)(e)
            end_stage(e, 6)

            def row_max(s):
                def body(t, b, p):
                    e.wait_ge(S["logits"], NT * s + t + 1)
                    e.tensor_reduce(out=col(nmax, t), in_=ps[:, b * 1536:b * 1536 + N], op=ALU.max, axis=AX_X, negate=True).then_inc(S["nmax"], 1)
                return body

            def search(s):
                e.wait_ge(S["exp_done"], NT * s + NT)
                link(ts(tau, Zs, P_TOP, None, ALU.mult))
                link(e.memset(lo, 0.0))
                link(e.memset(width, 0.5))
                link(e.memset(mid, 0.5))
                per = 4
                with e.Fori(0, ROUNDS) as r:
                    if True:
                        for t in range(NT):
                            if t >= 2:
                                e.wait_ge(S[f"search_e{s}"], NT * r + (t - 1))
                            e.scalar_tensor_tensor(out=ps[:, t % 2 * 1536:t % 2 * 1536 + N], in0=E[:, t, :], scalar=mid[:, t:t + 1], in1=E[:, t, :],
                                                   op0=ALU.is_gt, op1=ALU.mult, accum_out=Fm[:, t:t + 1]).then_inc(S[f"search_e{s}"], 1)
                        e.wait_ge(S[f"search_e{s}"], NT * r + NT)
                        q = S[f"search_s{s}"]
                        e.tensor_tensor(out=ge, in0=Fm, in1=tau, op=ALU.is_ge).then_inc(q, 1)
                        e.wait_ge(q, per * r + 1)
                        e.scalar_tensor_tensor(out=lo, in0=ge, scalar=width, in1=lo, op0=ALU.mult, op1=ALU.add).then_inc(q, 1)
                        e.wait_ge(q, per * r + 2)
                        ts(width, width, 0.5, None, ALU.mult).then_inc(q, 1)
                        e.wait_ge(q, per * r + 3)
                        ts(mid, lo, width, None, ALU.add).then_inc(q, 1)
                        e.wait_ge(q, per * r + 4)
                link(ts(hi, lo, 2.0 ** -ROUNDS, None, ALU.add))

            def select_and_use(s):
                def body(t, b, p):
                    two_back(e, S["pt_turned"], t, NT * s)
                    Et, Pt, sc = E[:, t, :], PT[b][:, 0:N], ps[:, 1536:1536 + N + 1]
                    e.scalar_tensor_tensor(out=Pt, in0=Et, scalar=col(hi, t), in1=Et, op0=ALU.is_gt, op1=ALU.mult,
                                           accum_out=col(Fm, t)).then_inc(S[f"pick0"], 1)
                    e.wait_ge(S["pick0"], 11 * s + t + 1)
                    e.tensor_tensor(out=Rem[b], in0=col(tau, t), in1=col(Fm, t), op=ALU.subtract).then_inc(S["pick1"], 1)
                    e.scalar_tensor_tensor(out=Et, in0=Et, scalar=col(lo, t), in1=Et, op0=ALU.is_gt, op1=ALU.mult).then_inc(S["pick1"], 1)
                    e.wait_ge(S["pick1"], 22 * s + 2 * t + 2)
                    e.tensor_tensor_scan(sc[:, 1:N + 1], Et, Pt, 0.0, ALU.add, ALU.subtract).then_inc(S["pick2"], 1)
                    e.wait_ge(S["pick2"], 11 * s + t + 1)
                    e.scalar_tensor_tensor(out=Et, in0=sc[:, 0:N], scalar=Rem[b], in1=Et, op0=ALU.is_lt, op1=ALU.mult).then_inc(S["pick3"], 1)
                    e.wait_ge(S["pick3"], 11 * s + t + 1)
                    e.scalar_tensor_tensor(out=Pt, in0=Pt, scalar=1.0, in1=Et, op0=ALU.mult, op1=ALU.max,
                                           accum_out=col(kept, t)).then_inc(S[f"keep_ready"], 1)
                    e.wait_ge(S["keep_ready"], 11 * s + t + 1)
                    e.reciprocal(col(rk, t), col(kept, t)).then_inc(S["pick4"], 1)
                    e.wait_ge(S["pick4"], 11 * s + t + 1)
                    e.wait_ge(S["att_done"], NT * s + t + 1)
                    if s == 0:
                        ts(XA[0], bank(6), col(rk, t), None, ALU.mult).then_inc(S["xa_ready0"], 1)
                        e.wait_ge(S["xu_done0"], t + 1)
                        e.tensor_tensor(out=F[0][:, t, :], in0=bank(6), in1=F[1][:, t, :], op=ALU.add).then_inc(S["xu_added0"], 1)
                    else:
                        e.scalar_tensor_tensor(out=F[0][:, t, :], in0=bank(6), scalar=col(rk, t), in1=F[0][:, t, :],
                                               op0=ALU.mult, op1=ALU.add).then_inc(S["xu_added0"], 1)
                return body

            for s in range(2):
                tiles(row_max(s))(e)
                search(s)
                end_stage(e, 7 + 2 * s)
                link(e.memset(ps[:, 1536:1537], 0.0))
                tiles(select_and_use(s))(e)
                e.wait_ge(S["xu_added0"], NT * (s + 1))
                end_stage(e, 8 + 2 * s)

            layer_norm_columns(F[0], 3)
            e.wait_ge(S["gam_in"], 32)
            e.wait_ge(S["x_back"], 16)

            def finish_y(t, b, p):
                e.wait_ge(S["y_ready"], t + 1)
                e.tensor_tensor(out=XA[b], in0=XA[b], in1=gamma_b, op=ALU.mult).then_inc(S["y_a"], 1)
                e.wait_ge(S["y_a"], t + 1)
                e.tensor_tensor(out=XA[b], in0=XA[b], in1=beta_b, op=ALU.add).then_inc(S["y_b"], 1)
                e.wait_ge(S["y_b"], t + 1)
                e.tensor_tensor(out=F[0][:, t, :], in0=XA[b], in1=F[1][:, t, :], op=ALU.add).then_inc(S["x3_ready"], 1)
            tiles(finish_y)(e)
            e.wait_ge(S["x3_ready"], NT)
            end_stage(e, 11)

            def masks(t, b, p):
                e.wait_ge(S[f"maskrow{b}_in"], 32 * (p + 1))
                ts(mneg[:, t, :], ST[b], 0.0, FAR, ALU.is_le, ALU.mult)
                ts(maskT[:, t, :], PT[b], 0.0, FAR, ALU.is_le, ALU.mult).then_inc(S["mask_done"], 1)
            tiles(masks)(e)
            end_stage(e, 12)

            layer_norm_columns(F[0], 4)
            e.wait_ge(S["wcat_in"], 48)

            def scores(t, b, p):
                e.wait_ge(S["h4_turned"], t + 1)
                two_back(e, S["wh_done"], t)
                e.tensor_copy(HT[b], bank(2 + b)).then_inc(S["h4_copied"], 1)
                e.wait_ge(S["wh_kept"], t + 1)
                for i, (ab, dst) in enumerate(((a1b, es[:, t, :]), (a2b, edst[b]))):
                    e.tensor_tensor(out=prod, in0=Wh[:, t, :], in1=ab, op=ALU.mult).then_inc(S["wh_prod"], 1)
                    e.wait_ge(S["wh_prod"], 2 * t + i + 1)
                    if i:
                        two_back(e, S["ed_turned"], t)
                    e.tensor_reduce(out=dst, in_=prod.rearrange("p (h d) -> p h d", d=HD), op=ALU.add, axis=AX_X).then_inc(S["wh_es"], 1)
                    e.wait_ge(S["wh_es"], 2 * t + i + 1)
                e.tensor_copy(ed[:, t, :], edst[b]).then_inc(S["ed_kept"], 1)
            tiles(scores)(e)
            e.wait_ge(S["ed_kept"], NT)
            for b in range(2):
                link(e.memset(WS[b][:, :, HD:], 1.0))
            end_stage(e, 13)

            def dmax(b):
                for t in range(NT):
                    e.tensor_tensor_reduce(out=junk[t], in0=DB[b], in1=mneg[:, t, 0:N], scale=1.0, scalar=4 * FAR,
                                           op0=ALU.add, op1=ALU.max, accum_out=Dst[b][:, t:t + 1]).then_inc(S["dmax_step"], 1)

            def keep_dmax(h, b):
                e.wait_ge(S["dmax_step"], NT * (h + 1))
                e.tensor_copy(Dm[:, :, bass.ds(h, 1)].rearrange("p t o -> p (t o)"), Dst[b]).then_inc(S["dmax_kept"], 1)

            e.wait_ge(S["db0_in"], 16)
            dmax(0)
            with e.Fori(1, HEADS // 2) as p:
                e.wait_ge(S["db1_in"], 16 * p)
                keep_dmax(2 * p - 2, 0)
                dmax(1)
                e.wait_ge(S["db0_in"], 16 * p + 16)
                keep_dmax(2 * p - 1, 1)
                dmax(0)
            e.wait_ge(S["db1_in"], 16 * (HEADS // 2))
            keep_dmax(HEADS - 2, 0)
            dmax(1)
            keep_dmax(HEADS - 1, 1)
            e.wait_ge(S["dmax_kept"], HEADS)
            link(e.scalar_tensor_tensor(out=Dm, in0=Dm, scalar=0.5 * FAR, in1=Dm, op0=ALU.is_gt, op1=ALU.mult))
            link(e.tensor_tensor(out=c1, in0=Dm, in1=es, op=ALU.add))
            link(e.scalar_tensor_tensor(out=c2, in0=c1, scalar=ALPHA, in1=c1, op0=ALU.mult, op1=ALU.max))
            link(e.tensor_tensor(out=abc[:, :, 0:8], in0=es, in1=c2, op=ALU.subtract))
            link(e.scalar_tensor_tensor(out=abc[:, :, 8:16], in0=es, scalar=ALPHA, in1=c2, op0=ALU.mult, op1=ALU.subtract))
            link(ts(ed8, ed, 1.0 - ALPHA, None, ALU.mult))
            ts(ed2, ed, ALPHA, None, ALU.mult).then_inc(S["ab_ready"], 1)
            end_stage(e, 14)

            def head(h, b, p, g0, first, wait_two):
                e.wait_ge(S[f"ab{b}_in"], 32 * (p + 1))
                for k in range(NT):
                    r = (k + first) % 2
                    if not isinstance(h, int) or h > 0 or k >= 2:
                        e.wait_ge(S["p_exp"], g0 + k - 1)
                    e.scalar_tensor_tensor(out=TP[r], in0=AB[b][0], scalar=ed8[:, k, bass.ds(h, 1)], in1=AB[b][1],
                                           op0=ALU.add, op1=ALU.max).then_inc(S["t_ready"], 1)

            def evacuate(h, b, c):
                o = (b * 3) * 512
                e.wait_ge(S["p_used"], NT * (h + 1))
                if not isinstance(h, int) or h >= 1:
                    e.wait_ge(S["enc_ready"], h)
                e.reciprocal(evA, ps[HD:2 * HD, o:o + N]).then_inc(S["ev_a"], 1)
                e.wait_ge(S["ev_a"], h + 1)
                e.tensor_tensor(out=evA, in0=ps[0:HD, o:o + N], in1=evA, op=ALU.mult).then_inc(S["ev_b"], 1)
                e.wait_ge(S["ev_b"], h + 1)
                ts(evB, evA, 0.0, None, ALU.min).then_inc(S["ev_c"], 1)
                e.wait_ge(S["ev_exp"], h + 1)
                dst = encT[b * HD:(b + 1) * HD, c, 0:N]
                e.scalar_tensor_tensor(out=dst, in0=evB, scalar=-1.0, in1=evA, op0=ALU.add, op1=ALU.max).then_inc(S["enc_ready"], 1)

            head(0, 0, 0, 0, 0, False)
            head(1, 1, 0, NT, 1, False)
            evacuate(0, 0, 0)
            with e.Fori(1, HEADS // 2) as p:
                head(2 * p, 0, p, 2 * p * NT, 0, True)
                evacuate(2 * p - 1, 1, p - 1)
                head(2 * p + 1, 1, p, (2 * p + 1) * NT, 1, True)
                evacuate(2 * p, 0, p)
            evacuate(HEADS - 1, 1, HEADS // 2 - 1)
            end_stage(e, 15)

            e.wait_ge(S["mlp_in"], 96)

            def finish(t, b, p):
                e.wait_ge(S["y4_done"], t + 1)
                two_back(e, S["out_ready"], t)
                e.tensor_tensor(out=XA[b], in0=bank(6 + b), in1=b4b, op=ALU.add).then_inc(S["out_a"], 1)
                e.wait_ge(S["out_a"], t + 1)
                e.tensor_tensor(out=F[0][:, t, :], in0=XA[b], in1=F[0][:, t, :], op=ALU.add).then_inc(S["out_ready"], 1)
            tiles(finish)(e)

        @block.tensor
        def _(e):
            def product(acc, lhs, rhs, last_open=False):
                for k in range(NT):
                    last = e.matmul(acc, lhs[:, k, :], rhs[:, k, :], start=(k == 0), stop=(k == NT - 1 and not last_open))
                return last

            def adjacency_product(name, rhs, base_bank, loads_before, free, with_self):
                def body(t, b, p):
                    e.wait_ge(S[f"at{b}_in"], 16 * (loads_before[b] + p + 1))
                    two_back(e, S[free], t)
                    last = product(bank(base_bank + b), STk[b], rhs, with_self)
                    if with_self:
                        last = e.matmul(bank(base_bank + b), ident, rhs[:, t, :], start=False, stop=True)
                    last.then_inc(S[f"{name}_product"], 1)
                return body

            e.wait_ge(S["const_id0"], 3)
            e.wait_ge(S["const_ready"], 2)
            e.wait_ge(S["wsum_ready"], 1)
            e.matmul(bank(0, 1), ones, small[:, 0:1], start=True, stop=True).then_inc(S["wtot_done"], 1)
            e.wait_ge(S["wsq_ready"], 1)
            e.matmul(bank(1, 1), ones, small[:, 2:3], start=True, stop=True).then_inc(S["wtot2_done"], 1)
            e.wait_ge(S["attn_w_in"], 48)
            for c in range(DC):
                last = e.matmul(bank(2)[:, c * ATTN:(c + 1) * ATTN], w1t[:, c * P:(c + 1) * P], w2, start=True, stop=True)
            last.then_inc(S["w12_done"], 1)
            end_stage(e, 0)
            end_stage(e, 1)

            e.wait_ge(S["l0_half"], NT)

            def l0(t, b, p):
                e.wait_ge(S["l0_staged"], t + 1)
                two_back(e, S["l0_scaled"], t)
                product(bank(b), STk[b], F[1]).then_inc(S["l0_product"], 1)
            tiles(l0)(e)
            end_stage(e, 2)
            tiles(adjacency_product("p1", F[2], 0, (0, 0), "p1_added", False))(e)
            end_stage(e, 3)

            def support(t, b, p):
                e.wait_ge(S["xi_ready"], t + 1)
                two_back(e, S["xi_copied"], t)
                for c in range(DC):
                    last = e.transpose(bank(2 + b, 256).bitcast(BF16)[:, c * P:(c + 1) * P], XI[b][:, c * P:(c + 1) * P], identb)
                last.then_inc(S["xi_turned"], 1)
                e.wait_ge(S["xi_copied"], t + 1)
                two_back(e, S["sup_a"], t)
                for c in range(DC):
                    last = e.matmul(bank(b), XIT[b][:, c * P:(c + 1) * P], wq[:, c, :], start=(c == 0), stop=(c == DC - 1))
                last.then_inc(S["sup_done"], 1)
            tiles(support)(e)
            end_stage(e, 4)
            tiles(adjacency_product("p2", F[2], 0, (6, 5), "p2_added", False))(e)
            end_stage(e, 5)

            e.wait_ge(S["u_in"], 32)

            def project(acc, turned, weights):
                for c in range(DC):
                    last = e.matmul(acc, turned[:, c, :], weights[:, c, :], start=(c == 0), stop=(c == DC - 1))
                return last

            def turn(acc, tile):
                for c in range(DC):
                    last = e.transpose(acc[:, c * P:(c + 1) * P], tile[:, c * P:(c + 1) * P], ident)
                return last

            def h3(t, b, p):
                e.wait_ge(S["h3_ready"], t + 1)
                two_back(e, S["h3_copied"], t)
                turn(bank(2 + b), XA[b]).then_inc(S["h3_turned"], 1)
                e.wait_ge(S["h3_copied"], t + 1)
                if not isinstance(t, int) or t >= 1:
                    e.wait_ge(S["g0_kept"], t)
                    e.wait_ge(S["g1_kept"], t)
                    e.wait_ge(S["qk_kept"], t)
                project(bank(0), HTc[b], U[:, 0]).then_inc(S["g0_done"], 1)
                project(bank(1), HTc[b], U[:, 1]).then_inc(S["g1_done"], 1)
                project(bank(4, P), WQK, HTc[b]).then_inc(S["qk_done"], 1)
            tiles(h3)(e)
            end_stage(e, 6)

            def logits(s):
                def body(t, b, p):
                    e.wait_ge(S["q_staged"], NT * s + t + 1)
                    two_back(e, S["exp_done"], t, NT * s)
                    for a, z in CHUNKS:
                        last = e.matmul(ps[:, b * 1536 + a:b * 1536 + z], QS[b][ATTN:, :], QKT[ATTN:, a:z], start=True, stop=True)
                    last.then_inc(S["logits"], 1)
                return body

            def attention(s):
                rhs = (F[1], F[3])[s]

                def body(t, b, p):
                    e.wait_ge(S["keep_ready"], NT * s + t + 1)
                    if not isinstance(t, int) or t >= 1:
                        e.wait_ge(S["pt_copied"], NT * s + t)
                        e.wait_ge(S["xu_added0"], NT * s + t)
                        if s == 0:
                            e.wait_ge(S["g2_kept0"], t)
                            e.wait_ge(S["qk2_kept0"], t)
                    for k in range(NT):
                        last = e.transpose(ps[:, k * P:(k + 1) * P], PT[b][:, k * P:(k + 1) * P], ident)
                    last.then_inc(S["pt_turned"], 1)
                    e.wait_ge(S["pt_copied"], NT * s + t + 1)
                    product(bank(6), STk[b], rhs).then_inc(S["att_done"], 1)
                    if s == 0:
                        e.wait_ge(S["xa_ready0"], t + 1)
                        turn(bank(7), XA[0]).then_inc(S["xa_turned0"], 1)
                        e.wait_ge(S["xa_copied0"], t + 1)
                        project(bank(6), HTc[0], U[:, 0]).then_inc(S["xu_done0"], 1)
                        project(bank(7), HTc[0], U[:, 1]).then_inc(S["g2_done0"], 1)
                        e.wait_ge(S["xu_added0"], t + 1)
                        project(bank(6, P), WQK, HTc[0]).then_inc(S["qk2_done0"], 1)
                return body

            for s in range(2):
                tiles(logits(s))(e)
                tiles(adjacency_product(("p3", "p4")[s], (F[3], F[2])[s], 6, ((12, 10), (18, 15))[s], ("p3_scaled", "p4_scaled")[s], True))(e)
                if s == 0:
                    e.wait_ge(S["u_in"], 64)
                end_stage(e, 7 + 2 * s)
                tiles(attention(s))(e)
                end_stage(e, 8 + 2 * s)
            end_stage(e, 11)
            end_stage(e, 12)
            e.wait_ge(S["wcat_in"], 48)

            def wh(t, b, p):
                e.wait_ge(S["h4_ready"], t + 1)
                two_back(e, S["h4_copied"], t)
                turn(bank(2 + b), XA[b]).then_inc(S["h4_turned"], 1)
                e.wait_ge(S["h4_copied"], t + 1)
                if not isinstance(t, int) or t >= 1:
                    e.wait_ge(S["wh_kept"], t)
                project(bank(0), HTc[b], Wcat).then_inc(S["wh_done"], 1)
                e.wait_ge(S["ed_kept"], t + 1)
                if not isinstance(t, int) or t >= 1:
                    e.wait_ge(S["ed_row"], t)
                e.transpose(bank(5, P)[0:8, :], edst[b], ident).then_inc(S["ed_turned"], 1)
            tiles(wh)(e)
            end_stage(e, 13)
            e.wait_ge(S["ab_ready"], 1)
            for t in range(NT):
                last = e.transpose(ps[0:16, t * P:(t + 1) * P], abc[:, t, :], ident)
            last.then_inc(S["ab_turned"], 1)
            end_stage(e, 14)

            def head(h, b, g0, first, wait_two):
                e.wait_ge(S["wh_staged"], h + 1)
                if wait_two:
                    e.wait_ge(S["enc_ready"], h - 1)
                for k in range(NT):
                    r = (k + first) % 2
                    e.wait_ge(S["p_exp"], g0 + k + 1)
                    for a, z in CHUNKS:
                        last = e.matmul(ps[:, b * 1536 + a:b * 1536 + z], WS[b][:, k, :], PP[r][:, a:z], start=(k == 0), stop=(k == NT - 1))
                    last.then_inc(S["p_used"], 1)
            head(0, 0, 0, 0, False)
            head(1, 1, NT, 1, False)
            with e.Fori(1, HEADS // 2) as p:
                head(2 * p, 0, 2 * p * NT, 0, True)
                head(2 * p + 1, 1, (2 * p + 1) * NT, 1, True)
            end_stage(e, 15)

            e.wait_ge(S["mlp_in"], 96)
            WIDE = [(0, 512), (512, 1024), (1024, NP)]
            for m in range(2):
                for a, z in WIDE:
                    for c in range(DC):
                        last = e.matmul(ps[:, m * 1536 + a:m * 1536 + z], m1[:, c, m * P:(m + 1) * P], encT[:, c, a:z], start=(c == 0), stop=(c == DC - 1))
                last.then_inc(S["o1_done"], 1)
            e.wait_ge(S["o1_kept"], 2)
            for a, z in WIDE:
                for c in range(2):
                    last = e.matmul(ps[:, a:z], m2[:, c, :], o1T[:, c, a:z], start=(c == 0), stop=(c == 1))
            last.then_inc(S["o2_done"], 1)
            e.wait_ge(S["o2_kept"], 1)
            for m in range(2):
                off = (1 - m) * 1536
                for a, z in WIDE:
                    last = e.matmul(ps[:, off + a:off + z], m3[:, m * P:(m + 1) * P], o2T[:, a:z], start=True, stop=True)
                last.then_inc(S["o3_done"], 1)
            e.wait_ge(S["o3_kept"], 2)
            for t in range(NT):
                if t >= 2:
                    e.wait_ge(S["out_a"], t - 1)
                for c in range(2):
                    last = e.matmul(bank(6 + t % 2), o3T[:, c, t * P:(t + 1) * P], m4[:, c, :], start=(c == 0), stop=(c == 1))
                last.then_inc(S["y4_done"], 1)


def kernel(**inputs):
    import numpy as np
    import concourse.bacc as bacc
    from concourse import mybir as mb
    from concourse.bass_utils import run_bass_kernel_spmd as run

    g = {k: np.asarray(v) for k, v in inputs.items()}
    adj = np.pad(g["adj"], ((0, NP - N), (0, NP - N)))
    adjT = np.ascontiguousarray(adj.T)
    broad = lambda v: np.ascontiguousarray(np.broadcast_to(v.reshape(1, -1), (P, v.size)))
    scalars = np.stack([g["L1_gnn_adj_scaling_factor"], g["L1_gnn_wgt_alpha"], g["L1_gnn_act_alpha"],
                        g["L1_gnn_act_alpha2"], g["L1_gnn_act_alpha2"]])
    arrays = {
        "x": np.pad(g["x"], ((0, NP - N), (0, 0))),
        "adj_rows": adj,
        "adjT_rows": adjT,
        "adjT_blocks": np.ascontiguousarray(adjT.reshape(NT, P, NT, P).transpose(2, 1, 0, 3)).reshape(NT, P, NP),
        "scalars": broad(scalars),
        "L1_gnn_weight": g["L1_gnn_weight"],
        "W1T": np.ascontiguousarray(g["L2_gnn_W1"].T),
        "L2_gnn_W2": g["L2_gnn_W2"], "L2_gnn_W3": g["L2_gnn_W3"],
        "L2_gnn_U1_0": g["L2_gnn_U1_0"], "L2_gnn_U1_1": g["L2_gnn_U1_1"],
        "L2_gnn_U2_0": g["L2_gnn_U2_0"], "L2_gnn_U2_1": g["L2_gnn_U2_1"],
        "gamma_b": broad(g["L2_gnn_gamma"]), "beta_b": broad(g["L2_gnn_beta"]),
        "Wcat": np.ascontiguousarray(g["L3_gnn_W"].transpose(1, 0, 2)).reshape(D, HEADS * HD),
        "a1_b": broad(g["L3_gnn_a1"]), "a2_b": broad(g["L3_gnn_a2"]),
        "M1": np.ascontiguousarray(g["L3_gnn_W1"].T), "M2": np.ascontiguousarray(g["L3_gnn_W2"].T),
        "M3": np.ascontiguousarray(g["L3_gnn_W3"].T), "M4": np.ascontiguousarray(g["L3_gnn_W4"].T),
        "b4_b": broad(g["L3_gnn_b4"]),
        "bcols": np.ascontiguousarray(np.concatenate([g["L3_gnn_b1"].reshape(2, P), g["L3_gnn_b2"].reshape(1, P),
                                                      g["L3_gnn_b3"].reshape(2, P)]).T),
    }
    nc = bacc.Bacc("TRN2", target_bir_lowering=False, num_devices=1)
    ins = {n: nc.dram_tensor(n, a.shape, mb.dt.from_np(a.dtype), kind="ExternalInput").ap() for n, a in arrays.items()}
    out = nc.dram_tensor("out", [N, D], F32, kind="ExternalOutput").ap()
    spill = nc.dram_tensor("x_spill", [NP, D], F32, kind="Internal").ap()
    rows = nc.dram_tensor("score_rows", [24, NP], F32, kind="Internal").ap()
    build(nc, ins, out, spill, rows)
    r = run(nc, [arrays], core_ids=[0])
    return r.results[0]["out"]
```

```python
import concourse.bass as bass
from concourse import mybir

F32 = mybir.dt.float32
BF16 = mybir.dt.bfloat16
ALU = mybir.AluOpType
ACT = mybir.ActivationFunctionType
AX_X = mybir.AxisListType.X

N, D, P = 1354, 512, 128
NT = -(-N // P)
NP = NT * P
DC = D // P
HEADS, HD, ATTN = 8, 64, 64
CHUNKS = [(0, 512), (512, 1024), (1024, N)]
MAGIC = 1.5 * 2.0 ** 23
ACT_LEVELS = 15.0
WGT_LEVELS = 7.0
GROUPS = [(0, 4, 6), (6, 9, NT)]
ROUNDS = 24
P_TOP = 0.9
EPS = 1e-5
FAR = -1.0e30
ALPHA = 0.2


def build(nc, ins, out, spill, rows_dram):
    sem_names = """
        const_id0 const_ready x_in scal_in w_in attn_w_in wsum_ready wtot_done wsq_ready wtot2_done w12_done w12_copied sqrt_in sqrt_out link row0_in row1_in deg_done rsum_done l0_staged l0_product l0_scaled l0_half at0_in at1_in p1_product p1_added p2_product p2_added p3_product p3_scaled p3_added p4_product p4_scaled p4_added q_a q_b xi_ready xi_turned xi_copied sup_done sup_a sup_b sup_c q_ready q_staged logits nmax exp_done pt_turned pt_copied att_done ln_stats ln_affine h3_ready h3_kept h3_turned h3_copied g0_done g1_done qk_done g0_kept g1_kept xa_ready xa_turned xa_copied xu_done xu_kept g2_done g2_kept qk2_done qk2_kept search_e search_s mid_ready act_sum rk_ready z_added qk_kept u_in pt_zero x_spilled pick0 pick1 pick2 pick3 keep_ready gam_in y_ready y_a y_b x3_ready x_back h4_ready h4_turned h4_copied wh_done wh_kept wh_prod scores_kept ed_turned ed_row wcat_in mask_done rows_out db0_in db1_in dmax_step dmax_kept ab_ready ab_turned ab_rows ab_out ab0_in ab1_in wh_staged t_ready t_own p_exp t_masked t_masked_own p_used h0_ready h1_ready head_kept inverses ev_b ev_c ev_exp enc_ready enc_zero mlp_in o1_done o1_kept o2_done o2_kept o3_done o3_kept y4_done out_a out_ready out_stored
    """.split()
    S = {n: nc.alloc_semaphore(n) for n in sem_names}
    STAGES = 14
    stage = [nc.alloc_semaphore(f"stage{i}_ended") for i in range(STAGES)]

    WORDS = 53208
    arena = nc.alloc_sbuf_tensor("arena", [P, WORDS], F32)
    at = [0]

    def region(words):
        at[0] += words
        assert at[0] <= WORDS, at[0]
        return at[0] - words

    def view(off, words):
        return arena[:, off:off + words]

    def nodes(off):
        return view(off, NT * D).rearrange("p (t d) -> p t d", d=D)

    oF = [region(NT * D) for _ in range(4)]
    F = [nodes(o) for o in oF]
    oE = region(NT * NP)
    Smat = view(oE, NT * NP).rearrange("p (t n) -> p t n", n=NP)
    E = view(oE, NT * N).rearrange("p (t n) -> p t n", n=N)
    oU = region(4224) + 128
    scratch0 = view(oE + NT * N, N // 2).bitcast(BF16)
    U = view(oU, 2 * DC * D).rearrange("p (u c d) -> p u c d", u=2, c=DC)
    oST = region(2 * NP)
    ST = [view(oST + b * NP, NP) for b in range(2)]
    STk = [s.rearrange("p (k n) -> p k n", n=P) for s in ST]
    oPT = region(2 * NP)
    PT = [view(oPT + b * NP, NP) for b in range(2)]
    QKT = view(region(NP), NP)
    oXA = region(2 * D)
    XA = [view(oXA + b * D, D) for b in range(2)]
    oHT = region(2 * D)
    HT = [view(oHT + b * D, D) for b in range(2)]
    HTc = [h.rearrange("p (c n) -> p c n", n=P) for h in HT]
    ones = view(region(P), P)
    oL = region(3 * NT * HEADS)
    scratch1 = view(oHT + D, N // 2).bitcast(BF16)
    SCRATCH = [scratch0, scratch1]
    ident = view(region(P), P)
    identb = view(region(P // 2), P // 2).bitcast(BF16)
    WQK = view(region(DC * P), DC * P).rearrange("p (c m) -> p c m", m=P)
    oQS = region(2 * P)
    QS = [view(oQS + b * P, P) for b in range(2)]
    scal = view(region(8), 8)
    cols = [view(region(NT), NT) for _ in range(18)]
    (deg, dinv, rsum, rinv, lna, lnb, rad, root, nmax, Zs, tau, lo, hi, Fm, mid, ge, kept, rk) = cols
    widths = view(region(ROUNDS + 1), ROUNDS + 1)
    small = view(region(16), 16)
    Dst = [view(region(NT), NT) for _ in range(2)]
    Rem = [view(region(1), 1) for _ in range(2)]

    ps = nc.alloc_psum_tensor("ps", [P, 8 * 512], F32)
    act_scratch = ps[:, 1536:1536 + N]
    bound, signs, base = deg, rsum, rad

    def bank(i, w=512):
        return ps[:, i * 512:i * 512 + w]

    wq = view(oF[3], 1024).bitcast(BF16).rearrange("p (c d) -> p c d", d=D)
    XI = [view(oF[3] + 1024 + b * 256, 256).bitcast(BF16) for b in range(2)]
    XIT = [view(oF[3] + 1536 + b * 256, 256).bitcast(BF16) for b in range(2)]
    QT = [view(oF[3] + 2048 + b * 512, 512) for b in range(2)]
    SQ = [view(oF[3] + 3072 + b * 512, 512) for b in range(2)]
    w_raw = view(oU, 2048)
    w_cen = view(oU + 2048, 2048)
    w1t = view(oPT, D)[0:ATTN, :]
    w2 = view(oPT + D, ATTN)[0:ATTN, :]
    stats = view(oQS, 6 * NT).rearrange("p (t s) -> p t s", s=6)
    lt = [view(oQS + 80 + i * NT, NT) for i in range(4)]

    mneg = view(oE, NT * NP // 2).bitcast(BF16).rearrange("p (t n) -> p t n", n=NP)
    maskT = view(oE + NT * NP // 2, NT * NP // 2).bitcast(BF16).rearrange("p (t n) -> p t n", n=NP)
    gamma_b = view(oE, D)
    beta_b = view(oE + D, D)
    Wcat = view(oU, 2048).rearrange("p (c d) -> p c d", d=D)
    a1b = view(oU + 2048, D)
    a2b = view(oU + 2560, D)
    Wh = F[1]
    prod = [view(oU + 3072 + i * D, D) for i in range(2)]
    encT = view(oF[2], DC * NP).rearrange("p (c n) -> p c n", n=NP)
    AB = [[view(oF[3] + (2 * b + i) * NP, N) for i in range(2)] for b in range(2)]
    DB = [view(oF[3] + b * NP, N) for b in range(2)]
    WS = [view(oU + b * NP, NP).rearrange("p (k m) -> p k m", m=P) for b in range(2)]
    oC = oF[2]
    junk = [view(o + i * 704, N // 2).bitcast(BF16) for o, m in ((oST, 8), (oF[3] + 2 * NP, 4)) for i in range(m)]
    TP = [view(o + b * NP, N) for o in (oST, oE) for b in range(2)]
    PP = [view(o + b * NP, N) for o in (oPT, oE + 2 * NP) for b in range(2)]
    BY_VECTOR = (2, 5, 8)
    BY_POOL = [k for k in range(NT) if k not in BY_VECTOR]
    sums = QKT[:, 0:N]
    heads2 = view(oE + 4 * NP, N)
    neg = view(oXA, N)
    es = view(oC, NT * HEADS).rearrange("p (t h) -> p t h", h=HEADS)
    ed = view(oL, NT * HEADS).rearrange("p (t h) -> p t h", h=HEADS)
    ed8 = view(oL + 88, NT * HEADS).rearrange("p (t h) -> p t h", h=HEADS)
    ed2 = view(oL + 176, NT * HEADS).rearrange("p (t h) -> p t h", h=HEADS)
    Dm = view(oC + 200, NT * HEADS).rearrange("p (t h) -> p t h", h=HEADS)
    c1 = view(oC + 300, NT * HEADS).rearrange("p (t h) -> p t h", h=HEADS)
    c2 = view(oC + 400, NT * HEADS).rearrange("p (t h) -> p t h", h=HEADS)
    abc = view(oC + 500, NT * 16).rearrange("p (t j) -> p t j", j=16)
    o1T = view(oE, 2 * NP).rearrange("p (m n) -> p m n", n=NP)
    o2T = view(oE + 2 * NP, NP)
    o3T = view(oE + 3 * NP, 2 * NP).rearrange("p (m n) -> p m n", n=NP)
    m1 = view(oF[3], 1024).rearrange("p (c m) -> p c m", m=256)
    m2 = view(oF[3] + 1024, 256).rearrange("p (c m) -> p c m", m=128)
    m3 = view(oF[3] + 1280, 256)
    m4 = view(oF[3] + 1536, 1024).rearrange("p (c m) -> p c m", m=512)
    b4b = view(oF[3] + 2560, 512)
    bcols = view(oF[3] + 3072, 8)

    def tiles(body):
        def run(e):
            body(0, 0, 0)
            body(1, 1, 0)
            with e.Fori(1, NT // 2) as p:
                body(2 * p, 0, p)
                body(2 * p + 1, 1, p)
            body(NT - 1, 0, NT // 2)
        return run

    def two_back(e, sem, t, base=0):
        if not isinstance(t, int) or t >= 2:
            e.wait_ge(sem, t + (base - 1))

    def ring_free(e, sem, h, k):
        if k >= 4 or not isinstance(h, int) or h > 0:
            e.wait_ge(sem, h * NT + (k + 1 - (3 if k < 3 else 4)))

    def col(c, t):
        return c[:, bass.ds(t, 1)]

    def end_stage(e, i):
        e.drain().then_inc(stage[i], 1)
        e.wait_ge(stage[i], 5)

    block = nc.Block()
    with block:
        @block.sync
        def _(e):
            def load_at_blocks(product):
                def body(t, b, p):
                    two_back(e, S[product], t)
                    e.dma_start(ST[b], ins["adjT_blocks"][bass.ds(t, 1), :, :].rearrange("o p n -> (o p) n")).then_inc(S[f"at{b}_in"], 16)
                tiles(body)(e)

            e.dma_start(F[0], ins["x"].rearrange("(t p) d -> p t d", p=P)).then_inc(S["x_in"], 16)
            e.dma_start(scal[:, 0:5], ins["scalars"]).then_inc(S["scal_in"], 16)
            e.dma_start(w_raw.rearrange("p (c d) -> p c d", d=D), ins["L1_gnn_weight"].rearrange("(c p) d -> p c d", p=P)).then_inc(S["w_in"], 16)
            e.dma_start(w1t, ins["W1T"]).then_inc(S["attn_w_in"], 16)
            e.dma_start(w2, ins["L2_gnn_W2"]).then_inc(S["attn_w_in"], 16)
            e.dma_start(WQK[:, :, ATTN:], ins["L2_gnn_W3"].rearrange("(c p) m -> p c m", p=P)).then_inc(S["attn_w_in"], 16)
            end_stage(e, 0)

            def rows(t, b, p):
                two_back(e, S["deg_done"], t)
                two_back(e, S["rsum_done"], t)
                e.dma_start(ST[b], ins["adj_rows"][bass.ds(t * P, P), :]).then_inc(S[f"row{b}_in"], 16)
                e.dma_start(PT[b], ins["adjT_rows"][bass.ds(t * P, P), :]).then_inc(S[f"row{b}_in"], 16)
            tiles(rows)(e)
            end_stage(e, 1)
            end_stage(e, 2)
            load_at_blocks("p1_product")
            end_stage(e, 3)
            end_stage(e, 4)
            load_at_blocks("p2_product")
            end_stage(e, 5)
            e.dma_start(spill.rearrange("(t p) d -> p t d", p=P), F[0]).then_inc(S["x_spilled"], 16)
            e.dma_start(U[:, 0], ins["L2_gnn_U1_0"].rearrange("(c p) d -> p c d", p=P)).then_inc(S["u_in"], 16)
            e.dma_start(U[:, 1], ins["L2_gnn_U1_1"].rearrange("(c p) d -> p c d", p=P)).then_inc(S["u_in"], 16)
            e.wait_ge(S["x_spilled"], 16)
            end_stage(e, 6)
            e.dma_start(U[:, 0], ins["L2_gnn_U2_0"].rearrange("(c p) d -> p c d", p=P)).then_inc(S["u_in"], 16)
            e.dma_start(U[:, 1], ins["L2_gnn_U2_1"].rearrange("(c p) d -> p c d", p=P)).then_inc(S["u_in"], 16)
            load_at_blocks("p3_product")
            end_stage(e, 7)
            load_at_blocks("p4_product")
            end_stage(e, 8)
            e.dma_start(gamma_b, ins["gamma_b"]).then_inc(S["gam_in"], 16)
            e.dma_start(beta_b, ins["beta_b"]).then_inc(S["gam_in"], 16)
            e.dma_start(F[1], spill.rearrange("(t p) d -> p t d", p=P)).then_inc(S["x_back"], 16)
            e.dma_start(Wcat, ins["Wcat"].rearrange("(c p) m -> p c m", p=P)).then_inc(S["wcat_in"], 16)
            e.dma_start(a1b, ins["a1_b"]).then_inc(S["wcat_in"], 16)
            e.dma_start(a2b, ins["a2_b"]).then_inc(S["wcat_in"], 16)
            end_stage(e, 9)

            def mask_rows(t, b, p):
                two_back(e, S["mask_done"], t)
                e.dma_start(ST[b], ins["adj_rows"][bass.ds(t * P, P), :]).then_inc(S[f"row{b}_in"], 16)
                e.dma_start(PT[b], ins["adjT_rows"][bass.ds(t * P, P), :]).then_inc(S[f"row{b}_in"], 16)
            tiles(mask_rows)(e)
            end_stage(e, 11)
            e.dma_start(rows_dram[0:8, :], QKT[0:8, :]).then_inc(S["rows_out"], 16)
            e.wait_ge(S["rows_out"], 16)
            for b in range(2):
                e.dma_start(DB[b], rows_dram[b:b + 1, 0:N].to_broadcast([P, N])).then_inc(S[f"db{b}_in"], 16)
            with e.Fori(1, HEADS // 2) as p:
                for b in range(2):
                    e.wait_ge(S["dmax_kept"], 2 * p + b - 1)
                    e.dma_start(DB[b], rows_dram[bass.ds(2 * p + b, 1), 0:N].to_broadcast([P, N])).then_inc(S[f"db{b}_in"], 16)
            e.wait_ge(S["ab_rows"], 1)
            e.dma_start(rows_dram[8:24, :], QKT[0:16, :]).then_inc(S["ab_out"], 16)
            e.wait_ge(S["ab_out"], 16)
            end_stage(e, 12)

            def load_ab(h, b):
                for i in range(2):
                    e.dma_start(AB[b][i], rows_dram[bass.ds(h + 8 + 8 * i, 1), 0:N].to_broadcast([P, N])).then_inc(S[f"ab{b}_in"], 16)
            load_ab(0, 0)
            load_ab(1, 1)
            with e.Fori(1, HEADS // 2) as p:
                for b in range(2):
                    e.wait_ge(S["p_exp"], (2 * p + b - 1) * NT)
                    load_ab(2 * p + b, b)
            end_stage(e, 13)
            e.dma_start(m1, ins["M1"].rearrange("(c p) m -> p c m", p=P)).then_inc(S["mlp_in"], 16)
            e.dma_start(m2, ins["M2"].rearrange("(c p) m -> p c m", p=P)).then_inc(S["mlp_in"], 16)
            e.dma_start(m3, ins["M3"]).then_inc(S["mlp_in"], 16)
            e.dma_start(m4, ins["M4"].rearrange("(c p) m -> p c m", p=P)).then_inc(S["mlp_in"], 16)
            e.dma_start(b4b, ins["b4_b"]).then_inc(S["mlp_in"], 16)
            e.dma_start(bcols[:, 0:5], ins["bcols"]).then_inc(S["mlp_in"], 16)
            e.wait_ge(S["out_ready"], NT)
            e.dma_start(out[0:(NT - 1) * P, :].rearrange("(t p) d -> p t d", p=P), F[0][:, 0:NT - 1, :]).then_inc(S["out_stored"], 16)
            e.dma_start(out[(NT - 1) * P:N, :], F[0][0:N - (NT - 1) * P, NT - 1, :]).then_inc(S["out_stored"], 16)
            e.wait_ge(S["out_stored"], 32)

        @block.gpsimd
        def _(e):
            e.memset(ident, 0.0).then_inc(S["const_id0"], 1)
            e.memset(identb, 0.0).then_inc(S["const_id0"], 1)
            e.memset(ones, 1.0).then_inc(S["const_id0"], 1)
            e.wait_ge(S["const_id0"], 3)
            e.affine_select(out=ident, in_=ident, compare_op=ALU.not_equal, fill=1.0, base=0,
                            pattern=[[-1, P]], channel_multiplier=1).then_inc(S["const_ready"], 1)
            e.affine_select(out=identb, in_=identb, compare_op=ALU.not_equal, fill=1.0, base=0,
                            pattern=[[-1, P]], channel_multiplier=1).then_inc(S["const_ready"], 1)
            for i in range(6):
                end_stage(e, i)

            def keep_h3(t, b, p):
                e.wait_ge(S["h3_ready"], t + 1)
                e.tensor_copy(F[1][:, t, :], XA[b]).then_inc(S["h3_kept"], 1)
            tiles(keep_h3)(e)
            for b in range(2):
                e.memset(PT[b][:, N:NP], 0.0).then_inc(S["pt_zero"], 1)
            end_stage(e, 6)

            def add_g0(t, b, p):
                e.wait_ge(S["p3_scaled"], t + 1)
                e.tensor_tensor(out=F[2][:, t, :], in0=XA[b], in1=F[2][:, t, :], op=ALU.add).then_inc(S["p3_added"], 1)
            tiles(add_g0)(e)
            end_stage(e, 7)

            def add_z(t, b, p):
                e.wait_ge(S["p4_scaled"], t + 1)
                e.tensor_tensor(out=F[0][:, t, :], in0=XA[b], in1=F[0][:, t, :], op=ALU.add).then_inc(S["p4_added"], 1)
            tiles(add_z)(e)

            def add_attention(t, b, p):
                e.wait_ge(S["xa_ready"], NT + t + 1)
                e.tensor_tensor(out=F[0][:, t, :], in0=XA[b], in1=F[0][:, t, :], op=ALU.add).then_inc(S["z_added"], 1)
            e.wait_ge(S["p4_added"], NT)
            tiles(add_attention)(e)
            for i in (8, 9, 11, 12):
                end_stage(e, i)
            e.memset(encT[:, :, N:NP], 0.0).then_inc(S["enc_zero"], 1)

            with e.Fori(0, HEADS) as h:
                for i, k in enumerate(BY_POOL):
                    e.wait_ge(S["t_ready"], h * len(BY_POOL) + (i + 1))
                    e.tensor_tensor(out=TP[k % 4], in0=TP[k % 4], in1=maskT[:, k, 0:N], op=ALU.add).then_inc(S["t_masked"], 1)
            end_stage(e, 13)

        @block.scalar
        def _(e):
            roots = [0]

            def root_of(width_):
                roots[0] += 1
                e.wait_ge(S["sqrt_in"], roots[0])
                e.activation(root[:, 0:width_], rad[:, 0:width_], ACT.Sqrt).then_inc(S["sqrt_out"], 1)

            root_of(1)
            e.wait_ge(S["w12_done"], 1)
            e.activation(WQK[:, :, 0:ATTN], ps[:, 1024:1024 + DC * ATTN].rearrange("p (c m) -> p c m", m=ATTN), ACT.Copy).then_inc(S["w12_copied"], 1)
            end_stage(e, 0)

            def row_sum(t, b, p):
                e.wait_ge(S[f"row{b}_in"], 32 * (p + 1))
                if not isinstance(t, int) or t >= 1:
                    e.wait_ge(S["rsum_done"], t)
                e.activation(F[2][:, 0:3, :].rearrange("p t d -> p (t d)")[:, 0:NP], ST[b], ACT.Copy, accum_out=col(rsum, t)).then_inc(S["rsum_done"], 1)
            tiles(row_sum)(e)
            root_of(NT)
            end_stage(e, 1)

            def norm_relu(src, dst, aff, ready, i):
                e.wait_ge(S["ln_affine"], i + 1)

                def body(t, b, p):
                    o = dst(t, b)
                    e.activation(o, src[:, t, :], ACT.Relu, scale=col(lna, t), bias=col(lnb, t)).then_inc(S[ready], 1)
                return body

            root_of(NT)
            tiles(norm_relu(F[0], lambda t, b: F[1][:, t, :], 0, "h0_ready", 0))(e)

            def stage_s(t, b, p):
                two_back(e, S["l0_product"], t)
                e.activation(STk[b], Smat[:, :, bass.ds(t * P, P)], ACT.Copy).then_inc(S["l0_staged"], 1)
            tiles(stage_s)(e)
            end_stage(e, 2)
            end_stage(e, 3)
            root_of(NT)
            tiles(norm_relu(F[0], lambda t, b: F[1][:, t, :], 0, "h1_ready", 1))(e)

            def copy_xi(t, b, p):
                e.wait_ge(S["xi_turned"], t + 1)
                two_back(e, S["sup_done"], t)
                e.activation(XIT[b], bank(2 + b, 256).bitcast(BF16), ACT.Copy).then_inc(S["xi_copied"], 1)
            tiles(copy_xi)(e)
            end_stage(e, 4)
            end_stage(e, 5)
            root_of(NT)
            e.wait_ge(S["ln_affine"], 3)

            def h3(t, b):
                two_back(e, S["h3_turned"], t)
                two_back(e, S["h3_kept"], t)
                e.activation(XA[b], F[0][:, t, :], ACT.Relu, scale=col(lna, t), bias=col(lnb, t)).then_inc(S["h3_ready"], 1)

            def keep_projections(t, b, p):
                e.wait_ge(S["h3_turned"], t + 1)
                two_back(e, S["qk_done"], t)
                e.activation(HT[b], bank(2 + b), ACT.Copy).then_inc(S["h3_copied"], 1)
                if not isinstance(t, int) or t < NT - 1:
                    h3(t + 1, 1 - b)
                e.wait_ge(S["g1_done"], t + 1)
                e.activation(F[3][:, t, :], bank(1 + 4 * b), ACT.Copy).then_inc(S["g1_kept"], 1)
                e.wait_ge(S["qk_done"], t + 1)
                e.activation(QKT[:, bass.ds(t * P, P)], bank(6 + b, P), ACT.Copy).then_inc(S["qk_kept"], 1)
            h3(0, 0)
            tiles(keep_projections)(e)
            end_stage(e, 6)

            def softmax(s):
                def body(t, b, p):
                    two_back(e, S["logits"], t, NT * s)
                    e.activation(QS[b][ATTN:, :], QKT[0:ATTN, bass.ds(t * P, P)], ACT.Copy).then_inc(S["q_staged"], 1)
                    e.wait_ge(S["nmax"], NT * s + t + 1)
                    e.activation(E[:, t, :], ps[:, b * 1536:b * 1536 + N], ACT.Exp, bias=col(nmax, t), accum_out=col(Zs, t)).then_inc(S["exp_done"], 1)
                return body

            def halve(s, g, r):
                n, (_, m, z) = s * len(GROUPS) + g, GROUPS[g]
                done = 2 * ROUNDS * sum(zz - mm for _, mm, zz in (GROUPS * 2)[:n])
                e.wait_ge(S["mid_ready"], (ROUNDS + 1) * n + 1 + r)
                for i, (func, sums) in enumerate(((ACT.Sign, signs), (ACT.Relu, bound))):
                    for t in range(m, z):
                        k = i * (z - m) + t - m
                        if k:
                            e.wait_ge(S["act_sum"], 2 * (z - m) * r + (done + k))
                        e.activation(act_scratch, E[:, t, :], func, bias=mid[:, t:t + 1],
                                     accum_out=sums[:, t:t + 1]).then_inc(S["act_sum"], 1)

            def scale_product(s):
                name = ("p3", "p4")[s]

                def body(t, b, p):
                    halve(s, 0, 2 * t)
                    e.wait_ge(S[f"{name}_product"], t + 1)
                    two_back(e, S[f"{name}_added"], t)
                    e.activation(XA[b], bank(6 + b), ACT.Identity, scale=col(rinv, t)).then_inc(S[f"{name}_scaled"], 1)
                    halve(s, 0, 2 * t + 1)
                return body

            def turned(s, t):
                e.wait_ge(S["pt_turned"], NT * s + t + 1)
                two_back(e, S["att_done"], t, NT * s)
                e.activation(ST[t % 2], ps[:, 0:NP], ACT.Copy).then_inc(S["pt_copied"], 1)

            def attention_steps(s, t):
                b = t % 2

                def scaled():
                    e.wait_ge(S["att_done"], NT * s + t + 1)
                    e.wait_ge(S["rk_ready"], NT * s + t + 1)
                    if s == 1:
                        two_back(e, S["z_added"], t)
                    e.activation(XA[b * s], bank(6), ACT.Identity, scale=col(rk, t)).then_inc(S["xa_ready"], 1)

                def xa_turned():
                    e.wait_ge(S["xa_turned"], t + 1)
                    e.activation(HT[0], bank(7), ACT.Copy).then_inc(S["xa_copied"], 1)

                def sums():
                    e.wait_ge(S["xu_done"], t + 1)
                    e.activation(F[0][:, t, :], bank(6), ACT.Copy).then_inc(S["xu_kept"], 1)
                    e.wait_ge(S["g2_done"], t + 1)
                    e.activation(F[3][:, t, :], bank(7), ACT.Copy).then_inc(S["g2_kept"], 1)

                def scores():
                    e.wait_ge(S["qk2_done"], t + 1)
                    e.activation(QKT[:, bass.ds(t * P, P)], bank(6, P), ACT.Copy).then_inc(S["qk2_kept"], 1)

                def next_turned():
                    if t + 1 not in [a for a, _, _ in GROUPS] + [NT]:
                        turned(s, t + 1)

                if s:
                    return [(.5, scaled), (.6, next_turned)]
                return [(.4, scaled), (.45, xa_turned), (.5, next_turned), (.9, sums), (.95, scores)]

            for s in range(2):
                tiles(softmax(s))(e)
                tiles(scale_product(s))(e)
                halve(s, 0, ROUNDS - 2)
                halve(s, 0, ROUNDS - 1)
                e.wait_ge(S[("p3_added", "p4_added")[s]], NT)
                for g, (a, m, z) in enumerate(GROUPS):
                    first = z - 3 if g + 1 < len(GROUPS) else z
                    turned(s, a)
                    for t in range(a, first):
                        for _, step in attention_steps(s, t):
                            step()
                    steps = [(int(ROUNDS * (t - first + part) / (z - first)), step)
                             for t in range(first, z) for part, step in attention_steps(s, t)]
                    for r in range(ROUNDS if steps else 0):
                        halve(s, g + 1, r)
                        for at_round, step in steps:
                            if at_round == r:
                                step()
                end_stage(e, 7 + s)
            root_of(NT)
            e.wait_ge(S["ln_affine"], 4)

            def y_norm(t, b, p):
                two_back(e, S["x3_ready"], t)
                e.activation(XA[b], F[0][:, t, :], ACT.Identity, scale=col(lna, t), bias=col(lnb, t)).then_inc(S["y_ready"], 1)
            tiles(y_norm)(e)
            end_stage(e, 9)
            root_of(NT)
            e.wait_ge(S["ln_affine"], 5)

            def h4(t, b):
                two_back(e, S["h4_turned"], t)
                e.activation(XA[b], F[0][:, t, :], ACT.Relu, scale=col(lna, t), bias=col(lnb, t)).then_inc(S["h4_ready"], 1)

            def keep_wh(t, b, p):
                e.wait_ge(S["h4_turned"], t + 1)
                two_back(e, S["wh_done"], t)
                e.activation(HT[b], bank(2 + b), ACT.Copy).then_inc(S["h4_copied"], 1)
                if not isinstance(t, int) or t < NT - 1:
                    h4(t + 1, 1 - b)
                e.wait_ge(S["wh_done"], t + 1)
                e.activation(Wh[:, t, :], bank(b), ACT.Copy).then_inc(S["wh_kept"], 1)
            h4(0, 0)
            tiles(keep_wh)(e)
            e.wait_ge(S["ed_turned"], 1)
            e.activation(QKT[0:8, :], ps[0:8, 4 * 512:4 * 512 + NP], ACT.Copy).then_inc(S["ed_row"], 1)
            e.wait_ge(S["ed_row"], 1)
            end_stage(e, 11)
            e.wait_ge(S["ab_turned"], 1)
            e.wait_ge(S["rows_out"], 16)
            e.activation(QKT[0:16, :], ps[0:16, 0:NP], ACT.Copy).then_inc(S["ab_rows"], 1)
            end_stage(e, 12)

            def head(h, b, p):
                if not isinstance(h, int):
                    e.wait_ge(S["p_used"], NT * (h - 1))
                e.activation(WS[b][:, :, b * HD:(b + 1) * HD], Wh[:, :, bass.ds(h * HD, HD)], ACT.Copy).then_inc(S["wh_staged"], 1)
                for k in range(NT):
                    if k in BY_VECTOR:
                        e.wait_ge(S["t_masked_own"], h * len(BY_VECTOR) + (BY_VECTOR.index(k) + 1))
                    else:
                        e.wait_ge(S["t_masked"], h * len(BY_POOL) + (BY_POOL.index(k) + 1))
                    ring_free(e, S["p_used"], h, k)
                    e.activation(PP[k % 4], TP[k % 4], ACT.Exp, bias=ed2[:, k, bass.ds(h, 1)]).then_inc(S["p_exp"], 1)
                    if k == 3 and not (isinstance(h, int) and h == 0):
                        keep_head(h - 1, 1 - b, p)
                if not isinstance(h, int) and b == 0:
                    elu(p - 1)

            def keep_head(h, b, p):
                e.wait_ge(S["p_used"], NT * (h + 1))
                if b == 0 and not isinstance(h, int):
                    e.wait_ge(S["enc_ready"], p)
                mine, other = slice(b * HD, (b + 1) * HD), slice((1 - b) * HD, (2 - b) * HD)
                e.activation(sums[mine], ps[other, b * 1536:b * 1536 + N], ACT.Copy).then_inc(S["head_kept"], 1)
                e.activation(heads2[mine], ps[mine, b * 1536:b * 1536 + N], ACT.Copy).then_inc(S["head_kept"], 1)

            def elu(pair):
                e.wait_ge(S["ev_c"], pair + 1)
                e.activation(neg, neg, ACT.Exp).then_inc(S["ev_exp"], 1)

            head(0, 0, 0)
            head(1, 1, 0)
            with e.Fori(1, HEADS // 2) as p:
                head(2 * p, 0, p)
                head(2 * p + 1, 1, p)
            keep_head(HEADS - 1, 1, 0)
            elu(HEADS // 2 - 1)
            end_stage(e, 13)
            e.wait_ge(S["mlp_in"], 96)
            for m in range(2):
                e.wait_ge(S["o1_done"], m + 1)
                e.activation(o1T[:, m, :], ps[:, m * 1536:m * 1536 + NP], ACT.Relu, bias=bcols[:, m:m + 1]).then_inc(S["o1_kept"], 1)
            e.wait_ge(S["o2_done"], 1)
            e.activation(o2T, ps[:, 0:NP], ACT.Relu, bias=bcols[:, 2:3]).then_inc(S["o2_kept"], 1)
            for m in range(2):
                e.wait_ge(S["o3_done"], m + 1)
                off = (1 - m) * 1536
                e.activation(o3T[:, m, :], ps[:, off:off + NP], ACT.Relu, bias=bcols[:, 3 + m:4 + m]).then_inc(S["o3_kept"], 1)

        @block.vector
        def _(e):
            chain = [0]
            roots = [0]

            def link(ins_):
                chain[0] += 1
                ins_.then_inc(S["link"], 1)
                e.wait_ge(S["link"], chain[0])

            def ts(out_, in_, s1, s2, op0, op1=None):
                if op1 is None:
                    return e.tensor_scalar(out_, in_, s1, None, op0)
                return e.tensor_scalar(out_, in_, s1, s2, op0, op1)

            def inverse_root(w, dst):
                r, q = root[:, 0:w], rad[:, 0:w]
                roots[0] += 1
                e.wait_ge(S["sqrt_out"], roots[0])
                link(e.reciprocal(dst, r))
                link(e.tensor_tensor(out=dst, in0=dst, in1=q, op=ALU.mult))
                link(e.tensor_tensor(out=dst, in0=dst, in1=r, op=ALU.add))
                link(ts(dst, dst, 0.5, None, ALU.mult))
                link(e.reciprocal(dst, dst))

            def layer_norm_columns(src, i):
                def st(t, b, p):
                    e.bn_stats(out=stats[:, t, :], in_=src[:, t, :]).then_inc(S["ln_stats"], 1)
                tiles(st)(e)
                e.wait_ge(S["ln_stats"], NT * (i + 1))
                me, se, mo, so = (stats[:, :, j] for j in (1, 2, 4, 5))
                link(e.tensor_tensor(out=lt[0], in0=me, in1=mo, op=ALU.add))
                link(e.tensor_tensor(out=lt[1], in0=me, in1=mo, op=ALU.subtract))
                link(e.tensor_tensor(out=lt[1], in0=lt[1], in1=lt[1], op=ALU.mult))
                link(e.tensor_tensor(out=lt[2], in0=se, in1=so, op=ALU.add))
                link(ts(lt[2], lt[2], 1.0 / D, EPS, ALU.mult, ALU.add))
                e.scalar_tensor_tensor(out=rad, in0=lt[1], scalar=0.25, in1=lt[2], op0=ALU.mult, op1=ALU.add).then_inc(S["sqrt_in"], 1)
                inverse_root(NT, lna)
                e.scalar_tensor_tensor(out=lnb, in0=lt[0], scalar=-0.5, in1=lna, op0=ALU.mult, op1=ALU.mult).then_inc(S["ln_affine"], 1)

            e.wait_ge(S["w_in"], 16)
            e.tensor_reduce(out=small[:, 0:1], in_=w_raw, op=ALU.add, axis=AX_X).then_inc(S["wsum_ready"], 1)
            e.wait_ge(S["wtot_done"], 1)
            link(ts(small[:, 1:2], bank(0, 1), 1.0 / (D * D), None, ALU.mult))
            link(ts(w_cen, w_raw, small[:, 1:2], None, ALU.subtract))
            e.scalar_tensor_tensor(out=w_raw, in0=w_cen, scalar=1.0, in1=w_cen, op0=ALU.mult, op1=ALU.mult,
                                   accum_out=small[:, 2:3]).then_inc(S["wsq_ready"], 1)
            e.wait_ge(S["wtot2_done"], 1)
            ts(rad[:, 0:1], bank(1, 1), 1.0 / (D * D - 1), None, ALU.mult).then_inc(S["sqrt_in"], 1)
            inverse_root(1, small[:, 3:4])
            e.wait_ge(S["scal_in"], 16)
            link(e.reciprocal(small[:, 4:8], scal[:, 0:4]))
            link(ts(w_cen, w_cen, small[:, 3:4], small[:, 5:6], ALU.mult, ALU.mult))
            link(ts(w_cen, w_cen, -1.0, 1.0, ALU.max, ALU.min))
            link(ts(w_cen, w_cen, WGT_LEVELS, MAGIC, ALU.mult, ALU.add))
            link(ts(wq.rearrange("p c d -> p (c d)"), w_cen, MAGIC, None, ALU.subtract))
            link(e.tensor_tensor(out=small[:, 8:9], in0=scal[:, 1:2], in1=scal[:, 2:3], op=ALU.mult))
            link(ts(small[:, 8:9], small[:, 8:9], 1.0 / (ACT_LEVELS * WGT_LEVELS), None, ALU.mult))
            link(e.tensor_tensor(out=small[:, 9:10], in0=scal[:, 0:1], in1=small[:, 4:5], op=ALU.mult))
            link(e.tensor_tensor(out=small[:, 9:10], in0=small[:, 9:10], in1=scal[:, 3:4], op=ALU.mult))
            link(ts(small[:, 9:10], small[:, 9:10], 1.0 / ACT_LEVELS, None, ALU.mult))
            end_stage(e, 0)

            def degrees(t, b, p):
                e.wait_ge(S[f"row{b}_in"], 32 * (p + 1))
                e.scalar_tensor_tensor(out=Smat[:, t, :], in0=ST[b], scalar=0.0, in1=PT[b], op0=ALU.add, op1=ALU.add,
                                       accum_out=col(deg, t)).then_inc(S["deg_done"], 1)
            tiles(degrees)(e)
            e.wait_ge(S["deg_done"], NT)
            link(ts(deg, deg, 0.5, 1.0, ALU.mult, ALU.add))
            e.tensor_scalar(rad, deg, 1e-30, None, ALU.max).then_inc(S["sqrt_in"], 1)
            inverse_root(NT, dinv)
            link(e.scalar_tensor_tensor(out=dinv, in0=deg, scalar=0.0, in1=dinv, op0=ALU.is_gt, op1=ALU.mult))
            e.wait_ge(S["rsum_done"], NT)
            link(ts(rinv, rsum, 1.0, 1e-12, ALU.add, ALU.max))
            link(e.reciprocal(rinv, rinv))
            end_stage(e, 1)

            e.wait_ge(S["x_in"], 16)
            layer_norm_columns(F[0], 0)

            def scale_h(t, b, p):
                e.wait_ge(S["h0_ready"], t + 1)
                ts(F[1][:, t, :], F[1][:, t, :], col(dinv, t), None, ALU.mult).then_inc(S["l0_half"], 1)
            tiles(scale_h)(e)

            def l0_evacuate(t, b, p):
                e.wait_ge(S["l0_product"], t + 1)
                two_back(e, S["l0_scaled"], t)
                e.scalar_tensor_tensor(out=XA[b], in0=bank(b), scalar=0.5, in1=F[1][:, t, :], op0=ALU.mult, op1=ALU.add).then_inc(S["l0_half"], 1)
                e.wait_ge(S["l0_half"], NT + t + 1)
                ts(F[2][:, t, :], XA[b], col(dinv, t), None, ALU.mult).then_inc(S["l0_scaled"], 1)
            tiles(l0_evacuate)(e)
            end_stage(e, 2)

            def add_p1(t, b, p):
                e.wait_ge(S["p1_product"], t + 1)
                e.tensor_tensor(out=F[0][:, t, :], in0=bank(b), in1=F[0][:, t, :], op=ALU.add).then_inc(S["p1_added"], 1)
            tiles(add_p1)(e)
            e.wait_ge(S["p1_added"], NT)
            end_stage(e, 3)

            layer_norm_columns(F[0], 1)

            def quantise(t, b, p):
                e.wait_ge(S["h1_ready"], t + 1)
                ts(QT[b], F[1][:, t, :], small[:, 6:7], 1.0, ALU.mult, ALU.min).then_inc(S["q_a"], 1)
                e.wait_ge(S["q_a"], t + 1)
                ts(SQ[b], QT[b], ACT_LEVELS, MAGIC, ALU.mult, ALU.add).then_inc(S["q_b"], 1)
                e.wait_ge(S["q_b"], t + 1)
                two_back(e, S["xi_turned"], t)
                ts(XI[b], SQ[b], MAGIC, None, ALU.subtract).then_inc(S["xi_ready"], 1)
                e.wait_ge(S["sup_done"], t + 1)
                ts(QT[b], bank(b), small[:, 8:9], 0.0, ALU.mult, ALU.max).then_inc(S["sup_a"], 1)
                e.wait_ge(S["sup_a"], t + 1)
                ts(SQ[b], QT[b], small[:, 7:8], 1.0, ALU.mult, ALU.min).then_inc(S["sup_b"], 1)
                e.wait_ge(S["sup_b"], t + 1)
                ts(QT[b], SQ[b], ACT_LEVELS, MAGIC, ALU.mult, ALU.add).then_inc(S["sup_c"], 1)
                e.wait_ge(S["sup_c"], t + 1)
                ts(F[2][:, t, :], QT[b], MAGIC, None, ALU.subtract).then_inc(S["q_ready"], 1)
            tiles(quantise)(e)
            end_stage(e, 4)

            def add_p2(t, b, p):
                e.wait_ge(S["p2_product"], t + 1)
                e.scalar_tensor_tensor(out=F[0][:, t, :], in0=bank(b), scalar=small[:, 9:10], in1=F[0][:, t, :],
                                       op0=ALU.mult, op1=ALU.add).then_inc(S["p2_added"], 1)
            tiles(add_p2)(e)
            e.wait_ge(S["p2_added"], NT)
            end_stage(e, 5)

            layer_norm_columns(F[0], 2)

            def keep_g0(t, b, p):
                e.wait_ge(S["g0_done"], t + 1)
                e.tensor_copy(F[2][:, t, :], bank(4 * b)).then_inc(S["g0_kept"], 1)
            tiles(keep_g0)(e)
            end_stage(e, 6)

            def row_max(s):
                def body(t, b, p):
                    e.wait_ge(S["logits"], NT * s + t + 1)
                    e.tensor_reduce(out=col(nmax, t), in_=ps[:, b * 1536:b * 1536 + N], op=ALU.max, axis=AX_X, negate=True).then_inc(S["nmax"], 1)
                return body

            def search(s, g):
                a, m, z = GROUPS[g]
                n, own, cs, sh = s * len(GROUPS) + g, m - a, slice(a, z), slice(m, z)
                before = (GROUPS * 2)[:n]
                q, q0 = S["search_s"], 4 * ROUNDS * n
                own0 = ROUNDS * sum(mm - aa for aa, mm, _ in before)
                act0 = 2 * ROUNDS * sum(zz - mm for _, mm, zz in before)

                def halve(r):
                    def sum_above(j):
                        t = a + j
                        if j >= 2:
                            e.wait_ge(S["search_e"], own * r + (own0 + j - 1))
                        e.scalar_tensor_tensor(out=SCRATCH[j % 2], in0=E[:, t, :], scalar=mid[:, t:t + 1], in1=E[:, t, :],
                                               op0=ALU.is_gt, op1=ALU.mult, accum_out=Fm[:, t:t + 1]).then_inc(S["search_e"], 1)
                    sum_above(0)
                    ts(base[:, cs], mid[:, cs], col(widths, r + 1), None, ALU.subtract).then_inc(q, 1)
                    for j in range(1, own - 1):
                        sum_above(j)
                    e.wait_ge(S["act_sum"], 2 * (z - m) * r + (act0 + z - m))
                    e.scalar_tensor_tensor(out=ge[:, sh], in0=signs[:, sh], scalar=float(N), in1=mid[:, sh],
                                           op0=ALU.add, op1=ALU.mult).then_inc(q, 1)
                    e.wait_ge(q, 4 * r + (q0 + 2))
                    e.scalar_tensor_tensor(out=Fm[:, sh], in0=ge[:, sh], scalar=0.5, in1=tau[:, sh],
                                           op0=ALU.mult, op1=ALU.add).then_inc(q, 1)
                    sum_above(own - 1)
                    e.wait_ge(q, 4 * r + (q0 + 3))
                    e.wait_ge(S["act_sum"], 2 * (z - m) * r + (act0 + 2 * (z - m)))
                    e.wait_ge(S["search_e"], own * r + (own0 + own))
                    e.tensor_tensor(out=ge[:, cs], in0=Fm[:, cs], in1=bound[:, cs], op=ALU.is_ge).then_inc(q, 1)
                    e.wait_ge(q, 4 * r + (q0 + 4))
                    e.scalar_tensor_tensor(out=mid[:, cs], in0=ge[:, cs], scalar=col(widths, r), in1=base[:, cs],
                                           op0=ALU.mult, op1=ALU.add).then_inc(S["mid_ready"], 1)
                    e.wait_ge(S["mid_ready"], r + ((ROUNDS + 1) * n + 2))

                link(e.tensor_copy(bound[:, a:m], tau[:, a:m]))
                link(e.memset(mid[:, a:m], 0.5))
                e.memset(mid[:, sh], -0.5).then_inc(S["mid_ready"], 1)
                e.wait_ge(S["mid_ready"], (ROUNDS + 1) * n + 1)
                with e.Fori(0, ROUNDS // 2) as i:
                    halve(2 * i)
                    halve(2 * i + 1)
                link(e.tensor_copy(lo[:, a:m], mid[:, a:m]))
                link(ts(hi[:, a:m], mid[:, a:m], 2.0 ** -ROUNDS, None, ALU.add))
                link(ts(hi[:, sh], mid[:, sh], -1.0, None, ALU.mult))
                link(ts(lo[:, sh], hi[:, sh], 2.0 ** -ROUNDS, None, ALU.subtract))

            def select(s, t, b, in_bracket):
                two_back(e, S["pt_turned"], t, NT * s)
                n = NT * s + t
                Et, Pt, sc = E[:, t, :], PT[b][:, 0:N], ps[:, 1536:1536 + N + 1]
                e.scalar_tensor_tensor(out=Pt, in0=Et, scalar=col(hi, t), in1=Et, op0=ALU.is_gt, op1=ALU.mult,
                                       accum_out=col(Fm, t)).then_inc(S["pick0"], 1)
                e.wait_ge(S["pick0"], n + 1)
                e.tensor_tensor(out=Rem[b], in0=col(tau, t), in1=col(Fm, t), op=ALU.subtract).then_inc(S["pick1"], 1)
                e.scalar_tensor_tensor(out=Et, in0=Et, scalar=col(lo, t), in1=Et, op0=in_bracket, op1=ALU.mult).then_inc(S["pick1"], 1)
                e.wait_ge(S["pick1"], 2 * n + 2)
                e.tensor_tensor_scan(sc[:, 1:N + 1], Et, Pt, 0.0, ALU.add, ALU.subtract).then_inc(S["pick2"], 1)
                e.wait_ge(S["pick2"], n + 1)
                e.scalar_tensor_tensor(out=Et, in0=sc[:, 0:N], scalar=Rem[b], in1=Et, op0=ALU.is_lt, op1=ALU.mult).then_inc(S["pick3"], 1)
                e.wait_ge(S["pick3"], n + 1)
                e.scalar_tensor_tensor(out=Pt, in0=Pt, scalar=1.0, in1=Et, op0=ALU.mult, op1=ALU.max,
                                       accum_out=col(kept, t)).then_inc(S["keep_ready"], 1)
                e.wait_ge(S["keep_ready"], n + 1)
                e.reciprocal(col(rk, t), col(kept, t)).then_inc(S["rk_ready"], 1)

            for r in range(ROUNDS + 1):
                link(e.memset(widths[:, r:r + 1], 2.0 ** -min(r + 1, ROUNDS)))
            for s in range(2):
                tiles(row_max(s))(e)
                e.wait_ge(S["exp_done"], NT * (s + 1))
                link(ts(tau, Zs, P_TOP, None, ALU.mult))
                for g, (a, m, z) in enumerate(GROUPS):
                    search(s, g)
                    link(e.memset(ps[:, 1536:1537], 0.0))
                    for t in range(a, z):
                        select(s, t, t % 2, ALU.is_gt if t < m else ALU.is_ge)
                end_stage(e, 7 + s)

            layer_norm_columns(F[0], 3)
            e.wait_ge(S["gam_in"], 32)
            e.wait_ge(S["x_back"], 16)

            def finish_y(t, b, p):
                e.wait_ge(S["y_ready"], t + 1)
                e.tensor_tensor(out=XA[b], in0=XA[b], in1=gamma_b, op=ALU.mult).then_inc(S["y_a"], 1)
                e.wait_ge(S["y_a"], t + 1)
                e.tensor_tensor(out=XA[b], in0=XA[b], in1=beta_b, op=ALU.add).then_inc(S["y_b"], 1)
                e.wait_ge(S["y_b"], t + 1)
                e.tensor_tensor(out=F[0][:, t, :], in0=XA[b], in1=F[1][:, t, :], op=ALU.add).then_inc(S["x3_ready"], 1)
            tiles(finish_y)(e)
            e.wait_ge(S["x3_ready"], NT)
            end_stage(e, 9)

            layer_norm_columns(F[0], 4)
            e.wait_ge(S["wcat_in"], 48)

            def scores(t, b, p):
                e.wait_ge(S["wh_kept"], t + 1)
                if not isinstance(t, int) or t >= 1:
                    e.wait_ge(S["scores_kept"], 2 * t)
                for i, ab in enumerate((a1b, a2b)):
                    e.tensor_tensor(out=prod[i], in0=Wh[:, t, :], in1=ab, op=ALU.mult).then_inc(S["wh_prod"], 1)
                for i, dst in enumerate((es[:, t, :], ed[:, t, :])):
                    e.wait_ge(S["wh_prod"], 2 * t + i + 1)
                    e.tensor_reduce(out=dst, in_=prod[i].rearrange("p (h d) -> p h d", d=HD), op=ALU.add, axis=AX_X).then_inc(S["scores_kept"], 1)
                e.wait_ge(S[f"row{b}_in"], 32 * (p + 1 + (6, 5)[b]))
                ts(mneg[:, t, :], ST[b], 0.0, FAR, ALU.is_le, ALU.mult)
                ts(maskT[:, t, :], PT[b], 0.0, FAR, ALU.is_le, ALU.mult).then_inc(S["mask_done"], 1)
            tiles(scores)(e)
            e.wait_ge(S["scores_kept"], 2 * NT)
            e.wait_ge(S["wh_done"], NT)
            for b in range(2):
                link(e.memset(WS[b][:, :, (1 - b) * HD:(2 - b) * HD], 1.0))
            end_stage(e, 11)

            def dmax(b):
                for t in range(NT):
                    e.tensor_tensor_reduce(out=junk[t], in0=DB[b], in1=mneg[:, t, 0:N], scale=1.0, scalar=4 * FAR,
                                           op0=ALU.add, op1=ALU.max, accum_out=Dst[b][:, t:t + 1]).then_inc(S["dmax_step"], 1)

            def keep_dmax(h, b):
                e.wait_ge(S["dmax_step"], NT * (h + 1))
                e.tensor_copy(Dm[:, :, bass.ds(h, 1)].rearrange("p t o -> p (t o)"), Dst[b]).then_inc(S["dmax_kept"], 1)

            e.wait_ge(S["db0_in"], 16)
            dmax(0)
            with e.Fori(1, HEADS // 2) as p:
                e.wait_ge(S["db1_in"], 16 * p)
                keep_dmax(2 * p - 2, 0)
                dmax(1)
                e.wait_ge(S["db0_in"], 16 * p + 16)
                keep_dmax(2 * p - 1, 1)
                dmax(0)
            e.wait_ge(S["db1_in"], 16 * (HEADS // 2))
            keep_dmax(HEADS - 2, 0)
            dmax(1)
            keep_dmax(HEADS - 1, 1)
            e.wait_ge(S["dmax_kept"], HEADS)
            link(e.scalar_tensor_tensor(out=Dm, in0=Dm, scalar=0.5 * FAR, in1=Dm, op0=ALU.is_gt, op1=ALU.mult))
            link(e.tensor_tensor(out=c1, in0=Dm, in1=es, op=ALU.add))
            link(e.scalar_tensor_tensor(out=c2, in0=c1, scalar=ALPHA, in1=c1, op0=ALU.mult, op1=ALU.max))
            link(e.tensor_tensor(out=abc[:, :, 0:8], in0=es, in1=c2, op=ALU.subtract))
            link(e.scalar_tensor_tensor(out=abc[:, :, 8:16], in0=es, scalar=ALPHA, in1=c2, op0=ALU.mult, op1=ALU.subtract))
            link(ts(ed8, ed, 1.0 - ALPHA, None, ALU.mult))
            ts(ed2, ed, ALPHA, None, ALU.mult).then_inc(S["ab_ready"], 1)
            end_stage(e, 12)

            def invert(pair):
                e.wait_ge(S["head_kept"], 4 * (pair + 1))
                e.reciprocal(sums, sums).then_inc(S["inverses"], 1)

            def divide(pair):
                e.wait_ge(S["inverses"], pair + 1)
                e.tensor_tensor(out=heads2, in0=heads2, in1=sums, op=ALU.mult).then_inc(S["ev_b"], 1)
                e.wait_ge(S["ev_b"], pair + 1)
                if not isinstance(pair, int) or pair > 0:
                    e.wait_ge(S["enc_ready"], pair)
                ts(neg, heads2, 0.0, None, ALU.min).then_inc(S["ev_c"], 1)

            def elu(pair):
                e.wait_ge(S["ev_exp"], pair + 1)
                dst = encT[:, bass.ds(pair, 1), 0:N].rearrange("p o n -> p (o n)")
                e.scalar_tensor_tensor(out=dst, in0=neg, scalar=-1.0, in1=heads2, op0=ALU.add, op1=ALU.max).then_inc(S["enc_ready"], 1)

            def head(h, b, p):
                e.wait_ge(S[f"ab{b}_in"], 32 * (p + 1))
                for k in range(NT):
                    ring_free(e, S["p_exp"], h, k)
                    e.scalar_tensor_tensor(out=TP[k % 4], in0=AB[b][0], scalar=ed8[:, k, bass.ds(h, 1)], in1=AB[b][1],
                                           op0=ALU.add, op1=ALU.max).then_inc(S["t_own" if k in BY_VECTOR else "t_ready"], 1)
                    if k - 1 in BY_VECTOR:
                        n = BY_VECTOR.index(k - 1) + 1
                        e.wait_ge(S["t_own"], h * len(BY_VECTOR) + n)
                        T = TP[(k - 1) % 4]
                        e.tensor_tensor(out=T, in0=T, in1=maskT[:, k - 1, 0:N], op=ALU.add).then_inc(S["t_masked_own"], 1)
                    if not isinstance(h, int) and (b, k) in FINISH:
                        FINISH[b, k](p - 1)

            FINISH = {(0, 6): invert, (0, 9): divide, (1, 1): elu}
            head(0, 0, 0)
            head(1, 1, 0)
            with e.Fori(1, HEADS // 2) as p:
                head(2 * p, 0, p)
                head(2 * p + 1, 1, p)
            for finish_pair in (invert, divide, elu):
                finish_pair(HEADS // 2 - 1)
            end_stage(e, 13)

            e.wait_ge(S["mlp_in"], 96)

            def finish(t, b, p):
                e.wait_ge(S["y4_done"], t + 1)
                two_back(e, S["out_ready"], t)
                e.tensor_tensor(out=XA[b], in0=bank(6 + b), in1=b4b, op=ALU.add).then_inc(S["out_a"], 1)
                e.wait_ge(S["out_a"], t + 1)
                e.tensor_tensor(out=F[0][:, t, :], in0=XA[b], in1=F[0][:, t, :], op=ALU.add).then_inc(S["out_ready"], 1)
            tiles(finish)(e)

        @block.tensor
        def _(e):
            def product(acc, lhs, rhs, last_open=False):
                for k in range(NT):
                    last = e.matmul(acc, lhs[:, k, :], rhs[:, k, :], start=(k == 0), stop=(k == NT - 1 and not last_open))
                return last

            def adjacency_product(name, rhs, base_bank, loads_before, free, with_self):
                def body(t, b, p):
                    e.wait_ge(S[f"at{b}_in"], 16 * (loads_before[b] + p + 1))
                    two_back(e, S[free], t)
                    last = product(bank(base_bank + b), STk[b], rhs, with_self)
                    if with_self:
                        last = e.matmul(bank(base_bank + b), ident, rhs[:, t, :], start=False, stop=True)
                    last.then_inc(S[f"{name}_product"], 1)
                return body

            e.wait_ge(S["const_id0"], 3)
            e.wait_ge(S["const_ready"], 2)
            e.wait_ge(S["wsum_ready"], 1)
            e.matmul(bank(0, 1), ones, small[:, 0:1], start=True, stop=True).then_inc(S["wtot_done"], 1)
            e.wait_ge(S["wsq_ready"], 1)
            e.matmul(bank(1, 1), ones, small[:, 2:3], start=True, stop=True).then_inc(S["wtot2_done"], 1)
            e.wait_ge(S["attn_w_in"], 48)
            for c in range(DC):
                last = e.matmul(bank(2)[:, c * ATTN:(c + 1) * ATTN], w1t[:, c * P:(c + 1) * P], w2, start=True, stop=True)
            last.then_inc(S["w12_done"], 1)
            end_stage(e, 0)
            end_stage(e, 1)

            e.wait_ge(S["l0_half"], NT)

            def l0(t, b, p):
                e.wait_ge(S["l0_staged"], t + 1)
                two_back(e, S["l0_scaled"], t)
                product(bank(b), STk[b], F[1]).then_inc(S["l0_product"], 1)
            tiles(l0)(e)
            end_stage(e, 2)
            tiles(adjacency_product("p1", F[2], 0, (0, 0), "p1_added", False))(e)
            end_stage(e, 3)

            def support(t, b, p):
                e.wait_ge(S["xi_ready"], t + 1)
                two_back(e, S["xi_copied"], t)
                for c in range(DC):
                    last = e.transpose(bank(2 + b, 256).bitcast(BF16)[:, c * P:(c + 1) * P], XI[b][:, c * P:(c + 1) * P], identb)
                last.then_inc(S["xi_turned"], 1)
                e.wait_ge(S["xi_copied"], t + 1)
                two_back(e, S["sup_a"], t)
                for c in range(DC):
                    last = e.matmul(bank(b), XIT[b][:, c * P:(c + 1) * P], wq[:, c, :], start=(c == 0), stop=(c == DC - 1))
                last.then_inc(S["sup_done"], 1)
            tiles(support)(e)
            end_stage(e, 4)
            tiles(adjacency_product("p2", F[2], 0, (6, 5), "p2_added", False))(e)
            end_stage(e, 5)

            e.wait_ge(S["u_in"], 32)

            def project(acc, turned, weights):
                for c in range(DC):
                    last = e.matmul(acc, turned[:, c, :], weights[:, c, :], start=(c == 0), stop=(c == DC - 1))
                return last

            def turn(acc, tile):
                for c in range(DC):
                    last = e.transpose(acc[:, c * P:(c + 1) * P], tile[:, c * P:(c + 1) * P], ident)
                return last

            def h3(t, b, p):
                e.wait_ge(S["h3_ready"], t + 1)
                two_back(e, S["h3_copied"], t)
                turn(bank(2 + b), XA[b]).then_inc(S["h3_turned"], 1)
                e.wait_ge(S["h3_copied"], t + 1)
                two_back(e, S["g0_kept"], t)
                project(bank(4 * b), HTc[b], U[:, 0]).then_inc(S["g0_done"], 1)
                two_back(e, S["g1_kept"], t)
                project(bank(1 + 4 * b), HTc[b], U[:, 1]).then_inc(S["g1_done"], 1)
                two_back(e, S["qk_kept"], t)
                project(bank(6 + b, P), WQK, HTc[b]).then_inc(S["qk_done"], 1)
            tiles(h3)(e)
            end_stage(e, 6)

            def logits(s):
                def body(t, b, p):
                    e.wait_ge(S["q_staged"], NT * s + t + 1)
                    two_back(e, S["exp_done"], t, NT * s)
                    for a, z in CHUNKS:
                        last = e.matmul(ps[:, b * 1536 + a:b * 1536 + z], QS[b][ATTN:, :], QKT[ATTN:, a:z], start=True, stop=True)
                    last.then_inc(S["logits"], 1)
                return body

            def turn_pt(n, b):
                e.wait_ge(S["keep_ready"], n + 1)
                if not isinstance(n, int) or n >= 1:
                    e.wait_ge(S["pt_copied"], n)
                for k in range(NT):
                    last = e.transpose(ps[:, k * P:(k + 1) * P], PT[b][:, k * P:(k + 1) * P], ident)
                last.then_inc(S["pt_turned"], 1)

            def attention(s, t, b, turn_next):
                n = NT * s + t
                e.wait_ge(S["pt_copied"], n + 1)
                if not isinstance(t, int) or t >= 1:
                    e.wait_ge(S["xa_ready" if s else "qk2_kept"], n)
                product(bank(6), STk[b], (F[1], F[3])[s]).then_inc(S["att_done"], 1)
                if turn_next:
                    turn_pt(n + 1, 1 - b)
                if s == 0:
                    e.wait_ge(S["xa_ready"], t + 1)
                    turn(bank(7), XA[0]).then_inc(S["xa_turned"], 1)
                    e.wait_ge(S["xa_copied"], t + 1)
                    e.matmul(bank(6), ident, F[1][:, t, :], start=True, stop=False)
                    for c in range(DC):
                        last = e.matmul(bank(6), HTc[0][:, c, :], U[:, 0][:, c, :], start=False, stop=(c == DC - 1))
                    last.then_inc(S["xu_done"], 1)
                    project(bank(7), HTc[0], U[:, 1]).then_inc(S["g2_done"], 1)
                    e.wait_ge(S["xu_kept"], t + 1)
                    project(bank(6, P), WQK, HTc[0]).then_inc(S["qk2_done"], 1)

            def group_attention(s, a, z):
                turn_pt(NT * s + a, a % 2)
                attention(s, a, a % 2, True)
                pairs = (z - a - 2) // 2
                with e.Fori(0, pairs) as i:
                    attention(s, 2 * i + (a + 1), (a + 1) % 2, True)
                    attention(s, 2 * i + (a + 2), a % 2, True)
                for t in range(a + 1 + 2 * pairs, z):
                    attention(s, t, t % 2, t < z - 1)

            for s in range(2):
                tiles(logits(s))(e)
                tiles(adjacency_product(("p3", "p4")[s], (F[3], F[2])[s], 6, ((12, 10), (18, 15))[s], ("p3_scaled", "p4_scaled")[s], True))(e)
                if s == 0:
                    e.wait_ge(S["u_in"], 64)
                for a, _, z in GROUPS:
                    group_attention(s, a, z)
                end_stage(e, 7 + s)
            end_stage(e, 9)
            e.wait_ge(S["wcat_in"], 48)

            def wh(t, b, p):
                e.wait_ge(S["h4_ready"], t + 1)
                two_back(e, S["h4_copied"], t)
                turn(bank(2 + b), XA[b]).then_inc(S["h4_turned"], 1)
                e.wait_ge(S["h4_copied"], t + 1)
                two_back(e, S["wh_kept"], t)
                project(bank(b), HTc[b], Wcat).then_inc(S["wh_done"], 1)
            tiles(wh)(e)
            e.wait_ge(S["scores_kept"], 2 * NT)
            for t in range(NT):
                last = e.transpose(ps[0:8, 4 * 512 + t * P:4 * 512 + (t + 1) * P], ed[:, t, :], ident)
            last.then_inc(S["ed_turned"], 1)
            end_stage(e, 11)
            e.wait_ge(S["ab_ready"], 1)
            for t in range(NT):
                last = e.transpose(ps[0:16, t * P:(t + 1) * P], abc[:, t, :], ident)
            last.then_inc(S["ab_turned"], 1)
            end_stage(e, 12)

            def head(h, b):
                e.wait_ge(S["wh_staged"], h + 1)
                if not isinstance(h, int):
                    e.wait_ge(S["head_kept"], 2 * (h - 1))
                for k in range(NT):
                    e.wait_ge(S["p_exp"], h * NT + (k + 1))
                    for a, z in CHUNKS:
                        last = e.matmul(ps[:, b * 1536 + a:b * 1536 + z], WS[b][:, k, :], PP[k % 4][:, a:z], start=(k == 0), stop=(k == NT - 1))
                    last.then_inc(S["p_used"], 1)
            head(0, 0)
            head(1, 1)
            with e.Fori(1, HEADS // 2) as p:
                head(2 * p, 0)
                head(2 * p + 1, 1)
            end_stage(e, 13)

            e.wait_ge(S["mlp_in"], 96)
            WIDE = [(0, 512), (512, 1024), (1024, NP)]
            for m in range(2):
                for a, z in WIDE:
                    for c in range(DC):
                        last = e.matmul(ps[:, m * 1536 + a:m * 1536 + z], m1[:, c, m * P:(m + 1) * P], encT[:, c, a:z], start=(c == 0), stop=(c == DC - 1))
                last.then_inc(S["o1_done"], 1)
            e.wait_ge(S["o1_kept"], 2)
            for a, z in WIDE:
                for c in range(2):
                    last = e.matmul(ps[:, a:z], m2[:, c, :], o1T[:, c, a:z], start=(c == 0), stop=(c == 1))
            last.then_inc(S["o2_done"], 1)
            e.wait_ge(S["o2_kept"], 1)
            for m in range(2):
                off = (1 - m) * 1536
                for a, z in WIDE:
                    last = e.matmul(ps[:, off + a:off + z], m3[:, m * P:(m + 1) * P], o2T[:, a:z], start=True, stop=True)
                last.then_inc(S["o3_done"], 1)
            e.wait_ge(S["o3_kept"], 2)
            for t in range(NT):
                if t >= 2:
                    e.wait_ge(S["out_a"], t - 1)
                for c in range(2):
                    last = e.matmul(bank(6 + t % 2), o3T[:, c, t * P:(t + 1) * P], m4[:, c, :], start=(c == 0), stop=(c == 1))
                last.then_inc(S["y4_done"], 1)


def kernel(**inputs):
    import numpy as np
    import concourse.bacc as bacc
    from concourse import mybir as mb
    from concourse.bass_utils import run_bass_kernel_spmd as run

    g = {k: np.asarray(v) for k, v in inputs.items()}
    adj = np.pad(g["adj"], ((0, NP - N), (0, NP - N)))
    adjT = np.ascontiguousarray(adj.T)
    broad = lambda v: np.ascontiguousarray(np.broadcast_to(v.reshape(1, -1), (P, v.size)))
    scalars = np.stack([g["L1_gnn_adj_scaling_factor"], g["L1_gnn_wgt_alpha"], g["L1_gnn_act_alpha"],
                        g["L1_gnn_act_alpha2"], g["L1_gnn_act_alpha2"]])
    arrays = {
        "x": np.pad(g["x"], ((0, NP - N), (0, 0))),
        "adj_rows": adj,
        "adjT_rows": adjT,
        "adjT_blocks": np.ascontiguousarray(adjT.reshape(NT, P, NT, P).transpose(2, 1, 0, 3)).reshape(NT, P, NP),
        "scalars": broad(scalars),
        "L1_gnn_weight": g["L1_gnn_weight"],
        "W1T": np.ascontiguousarray(g["L2_gnn_W1"].T),
        "L2_gnn_W2": g["L2_gnn_W2"], "L2_gnn_W3": g["L2_gnn_W3"],
        "L2_gnn_U1_0": g["L2_gnn_U1_0"], "L2_gnn_U1_1": g["L2_gnn_U1_1"],
        "L2_gnn_U2_0": g["L2_gnn_U2_0"], "L2_gnn_U2_1": g["L2_gnn_U2_1"],
        "gamma_b": broad(g["L2_gnn_gamma"]), "beta_b": broad(g["L2_gnn_beta"]),
        "Wcat": np.ascontiguousarray(g["L3_gnn_W"].transpose(1, 0, 2)).reshape(D, HEADS * HD),
        "a1_b": broad(g["L3_gnn_a1"]), "a2_b": broad(g["L3_gnn_a2"]),
        "M1": np.ascontiguousarray(g["L3_gnn_W1"].T), "M2": np.ascontiguousarray(g["L3_gnn_W2"].T),
        "M3": np.ascontiguousarray(g["L3_gnn_W3"].T), "M4": np.ascontiguousarray(g["L3_gnn_W4"].T),
        "b4_b": broad(g["L3_gnn_b4"]),
        "bcols": np.ascontiguousarray(np.concatenate([g["L3_gnn_b1"].reshape(2, P), g["L3_gnn_b2"].reshape(1, P),
                                                      g["L3_gnn_b3"].reshape(2, P)]).T),
    }
    nc = bacc.Bacc("TRN2", target_bir_lowering=False, num_devices=1)
    ins = {n: nc.dram_tensor(n, a.shape, mb.dt.from_np(a.dtype), kind="ExternalInput").ap() for n, a in arrays.items()}
    out = nc.dram_tensor("out", [N, D], F32, kind="ExternalOutput").ap()
    spill = nc.dram_tensor("x_spill", [NP, D], F32, kind="Internal").ap()
    rows = nc.dram_tensor("score_rows", [24, NP], F32, kind="Internal").ap()
    build(nc, ins, out, spill, rows)
    r = run(nc, [arrays], core_ids=[0])
    return r.results[0]["out"]
```

```python
import concourse.bass as bass
from concourse import mybir

F32 = mybir.dt.float32
BF16 = mybir.dt.bfloat16
ALU = mybir.AluOpType
ACT = mybir.ActivationFunctionType
AX_X = mybir.AxisListType.X

N, D, P = 1354, 512, 128
NT = -(-N // P)
NP = NT * P
DC = D // P
HEADS, HD, ATTN = 8, 64, 64
CHUNKS = [(0, 512), (512, 1024), (1024, N)]
MAGIC = 1.5 * 2.0 ** 23
ACT_LEVELS = 15.0
WGT_LEVELS = 7.0
GROUPS = ([(0, 3, 5), (5, 7, 8), (8, 10, NT)], [(0, 3, 5), (5, 9, NT)])
ROUNDS = 24
P_TOP = 0.9
EPS = 1e-5
FAR = -1.0e30
ALPHA = 0.2


def build(nc, ins, out, spill, rows_dram):
    sem_names = """
        const_id0 const_ready x_in scal_in w_in attn_w_in wsum_ready wtot_done wsq_ready wtot2_done
        w12_done sqrt_in sqrt_out link row0_in row1_in deg_done rsum_done l0_staged l0_product
        l0_scaled l0_half at0_in at1_in p1_product p1_added a_high a_rest a_mid a_low p2_product
        p2_added p3_product p3_scaled p3_added p4_product p4_scaled p4_added q_a q_b xi_ready
        xi_turned xi_copied sup_done sup_a sup_b sup_c q_ready q_staged logits nmax exp_done
        pt_turned pt_copied att_done ln_stats ln_affine h3_ready h3_kept h3_turned h3_copied g0_done
        g1_done qk_done g0_kept g1_kept xa_ready xa_turned xa_copied xu_done xu_kept g2_done
        qk2_done qk2_kept search_e search_s mid_ready act_sum rk_ready z_added qk_kept u_in
        x_spilled pick0 pick1 pick2 pick3 keep_ready gam_in beta_in x_beta y_ready y_a x3_ready
        x_back h4_ready h4_turned h4_copied wh_done wh_kept wh_prod scores_kept ed_turned ed_row
        wcat_in mask_done rows_out db0_in db1_in dmax_step dmax_kept ab_ready ab_turned ab_rows
        ab_out ab0_in ab1_in wh_staged t_ready t_own p_exp t_masked t_masked_own p_used h0_ready
        h1_ready head_kept inverses ev_b ev_c ev_exp enc_ready mlp_in o1_done o1_kept o2_done
        o2_kept o3_done o3_kept y4_done out_a out_ready out_stored
    """.split()
    S = {n: nc.alloc_semaphore(n) for n in sem_names}
    STAGES = 11
    stage = [nc.alloc_semaphore(f"stage{i}_ended") for i in range(STAGES)]

    WORDS = 53208
    arena = nc.alloc_sbuf_tensor("arena", [P, WORDS], F32)
    at = [0]

    def region(words):
        at[0] += words
        assert at[0] <= WORDS, at[0]
        return at[0] - words

    def view(off, words):
        return arena[:, off:off + words]

    def nodes(off):
        return view(off, NT * D).rearrange("p (t d) -> p t d", d=D)

    oF = [region(NT * D) for _ in range(4)]
    F = [nodes(o) for o in oF]
    oE = region(NT * NP)
    Smat = view(oE, NT * NP).rearrange("p (t n) -> p t n", n=NP)
    E = view(oE, NT * N).rearrange("p (t n) -> p t n", n=N)
    oU = region(4224) + 128
    scratch0 = view(oE + NT * N, N // 2).bitcast(BF16)
    U = view(oU, 2 * DC * D).rearrange("p (u c d) -> p u c d", u=2, c=DC)
    oST = region(2 * NP)
    ST = [view(oST + b * NP, NP) for b in range(2)]
    STk = [s.rearrange("p (k n) -> p k n", n=P) for s in ST]
    oPT = region(2 * NP)
    PT = [view(oPT + b * NP, NP) for b in range(2)]
    QKT = view(region(NP), NP)
    oXA = region(2 * D)
    XA = [view(oXA + b * D, D) for b in range(2)]
    oHT = region(2 * D)
    HT = [view(oHT + b * D, D) for b in range(2)]
    HTc = [h.rearrange("p (c n) -> p c n", n=P) for h in HT]
    ones = view(region(P), P)
    oL = region(3 * NT * HEADS)
    scratch1 = view(oHT + D, N // 2).bitcast(BF16)
    SCRATCH = [scratch0, scratch1]
    ident = view(region(P), P)
    identb = view(region(P // 2), P // 2).bitcast(BF16)
    WQK = view(region(DC * P), DC * P).rearrange("p (c m) -> p c m", m=P)
    oQS = region(2 * P)
    QS = [view(oQS + b * P, P) for b in range(2)]
    scal = view(region(8), 8)
    cols = [view(region(NT), NT) for _ in range(18)]
    (deg, dinv, rsum, rinv, lna, lnb, rad, root, nmax, Zs, tau, lo, hi, Fm, mid, ge, kept, rk) = cols
    widths = view(region(ROUNDS + 1), ROUNDS + 1)
    small = view(region(16), 16)
    Dst = [view(region(NT), NT) for _ in range(2)]
    Rem = [view(region(1), 1) for _ in range(2)]

    ps = nc.alloc_psum_tensor("ps", [P, 8 * 512], F32)
    act_scratch = ps[:, 1536:1536 + N]
    bound, signs, base = deg, rsum, rad

    def bank(i, w=512):
        return ps[:, i * 512:i * 512 + w]

    wq = view(oF[3], 1024).bitcast(BF16).rearrange("p (c d) -> p c d", d=D)
    XI = [view(oF[3] + 1024 + b * 256, 256).bitcast(BF16) for b in range(2)]
    XIT = [view(oF[3] + 1536 + b * 256, 256).bitcast(BF16) for b in range(2)]
    QT = [view(oF[3] + 2048 + b * 512, 512) for b in range(2)]
    SQ = [view(oF[3] + 3072 + b * 512, 512) for b in range(2)]
    w_raw = view(oU, 2048)
    w_cen = view(oU + 2048, 2048)
    w1t = view(oF[1], D)[0:ATTN, :]
    w2 = view(oF[1] + D, ATTN)[0:ATTN, :]
    stats = view(oQS, 6 * NT).rearrange("p (t s) -> p t s", s=6)
    lt = [view(oQS + 80 + i * NT, NT) for i in range(4)]

    A_PARTS = [[view(oF[3] + (2 * i + b) * NP // 2, NP // 2).bitcast(BF16) for b in range(2)] for i in range(3)]
    a_left = view(oF[3] + 3 * NP, NP)
    q16 = view(oF[2], NT * D // 2).bitcast(BF16).rearrange("p (t d) -> p t d", d=D)

    mneg = view(oE, NT * NP // 2).bitcast(BF16).rearrange("p (t n) -> p t n", n=NP)
    maskT = view(oE + NT * NP // 2, NT * NP // 2).bitcast(BF16).rearrange("p (t n) -> p t n", n=NP)
    gamma_b = view(oU + 3072, D)
    beta_b = view(oU + 3584, D)
    Wcat = view(oU, 2048).rearrange("p (c d) -> p c d", d=D)
    a1b = view(oU + 2048, D)
    a2b = view(oU + 2560, D)
    Wh = F[1]
    prod = [view(oU + 3072 + i * D, D) for i in range(2)]
    encT = view(oF[2], DC * NP).rearrange("p (c n) -> p c n", n=NP)
    AB = [[view(oF[3] + (2 * b + i) * NP, N) for i in range(2)] for b in range(2)]
    DB = [view(oF[3] + b * NP, N) for b in range(2)]
    WS = [view(oU + b * NP, NP).rearrange("p (k m) -> p k m", m=P) for b in range(2)]
    oC = oF[2]
    junk = [view(o + i * 704, N // 2).bitcast(BF16) for o, m in ((oST, 8), (oF[3] + 2 * NP, 4)) for i in range(m)]
    TP = [view(o + b * NP, N) for o in (oST, oE) for b in range(2)]
    PP = [view(o + b * NP, N) for o in (oPT, oE + 2 * NP) for b in range(2)]
    BY_VECTOR = (2, 5, 8)
    BY_POOL = [k for k in range(NT) if k not in BY_VECTOR]
    sums = QKT[:, 0:N]
    heads2 = view(oE + 4 * NP, N)
    neg = view(oXA, N)
    es = view(oC, NT * HEADS).rearrange("p (t h) -> p t h", h=HEADS)
    ed = view(oL, NT * HEADS).rearrange("p (t h) -> p t h", h=HEADS)
    ed8 = view(oL + 88, NT * HEADS).rearrange("p (t h) -> p t h", h=HEADS)
    ed2 = view(oL + 176, NT * HEADS).rearrange("p (t h) -> p t h", h=HEADS)
    Dm = view(oC + 200, NT * HEADS).rearrange("p (t h) -> p t h", h=HEADS)
    c1 = view(oC + 300, NT * HEADS).rearrange("p (t h) -> p t h", h=HEADS)
    c2 = view(oC + 400, NT * HEADS).rearrange("p (t h) -> p t h", h=HEADS)
    abc = view(oC + 500, NT * 16).rearrange("p (t j) -> p t j", j=16)
    o1T = view(oE, 2 * NP).rearrange("p (m n) -> p m n", n=NP)
    o2T = view(oE + 2 * NP, NP)
    o3T = view(oE + 3 * NP, 2 * NP).rearrange("p (m n) -> p m n", n=NP)
    m1 = view(oF[3], 1024).rearrange("p (c m) -> p c m", m=256)
    m2 = view(oF[3] + 1024, 256).rearrange("p (c m) -> p c m", m=128)
    m3 = view(oF[3] + 1280, 256)
    m4 = view(oF[3] + 1536, 1024).rearrange("p (c m) -> p c m", m=512)
    b4b = view(oU + 2 * NP, 512)
    bcols = view(oU + 2 * NP + 512, 8)

    def tiles(body, after_two=None):
        def run(e):
            body(0, 0, 0)
            body(1, 1, 0)
            if after_two:
                after_two()
            with e.Fori(1, NT // 2) as p:
                body(2 * p, 0, p)
                body(2 * p + 1, 1, p)
            body(NT - 1, 0, NT // 2)
        return run

    def two_back(e, sem, t, base=0):
        if not isinstance(t, int) or t >= 2:
            e.wait_ge(sem, t + (base - 1))

    def ring_free(e, sem, h, k):
        if k >= 4 or not isinstance(h, int) or h > 0:
            e.wait_ge(sem, h * NT + (k + 1 - (3 if k < 3 else 4)))

    def col(c, t):
        return c[:, bass.ds(t, 1)]

    def end_stage(e, i):
        e.drain().then_inc(stage[i], 1)
        e.wait_ge(stage[i], 5)

    block = nc.Block()
    with block:
        @block.sync
        def _(e):
            def load_at_blocks(used, ends=None):
                def body(t, b, p):
                    two_back(e, S[used], t)
                    e.dma_start(ST[b], ins["adjT_blocks"][bass.ds(t, 1), :, :].rearrange("o p n -> (o p) n")).then_inc(S[f"at{b}_in"], 16)
                tiles(body, None if ends is None else lambda: end_stage(e, ends))(e)

            e.dma_start(scal[:, 0:5], ins["scalars"]).then_inc(S["scal_in"], 16)
            e.dma_start(w_raw.rearrange("p (c d) -> p c d", d=D), ins["L1_gnn_weight"].rearrange("(c p) d -> p c d", p=P)).then_inc(S["w_in"], 16)
            e.dma_start(w1t, ins["W1T"]).then_inc(S["attn_w_in"], 16)
            e.dma_start(w2, ins["L2_gnn_W2"]).then_inc(S["attn_w_in"], 16)
            e.dma_start(WQK[:, :, ATTN:], ins["L2_gnn_W3"].rearrange("(c p) m -> p c m", p=P)).then_inc(S["attn_w_in"], 16)

            def rows(t, b, p):
                two_back(e, S["deg_done"], t)
                two_back(e, S["rsum_done"], t)
                e.dma_start(ST[b], ins["adj_rows"][bass.ds(t * P, P), :]).then_inc(S[f"row{b}_in"], 16)
                e.dma_start(PT[b], ins["adjT_rows"][bass.ds(t * P, P), :]).then_inc(S[f"row{b}_in"], 16)
            tiles(rows, lambda: e.dma_start(F[0], ins["x"].rearrange("(t p) d -> p t d", p=P)).then_inc(S["x_in"], 16))(e)
            end_stage(e, 0)
            end_stage(e, 1)
            load_at_blocks("p1_product")
            end_stage(e, 2)
            load_at_blocks("a_rest", 3)
            end_stage(e, 4)
            e.dma_start(spill.rearrange("(t p) d -> p t d", p=P), F[0]).then_inc(S["x_spilled"], 16)
            e.dma_start(U[:, 0], ins["L2_gnn_U1_0"].rearrange("(c p) d -> p c d", p=P)).then_inc(S["u_in"], 16)
            e.dma_start(U[:, 1], ins["L2_gnn_U1_1"].rearrange("(c p) d -> p c d", p=P)).then_inc(S["u_in"], 16)
            e.wait_ge(S["x_spilled"], 16)
            load_at_blocks("p3_product", 5)
            e.dma_start(U[:, 0], ins["L2_gnn_U2_0"].rearrange("(c p) d -> p c d", p=P)).then_inc(S["u_in"], 16)
            e.dma_start(U[:, 1], ins["L2_gnn_U2_1"].rearrange("(c p) d -> p c d", p=P)).then_inc(S["u_in"], 16)
            end_stage(e, 6)
            e.dma_start(gamma_b, ins["gamma_b"]).then_inc(S["gam_in"], 16)
            e.dma_start(beta_b, ins["beta_b"]).then_inc(S["beta_in"], 16)
            e.dma_start(F[1], spill.rearrange("(t p) d -> p t d", p=P)).then_inc(S["x_back"], 16)
            e.dma_start(Wcat, ins["Wcat"].rearrange("(c p) m -> p c m", p=P)).then_inc(S["wcat_in"], 16)
            e.dma_start(a1b, ins["a1_b"]).then_inc(S["wcat_in"], 16)
            e.dma_start(a2b, ins["a2_b"]).then_inc(S["wcat_in"], 16)
            load_at_blocks("p4_product")
            end_stage(e, 7)

            def mask_rows(t, b, p):
                two_back(e, S["mask_done"], t)
                e.dma_start(ST[b], ins["adj_rows"][bass.ds(t * P, P), :]).then_inc(S[f"row{b}_in"], 16)
                e.dma_start(PT[b], ins["adjT_rows"][bass.ds(t * P, P), :]).then_inc(S[f"row{b}_in"], 16)
            tiles(mask_rows, lambda: end_stage(e, 8))(e)
            end_stage(e, 9)
            e.dma_start(rows_dram[0:8, :], QKT[0:8, :]).then_inc(S["rows_out"], 16)
            e.wait_ge(S["rows_out"], 16)
            for b in range(2):
                e.dma_start(DB[b], rows_dram[b:b + 1, 0:N].to_broadcast([P, N])).then_inc(S[f"db{b}_in"], 16)
            with e.Fori(1, HEADS // 2) as p:
                for b in range(2):
                    e.wait_ge(S["dmax_kept"], 2 * p + b - 1)
                    e.dma_start(DB[b], rows_dram[bass.ds(2 * p + b, 1), 0:N].to_broadcast([P, N])).then_inc(S[f"db{b}_in"], 16)
            e.wait_ge(S["ab_rows"], 1)
            e.dma_start(rows_dram[8:24, :], QKT[0:16, :]).then_inc(S["ab_out"], 16)
            e.wait_ge(S["ab_out"], 16)

            def load_ab(h, b):
                for i in range(2):
                    e.dma_start(AB[b][i], rows_dram[bass.ds(h + 8 + 8 * i, 1), 0:N].to_broadcast([P, N])).then_inc(S[f"ab{b}_in"], 16)
            load_ab(0, 0)
            load_ab(1, 1)
            end_stage(e, 10)
            with e.Fori(1, HEADS // 2) as p:
                for b in range(2):
                    e.wait_ge(S["p_exp"], (2 * p + b - 1) * NT)
                    load_ab(2 * p + b, b)
            e.wait_ge(S["p_exp"], (HEADS - 1) * NT)
            e.dma_start(m1, ins["M1"].rearrange("(c p) m -> p c m", p=P)).then_inc(S["mlp_in"], 16)
            e.dma_start(m2, ins["M2"].rearrange("(c p) m -> p c m", p=P)).then_inc(S["mlp_in"], 16)
            e.dma_start(m3, ins["M3"]).then_inc(S["mlp_in"], 16)
            e.dma_start(m4, ins["M4"].rearrange("(c p) m -> p c m", p=P)).then_inc(S["mlp_in"], 16)
            e.dma_start(b4b, ins["b4_b"]).then_inc(S["mlp_in"], 16)
            e.dma_start(bcols[:, 0:5], ins["bcols"]).then_inc(S["mlp_in"], 16)
            full = NT - 1
            for a, z in ((0, full // 2), (full // 2, full)):
                e.wait_ge(S["out_ready"], z)
                e.dma_start(out[a * P:z * P, :].rearrange("(t p) d -> p t d", p=P), F[0][:, a:z, :]).then_inc(S["out_stored"], 16)
            e.wait_ge(S["out_ready"], NT)
            e.dma_start(out[full * P:N, :], F[0][0:N - full * P, full, :]).then_inc(S["out_stored"], 16)
            e.wait_ge(S["out_stored"], 48)

        @block.gpsimd
        def _(e):
            e.memset(ident, 0.0).then_inc(S["const_id0"], 1)
            e.memset(identb, 0.0).then_inc(S["const_id0"], 1)
            e.memset(ones, 1.0).then_inc(S["const_id0"], 1)
            e.wait_ge(S["const_id0"], 3)
            e.affine_select(out=ident, in_=ident, compare_op=ALU.not_equal, fill=1.0, base=0,
                            pattern=[[-1, P]], channel_multiplier=1).then_inc(S["const_ready"], 1)
            e.affine_select(out=identb, in_=identb, compare_op=ALU.not_equal, fill=1.0, base=0,
                            pattern=[[-1, P]], channel_multiplier=1).then_inc(S["const_ready"], 1)
            for i in range(5):
                end_stage(e, i)

            def keep_h3(t, b, p):
                e.wait_ge(S["h3_ready"], t + 1)
                e.tensor_copy(F[1][:, t, :], XA[b]).then_inc(S["h3_kept"], 1)
            tiles(keep_h3)(e)
            for b in range(2):
                e.memset(PT[b][:, N:NP], 0.0)
            end_stage(e, 5)

            def add_g0(t, b, p):
                e.wait_ge(S["p3_scaled"], t + 1)
                e.tensor_tensor(out=F[2][:, t, :], in0=XA[b], in1=F[2][:, t, :], op=ALU.add).then_inc(S["p3_added"], 1)
            tiles(add_g0)(e)
            end_stage(e, 6)
            e.wait_ge(S["beta_in"], 16)
            e.wait_ge(S["x_back"], 16)

            def add_beta(t, b, p):
                e.tensor_tensor(out=F[1][:, t, :], in0=F[1][:, t, :], in1=beta_b, op=ALU.add).then_inc(S["x_beta"], 1)
            tiles(add_beta)(e)

            def add_z(t, b, p):
                e.wait_ge(S["p4_scaled"], t + 1)
                e.tensor_tensor(out=F[0][:, t, :], in0=XA[b], in1=F[0][:, t, :], op=ALU.add).then_inc(S["p4_added"], 1)
            tiles(add_z)(e)

            def add_attention(t, b, p):
                e.wait_ge(S["xa_ready"], NT + t + 1)
                e.tensor_tensor(out=F[0][:, t, :], in0=XA[b], in1=F[0][:, t, :], op=ALU.add).then_inc(S["z_added"], 1)
            e.wait_ge(S["p4_added"], NT)
            tiles(add_attention)(e)
            for i in (7, 8, 9, 10):
                end_stage(e, i)
            e.memset(encT[:, :, N:NP], 0.0)

            with e.Fori(0, HEADS) as h:
                for i, k in enumerate(BY_POOL):
                    e.wait_ge(S["t_ready"], h * len(BY_POOL) + (i + 1))
                    e.tensor_tensor(out=TP[k % 4], in0=TP[k % 4], in1=maskT[:, k, 0:N], op=ALU.add).then_inc(S["t_masked"], 1)

        @block.scalar
        def _(e):
            roots = [0]

            def root_of(width_):
                roots[0] += 1
                e.wait_ge(S["sqrt_in"], roots[0])
                e.activation(root[:, 0:width_], rad[:, 0:width_], ACT.Sqrt).then_inc(S["sqrt_out"], 1)

            root_of(1)
            e.wait_ge(S["w12_done"], 1)
            e.activation(WQK[:, :, 0:ATTN], ps[:, 1024:1024 + DC * ATTN].rearrange("p (c m) -> p c m", m=ATTN), ACT.Copy)

            def norm_relu(ready, i):
                e.wait_ge(S["ln_affine"], i + 1)

                def body(t, b, p):
                    e.activation(F[1][:, t, :], F[0][:, t, :], ACT.Relu, scale=col(lna, t), bias=col(lnb, t)).then_inc(S[ready], 1)
                return body

            def row_sum(t, b, p):
                e.wait_ge(S[f"row{b}_in"], 32 * (p + 1))
                if not isinstance(t, int) or t >= 1:
                    e.wait_ge(S["rsum_done"], t)
                e.activation(F[2][:, 0:3, :].rearrange("p t d -> p (t d)")[:, 0:NP], ST[b], ACT.Copy, accum_out=col(rsum, t)).then_inc(S["rsum_done"], 1)
            tiles(row_sum, lambda: root_of(NT))(e)
            root_of(NT)
            tiles(norm_relu("h0_ready", 0))(e)
            end_stage(e, 0)


            def stage_s(t, b, p):
                two_back(e, S["l0_product"], t)
                e.activation(STk[b], Smat[:, :, bass.ds(t * P, P)], ACT.Copy).then_inc(S["l0_staged"], 1)
            tiles(stage_s)(e)
            end_stage(e, 1)
            end_stage(e, 2)
            root_of(NT)
            tiles(norm_relu("h1_ready", 1))(e)

            def copy_xi(t, b, p):
                e.wait_ge(S["xi_turned"], t + 1)
                two_back(e, S["sup_done"], t)
                e.activation(XIT[b], bank(2 + b, 256).bitcast(BF16), ACT.Copy).then_inc(S["xi_copied"], 1)
            tiles(copy_xi)(e)
            end_stage(e, 3)

            def split_a(t, b, p):
                e.wait_ge(S[f"at{b}_in"], 16 * ((6, 5)[b] + p + 1))
                two_back(e, S["p2_product"], t)
                e.activation(A_PARTS[0][b], ST[b], ACT.Copy).then_inc(S["a_high"], 1)
                e.wait_ge(S["a_rest"], t + 1)
                e.activation(A_PARTS[1][b], a_left, ACT.Copy).then_inc(S["a_mid"], 1)
            tiles(split_a)(e)
            end_stage(e, 4)
            root_of(NT)
            e.wait_ge(S["ln_affine"], 3)

            def h3(t, b):
                two_back(e, S["h3_turned"], t)
                two_back(e, S["h3_kept"], t)
                e.activation(XA[b], F[0][:, t, :], ACT.Relu, scale=col(lna, t), bias=col(lnb, t)).then_inc(S["h3_ready"], 1)

            def keep_projections(t, b, p):
                e.wait_ge(S["h3_turned"], t + 1)
                two_back(e, S["qk_done"], t)
                e.activation(HT[b], bank(2 + b), ACT.Copy).then_inc(S["h3_copied"], 1)
                if not isinstance(t, int) or t < NT - 1:
                    h3(t + 1, 1 - b)
                e.wait_ge(S["g1_done"], t + 1)
                e.activation(F[3][:, t, :], bank(1 + 4 * b), ACT.Copy).then_inc(S["g1_kept"], 1)
                e.wait_ge(S["qk_done"], t + 1)
                e.activation(QKT[:, bass.ds(t * P, P)], bank(6 + b, P), ACT.Copy).then_inc(S["qk_kept"], 1)
            h3(0, 0)
            tiles(keep_projections)(e)
            end_stage(e, 5)

            def stage_q(s, t, b):
                two_back(e, S["logits"], t, NT * s)
                e.activation(QS[b][ATTN:, :], QKT[0:ATTN, bass.ds(t * P, P)], ACT.Copy).then_inc(S["q_staged"], 1)

            def softmax(s):
                def body(t, b, p):
                    if not isinstance(t, int) or t < NT - 1:
                        stage_q(s, t + 1, 1 - b)
                    e.wait_ge(S["nmax"], NT * s + t + 1)
                    e.activation(E[:, t, :], ps[:, b * 1536:b * 1536 + N], ACT.Exp, bias=col(nmax, t), accum_out=col(Zs, t)).then_inc(S["exp_done"], 1)
                return body

            def halve(s, g, r):
                n, (_, m, z) = s * len(GROUPS[0]) + g, GROUPS[s][g]
                done = 2 * ROUNDS * sum(zz - mm for _, mm, zz in (GROUPS[0] + GROUPS[1])[:n])
                e.wait_ge(S["mid_ready"], (ROUNDS + 1) * n + 1 + r)
                for i, (func, sums) in enumerate(((ACT.Sign, signs), (ACT.Relu, bound))):
                    for t in range(m, z):
                        k = i * (z - m) + t - m
                        if k:
                            e.wait_ge(S["act_sum"], 2 * (z - m) * r + (done + k))
                        e.activation(act_scratch, E[:, t, :], func, bias=mid[:, t:t + 1],
                                     accum_out=sums[:, t:t + 1]).then_inc(S["act_sum"], 1)

            def scale_product(s):
                name = ("p3", "p4")[s]

                def body(t, b, p):
                    halve(s, 0, 2 * t)
                    e.wait_ge(S[f"{name}_product"], t + 1)
                    two_back(e, S[f"{name}_added"], t)
                    e.activation(XA[b], bank(6 + b), ACT.Identity, scale=col(rinv, t)).then_inc(S[f"{name}_scaled"], 1)
                    halve(s, 0, 2 * t + 1)
                return body

            def turned(s, t):
                e.wait_ge(S["pt_turned"], NT * s + t + 1)
                two_back(e, S["att_done"], t, NT * s)
                e.activation(ST[t % 2], ps[:, 0:NP], ACT.Copy).then_inc(S["pt_copied"], 1)

            def attention_steps(s, t):
                b = t % 2

                def scaled():
                    e.wait_ge(S["att_done"], NT * s + t + 1)
                    e.wait_ge(S["rk_ready"], NT * s + t + 1)
                    if s == 1:
                        two_back(e, S["z_added"], t)
                    e.activation(XA[b * s], bank(6), ACT.Identity, scale=col(rk, t)).then_inc(S["xa_ready"], 1)

                def xa_turned():
                    e.wait_ge(S["xa_turned"], t + 1)
                    e.activation(HT[0], bank(7), ACT.Copy).then_inc(S["xa_copied"], 1)

                def sums():
                    e.wait_ge(S["xu_done"], t + 1)
                    e.activation(F[0][:, t, :], bank(6), ACT.Copy).then_inc(S["xu_kept"], 1)
                    e.wait_ge(S["g2_done"], t + 1)
                    e.activation(F[3][:, t, :], bank(7), ACT.Copy)

                def scores():
                    e.wait_ge(S["qk2_done"], t + 1)
                    e.activation(QKT[:, bass.ds(t * P, P)], bank(6, P), ACT.Copy).then_inc(S["qk2_kept"], 1)

                def next_turned():
                    if t + 1 not in [a for a, _, _ in GROUPS[s]] + [NT]:
                        turned(s, t + 1)

                if s:
                    return [(.5, scaled), (.6, next_turned)]
                return [(.4, scaled), (.45, xa_turned), (.5, next_turned), (.9, sums), (.95, scores)]

            for s in range(2):
                stage_q(s, 0, 0)
                tiles(softmax(s))(e)
                tiles(scale_product(s))(e)
                halve(s, 0, ROUNDS - 2)
                halve(s, 0, ROUNDS - 1)
                e.wait_ge(S[("p3_added", "p4_added")[s]], NT)
                for g, (a, m, z) in enumerate(GROUPS[s]):
                    first = z - 3 if g + 1 < len(GROUPS[s]) else z
                    turned(s, a)
                    for t in range(a, first):
                        for _, step in attention_steps(s, t):
                            step()
                    steps = [(int(ROUNDS * (t - first + part) / (z - first)), step)
                             for t in range(first, z) for part, step in attention_steps(s, t)]
                    for r in range(ROUNDS if steps else 0):
                        halve(s, g + 1, r)
                        for at_round, step in steps:
                            if at_round == r:
                                step()
                end_stage(e, 6 + s)
            root_of(NT)
            e.wait_ge(S["ln_affine"], 4)

            def y_norm(t, b, p):
                two_back(e, S["x3_ready"], t)
                e.activation(XA[b], F[0][:, t, :], ACT.Identity, scale=col(lna, t), bias=col(lnb, t)).then_inc(S["y_ready"], 1)
            tiles(y_norm)(e)
            end_stage(e, 8)
            root_of(NT)
            e.wait_ge(S["ln_affine"], 5)

            def h4(t, b):
                two_back(e, S["h4_turned"], t)
                e.activation(XA[b], F[0][:, t, :], ACT.Relu, scale=col(lna, t), bias=col(lnb, t)).then_inc(S["h4_ready"], 1)

            def keep_wh(t, b, p):
                e.wait_ge(S["h4_turned"], t + 1)
                two_back(e, S["wh_done"], t)
                e.activation(HT[b], bank(2 + b), ACT.Copy).then_inc(S["h4_copied"], 1)
                if not isinstance(t, int) or t < NT - 1:
                    h4(t + 1, 1 - b)
                e.wait_ge(S["wh_done"], t + 1)
                e.activation(Wh[:, t, :], bank(b), ACT.Copy).then_inc(S["wh_kept"], 1)
            h4(0, 0)
            tiles(keep_wh)(e)
            e.wait_ge(S["ed_turned"], 1)
            e.activation(QKT[0:8, :], ps[0:8, 4 * 512:4 * 512 + NP], ACT.Copy).then_inc(S["ed_row"], 1)
            e.wait_ge(S["ed_row"], 1)
            end_stage(e, 9)
            e.wait_ge(S["ab_turned"], 1)
            e.wait_ge(S["rows_out"], 16)
            e.activation(QKT[0:16, :], ps[0:16, 0:NP], ACT.Copy).then_inc(S["ab_rows"], 1)
            end_stage(e, 10)

            def head(h, b, p):
                if not isinstance(h, int):
                    e.wait_ge(S["p_used"], NT * (h - 1))
                e.activation(WS[b][:, :, b * HD:(b + 1) * HD], Wh[:, :, bass.ds(h * HD, HD)], ACT.Copy).then_inc(S["wh_staged"], 1)
                for k in range(NT):
                    if k in BY_VECTOR:
                        e.wait_ge(S["t_masked_own"], h * len(BY_VECTOR) + (BY_VECTOR.index(k) + 1))
                    else:
                        e.wait_ge(S["t_masked"], h * len(BY_POOL) + (BY_POOL.index(k) + 1))
                    ring_free(e, S["p_used"], h, k)
                    e.activation(PP[k % 4], TP[k % 4], ACT.Exp, bias=ed2[:, k, bass.ds(h, 1)]).then_inc(S["p_exp"], 1)
                    if k == 3 and not (isinstance(h, int) and h == 0):
                        keep_head(h - 1, 1 - b, p)
                if not isinstance(h, int) and b == 0:
                    elu(p - 1)

            def keep_head(h, b, p):
                e.wait_ge(S["p_used"], NT * (h + 1))
                if b == 0 and not isinstance(h, int):
                    e.wait_ge(S["enc_ready"], p)
                mine, other = slice(b * HD, (b + 1) * HD), slice((1 - b) * HD, (2 - b) * HD)
                e.activation(sums[mine], ps[other, b * 1536:b * 1536 + N], ACT.Copy).then_inc(S["head_kept"], 1)
                e.activation(heads2[mine], ps[mine, b * 1536:b * 1536 + N], ACT.Copy).then_inc(S["head_kept"], 1)

            def elu(pair):
                e.wait_ge(S["ev_c"], pair + 1)
                e.activation(neg, neg, ACT.Exp).then_inc(S["ev_exp"], 1)

            head(0, 0, 0)
            head(1, 1, 0)
            with e.Fori(1, HEADS // 2) as p:
                head(2 * p, 0, p)
                head(2 * p + 1, 1, p)
            keep_head(HEADS - 1, 1, 0)
            elu(HEADS // 2 - 1)
            e.wait_ge(S["mlp_in"], 96)
            for m in range(2):
                e.wait_ge(S["o1_done"], m + 1)
                e.activation(o1T[:, m, :], ps[:, m * 1536:m * 1536 + NP], ACT.Relu, bias=bcols[:, m:m + 1]).then_inc(S["o1_kept"], 1)
            e.wait_ge(S["o2_done"], 1)
            e.activation(o2T, ps[:, 0:NP], ACT.Relu, bias=bcols[:, 2:3]).then_inc(S["o2_kept"], 1)
            for m in range(2):
                e.wait_ge(S["o3_done"], m + 1)
                off = (1 - m) * 1536
                e.activation(o3T[:, m, :], ps[:, off:off + NP], ACT.Relu, bias=bcols[:, 3 + m:4 + m]).then_inc(S["o3_kept"], 1)

        @block.vector
        def _(e):
            chain = [0]
            roots = [0]

            def link(ins_):
                chain[0] += 1
                ins_.then_inc(S["link"], 1)
                e.wait_ge(S["link"], chain[0])

            def ts(out_, in_, s1, s2, op0, op1=None):
                if op1 is None:
                    return e.tensor_scalar(out_, in_, s1, None, op0)
                return e.tensor_scalar(out_, in_, s1, s2, op0, op1)

            def inverse_root(w, dst):
                r, q = root[:, 0:w], rad[:, 0:w]
                roots[0] += 1
                e.wait_ge(S["sqrt_out"], roots[0])
                link(e.reciprocal(dst, r))
                link(e.tensor_tensor(out=dst, in0=dst, in1=q, op=ALU.mult))
                link(e.tensor_tensor(out=dst, in0=dst, in1=r, op=ALU.add))
                link(ts(dst, dst, 0.5, None, ALU.mult))
                link(e.reciprocal(dst, dst))

            def layer_norm_stats(src):
                def body(t, b, p):
                    e.bn_stats(out=stats[:, t, :], in_=src[:, t, :]).then_inc(S["ln_stats"], 1)
                return body

            def layer_norm_columns(i):
                e.wait_ge(S["ln_stats"], NT * (i + 1))
                me, se, mo, so = (stats[:, :, j] for j in (1, 2, 4, 5))
                link(e.tensor_tensor(out=lt[0], in0=me, in1=mo, op=ALU.add))
                link(e.tensor_tensor(out=lt[1], in0=me, in1=mo, op=ALU.subtract))
                link(e.tensor_tensor(out=lt[1], in0=lt[1], in1=lt[1], op=ALU.mult))
                link(e.tensor_tensor(out=lt[2], in0=se, in1=so, op=ALU.add))
                link(ts(lt[2], lt[2], 1.0 / D, EPS, ALU.mult, ALU.add))
                e.scalar_tensor_tensor(out=rad, in0=lt[1], scalar=0.25, in1=lt[2], op0=ALU.mult, op1=ALU.add).then_inc(S["sqrt_in"], 1)
                inverse_root(NT, lna)
                e.scalar_tensor_tensor(out=lnb, in0=lt[0], scalar=-0.5, in1=lna, op0=ALU.mult, op1=ALU.mult).then_inc(S["ln_affine"], 1)

            e.wait_ge(S["w_in"], 16)
            e.tensor_reduce(out=small[:, 0:1], in_=w_raw, op=ALU.add, axis=AX_X).then_inc(S["wsum_ready"], 1)
            e.wait_ge(S["wtot_done"], 1)
            link(ts(small[:, 1:2], bank(0, 1), 1.0 / (D * D), None, ALU.mult))
            link(ts(w_cen, w_raw, small[:, 1:2], None, ALU.subtract))
            e.scalar_tensor_tensor(out=w_raw, in0=w_cen, scalar=1.0, in1=w_cen, op0=ALU.mult, op1=ALU.mult,
                                   accum_out=small[:, 2:3]).then_inc(S["wsq_ready"], 1)
            e.wait_ge(S["wtot2_done"], 1)
            ts(rad[:, 0:1], bank(1, 1), 1.0 / (D * D - 1), None, ALU.mult).then_inc(S["sqrt_in"], 1)
            inverse_root(1, small[:, 3:4])
            e.wait_ge(S["scal_in"], 16)
            link(e.reciprocal(small[:, 4:8], scal[:, 0:4]))
            link(ts(w_cen, w_cen, small[:, 3:4], small[:, 5:6], ALU.mult, ALU.mult))
            link(ts(w_cen, w_cen, -1.0, 1.0, ALU.max, ALU.min))
            link(ts(w_cen, w_cen, WGT_LEVELS, MAGIC, ALU.mult, ALU.add))
            link(ts(wq.rearrange("p c d -> p (c d)"), w_cen, MAGIC, None, ALU.subtract))
            link(e.tensor_tensor(out=small[:, 8:9], in0=scal[:, 1:2], in1=scal[:, 2:3], op=ALU.mult))
            link(ts(small[:, 8:9], small[:, 8:9], 1.0 / (ACT_LEVELS * WGT_LEVELS), None, ALU.mult))
            link(e.tensor_tensor(out=small[:, 9:10], in0=scal[:, 0:1], in1=small[:, 4:5], op=ALU.mult))
            link(e.tensor_tensor(out=small[:, 9:10], in0=small[:, 9:10], in1=scal[:, 3:4], op=ALU.mult))
            link(ts(small[:, 9:10], small[:, 9:10], 1.0 / ACT_LEVELS, None, ALU.mult))

            def x_columns():
                e.wait_ge(S["x_in"], 16)
                tiles(layer_norm_stats(F[0]))(e)
                layer_norm_columns(0)

            def degrees(t, b, p):
                e.wait_ge(S[f"row{b}_in"], 32 * (p + 1))
                e.scalar_tensor_tensor(out=Smat[:, t, :], in0=ST[b], scalar=0.0, in1=PT[b], op0=ALU.add, op1=ALU.add,
                                       accum_out=col(deg, t)).then_inc(S["deg_done"], 1)
            tiles(degrees, x_columns)(e)
            e.wait_ge(S["deg_done"], NT)
            link(ts(deg, deg, 0.5, 1.0, ALU.mult, ALU.add))
            e.tensor_scalar(rad, deg, 1e-30, None, ALU.max).then_inc(S["sqrt_in"], 1)
            inverse_root(NT, dinv)
            link(e.scalar_tensor_tensor(out=dinv, in0=deg, scalar=0.0, in1=dinv, op0=ALU.is_gt, op1=ALU.mult))
            e.wait_ge(S["rsum_done"], NT)
            link(ts(rinv, rsum, 1.0, 1e-12, ALU.add, ALU.max))
            link(e.reciprocal(rinv, rinv))
            end_stage(e, 0)

            def scale_h(t, b, p):
                e.wait_ge(S["h0_ready"], t + 1)
                ts(F[1][:, t, :], F[1][:, t, :], col(dinv, t), None, ALU.mult).then_inc(S["l0_half"], 1)
            tiles(scale_h)(e)

            def l0_evacuate(t, b, p):
                e.wait_ge(S["l0_product"], t + 1)
                two_back(e, S["l0_scaled"], t)
                e.scalar_tensor_tensor(out=XA[b], in0=bank(b), scalar=0.5, in1=F[1][:, t, :], op0=ALU.mult, op1=ALU.add).then_inc(S["l0_half"], 1)
                e.wait_ge(S["l0_half"], NT + t + 1)
                ts(F[2][:, t, :], XA[b], col(dinv, t), None, ALU.mult).then_inc(S["l0_scaled"], 1)
            tiles(l0_evacuate)(e)
            end_stage(e, 1)

            def add_p1(t, b, p):
                e.wait_ge(S["p1_product"], t + 1)
                e.tensor_tensor(out=F[0][:, t, :], in0=bank(b), in1=F[0][:, t, :], op=ALU.add).then_inc(S["p1_added"], 1)
                e.wait_ge(S["p1_added"], t + 1)
                layer_norm_stats(F[0])(t, b, p)
            tiles(add_p1)(e)
            end_stage(e, 2)

            layer_norm_columns(1)

            def quantise_input(t, b):
                e.wait_ge(S["h1_ready"], t + 1)
                two_back(e, S["q_ready"], t)
                ts(QT[b], F[1][:, t, :], small[:, 6:7], 1.0, ALU.mult, ALU.min).then_inc(S["q_a"], 1)
                e.wait_ge(S["q_a"], t + 1)
                ts(SQ[b], QT[b], ACT_LEVELS, MAGIC, ALU.mult, ALU.add).then_inc(S["q_b"], 1)
                e.wait_ge(S["q_b"], t + 1)
                two_back(e, S["xi_turned"], t)
                ts(XI[b], SQ[b], MAGIC, None, ALU.subtract).then_inc(S["xi_ready"], 1)

            def quantise_support(t, b, p):
                if not isinstance(t, int) or t < NT - 1:
                    quantise_input(t + 1, 1 - b)
                e.wait_ge(S["sup_done"], t + 1)
                ts(QT[b], bank(b), small[:, 8:9], 0.0, ALU.mult, ALU.max).then_inc(S["sup_a"], 1)
                e.wait_ge(S["sup_a"], t + 1)
                ts(SQ[b], QT[b], small[:, 7:8], 1.0, ALU.mult, ALU.min).then_inc(S["sup_b"], 1)
                e.wait_ge(S["sup_b"], t + 1)
                ts(QT[b], SQ[b], ACT_LEVELS, MAGIC, ALU.mult, ALU.add).then_inc(S["sup_c"], 1)
                e.wait_ge(S["sup_c"], t + 1)
                ts(q16[:, t, :], QT[b], MAGIC, None, ALU.subtract).then_inc(S["q_ready"], 1)
            quantise_input(0, 0)
            tiles(quantise_support)(e)
            end_stage(e, 3)

            def split_a(t, b):
                e.wait_ge(S["a_high"], t + 1)
                if not isinstance(t, int) or t >= 1:
                    e.wait_ge(S["a_low"], t)
                e.tensor_tensor(out=a_left, in0=ST[b], in1=A_PARTS[0][b], op=ALU.subtract).then_inc(S["a_rest"], 1)
                e.wait_ge(S["a_mid"], t + 1)
                two_back(e, S["p2_product"], t)
                e.tensor_tensor(out=A_PARTS[2][b], in0=a_left, in1=A_PARTS[1][b], op=ALU.subtract).then_inc(S["a_low"], 1)

            def add_p2(t, b, p):
                if not isinstance(t, int) or t < NT - 1:
                    split_a(t + 1, 1 - b)
                e.wait_ge(S["p2_product"], t + 1)
                e.scalar_tensor_tensor(out=F[0][:, t, :], in0=bank(b), scalar=small[:, 9:10], in1=F[0][:, t, :],
                                       op0=ALU.mult, op1=ALU.add).then_inc(S["p2_added"], 1)
                e.wait_ge(S["p2_added"], t + 1)
                layer_norm_stats(F[0])(t, b, p)
            split_a(0, 0)
            tiles(add_p2)(e)
            end_stage(e, 4)

            layer_norm_columns(2)

            def keep_g0(t, b, p):
                e.wait_ge(S["g0_done"], t + 1)
                e.tensor_copy(F[2][:, t, :], bank(4 * b)).then_inc(S["g0_kept"], 1)
            tiles(keep_g0)(e)
            end_stage(e, 5)

            def row_max(s):
                def body(t, b, p):
                    e.wait_ge(S["logits"], NT * s + t + 1)
                    e.tensor_reduce(out=col(nmax, t), in_=ps[:, b * 1536:b * 1536 + N], op=ALU.max, axis=AX_X, negate=True).then_inc(S["nmax"], 1)
                return body

            def search(s, g):
                a, m, z = GROUPS[s][g]
                n, own, cs, sh = s * len(GROUPS[0]) + g, m - a, slice(a, z), slice(m, z)
                before = (GROUPS[0] + GROUPS[1])[:n]
                q, q0 = S["search_s"], 4 * ROUNDS * n
                own0 = ROUNDS * sum(mm - aa for aa, mm, _ in before)
                act0 = 2 * ROUNDS * sum(zz - mm for _, mm, zz in before)

                def halve(r):
                    def sum_above(j):
                        t = a + j
                        if j >= 2:
                            e.wait_ge(S["search_e"], own * r + (own0 + j - 1))
                        e.scalar_tensor_tensor(out=SCRATCH[j % 2], in0=E[:, t, :], scalar=mid[:, t:t + 1], in1=E[:, t, :],
                                               op0=ALU.is_gt, op1=ALU.mult, accum_out=Fm[:, t:t + 1]).then_inc(S["search_e"], 1)
                    sum_above(0)
                    ts(base[:, cs], mid[:, cs], col(widths, r + 1), None, ALU.subtract).then_inc(q, 1)
                    for j in range(1, own - 1):
                        sum_above(j)
                    e.wait_ge(S["act_sum"], 2 * (z - m) * r + (act0 + z - m))
                    e.scalar_tensor_tensor(out=ge[:, sh], in0=signs[:, sh], scalar=float(N), in1=mid[:, sh],
                                           op0=ALU.add, op1=ALU.mult).then_inc(q, 1)
                    e.wait_ge(q, 4 * r + (q0 + 2))
                    e.scalar_tensor_tensor(out=Fm[:, sh], in0=ge[:, sh], scalar=0.5, in1=tau[:, sh],
                                           op0=ALU.mult, op1=ALU.add).then_inc(q, 1)
                    sum_above(own - 1)
                    e.wait_ge(q, 4 * r + (q0 + 3))
                    e.wait_ge(S["act_sum"], 2 * (z - m) * r + (act0 + 2 * (z - m)))
                    e.wait_ge(S["search_e"], own * r + (own0 + own))
                    e.tensor_tensor(out=ge[:, cs], in0=Fm[:, cs], in1=bound[:, cs], op=ALU.is_ge).then_inc(q, 1)
                    e.wait_ge(q, 4 * r + (q0 + 4))
                    e.scalar_tensor_tensor(out=mid[:, cs], in0=ge[:, cs], scalar=col(widths, r), in1=base[:, cs],
                                           op0=ALU.mult, op1=ALU.add).then_inc(S["mid_ready"], 1)
                    e.wait_ge(S["mid_ready"], r + ((ROUNDS + 1) * n + 2))

                link(e.tensor_copy(bound[:, a:m], tau[:, a:m]))
                link(e.memset(mid[:, a:m], 0.5))
                e.memset(mid[:, sh], -0.5).then_inc(S["mid_ready"], 1)
                e.wait_ge(S["mid_ready"], (ROUNDS + 1) * n + 1)
                with e.Fori(0, ROUNDS // 4) as i:
                    for u in range(4):
                        halve(4 * i + u)
                link(e.tensor_copy(lo[:, a:m], mid[:, a:m]))
                link(ts(hi[:, a:m], mid[:, a:m], 2.0 ** -ROUNDS, None, ALU.add))
                link(ts(hi[:, sh], mid[:, sh], -1.0, None, ALU.mult))
                link(ts(lo[:, sh], hi[:, sh], 2.0 ** -ROUNDS, None, ALU.subtract))

            def select(s, t, b, in_bracket):
                two_back(e, S["pt_turned"], t, NT * s)
                n = NT * s + t
                Et, Pt, sc = E[:, t, :], PT[b][:, 0:N], ps[:, 1536:1536 + N + 1]
                e.scalar_tensor_tensor(out=Pt, in0=Et, scalar=col(hi, t), in1=Et, op0=ALU.is_gt, op1=ALU.mult,
                                       accum_out=col(Fm, t)).then_inc(S["pick0"], 1)
                e.wait_ge(S["pick0"], n + 1)
                e.tensor_tensor(out=Rem[b], in0=col(tau, t), in1=col(Fm, t), op=ALU.subtract).then_inc(S["pick1"], 1)
                e.scalar_tensor_tensor(out=Et, in0=Et, scalar=col(lo, t), in1=Et, op0=in_bracket, op1=ALU.mult).then_inc(S["pick1"], 1)
                e.wait_ge(S["pick1"], 2 * n + 2)
                e.tensor_tensor_scan(sc[:, 1:N + 1], Et, Pt, 0.0, ALU.add, ALU.subtract).then_inc(S["pick2"], 1)
                e.wait_ge(S["pick2"], n + 1)
                e.scalar_tensor_tensor(out=Et, in0=sc[:, 0:N], scalar=Rem[b], in1=Et, op0=ALU.is_lt, op1=ALU.mult).then_inc(S["pick3"], 1)
                e.wait_ge(S["pick3"], n + 1)
                e.scalar_tensor_tensor(out=Pt, in0=Pt, scalar=1.0, in1=Et, op0=ALU.mult, op1=ALU.max,
                                       accum_out=col(kept, t)).then_inc(S["keep_ready"], 1)
                e.wait_ge(S["keep_ready"], n + 1)
                e.reciprocal(col(rk, t), col(kept, t)).then_inc(S["rk_ready"], 1)

            for r in range(ROUNDS + 1):
                link(e.memset(widths[:, r:r + 1], 2.0 ** -min(r + 1, ROUNDS)))
            for s in range(2):
                tiles(row_max(s))(e)
                e.wait_ge(S["exp_done"], NT * (s + 1))
                link(ts(tau, Zs, P_TOP, None, ALU.mult))
                for g, (a, m, z) in enumerate(GROUPS[s]):
                    search(s, g)
                    link(e.memset(ps[:, 1536:1537], 0.0))
                    for t in range(a, z):
                        select(s, t, t % 2, ALU.is_gt if t < m else ALU.is_ge)
                if s == 1:
                    def y_stats(t, b, p):
                        e.wait_ge(S["z_added"], t + 1)
                        layer_norm_stats(F[0])(t, b, p)
                    tiles(y_stats)(e)
                end_stage(e, 6 + s)

            layer_norm_columns(3)
            e.wait_ge(S["gam_in"], 16)

            def finish_y(t, b, p):
                e.wait_ge(S["y_ready"], t + 1)
                e.tensor_tensor(out=XA[b], in0=XA[b], in1=gamma_b, op=ALU.mult).then_inc(S["y_a"], 1)
                e.wait_ge(S["y_a"], t + 1)
                e.wait_ge(S["x_beta"], t + 1)
                e.tensor_tensor(out=F[0][:, t, :], in0=XA[b], in1=F[1][:, t, :], op=ALU.add).then_inc(S["x3_ready"], 1)
                e.wait_ge(S["x3_ready"], t + 1)
                layer_norm_stats(F[0])(t, b, p)
            tiles(finish_y)(e)
            end_stage(e, 8)

            layer_norm_columns(4)
            e.wait_ge(S["wcat_in"], 48)

            def scores(t, b, p):
                e.wait_ge(S["wh_kept"], t + 1)
                if not isinstance(t, int) or t >= 1:
                    e.wait_ge(S["scores_kept"], 2 * t)
                for i, ab in enumerate((a1b, a2b)):
                    e.tensor_tensor(out=prod[i], in0=Wh[:, t, :], in1=ab, op=ALU.mult).then_inc(S["wh_prod"], 1)
                for i, dst in enumerate((es[:, t, :], ed[:, t, :])):
                    e.wait_ge(S["wh_prod"], 2 * t + i + 1)
                    e.tensor_reduce(out=dst, in_=prod[i].rearrange("p (h d) -> p h d", d=HD), op=ALU.add, axis=AX_X).then_inc(S["scores_kept"], 1)
                e.wait_ge(S[f"row{b}_in"], 32 * (p + 1 + (6, 5)[b]))
                ts(mneg[:, t, :], ST[b], 0.0, FAR, ALU.is_le, ALU.mult)
                ts(maskT[:, t, :], PT[b], 0.0, FAR, ALU.is_le, ALU.mult).then_inc(S["mask_done"], 1)
            tiles(scores)(e)
            e.wait_ge(S["scores_kept"], 2 * NT)
            e.wait_ge(S["wh_done"], NT)
            for b in range(2):
                link(e.memset(WS[b][:, :, (1 - b) * HD:(2 - b) * HD], 1.0))
            end_stage(e, 9)

            def dmax(b):
                for t in range(NT):
                    e.tensor_tensor_reduce(out=junk[t], in0=DB[b], in1=mneg[:, t, 0:N], scale=1.0, scalar=4 * FAR,
                                           op0=ALU.add, op1=ALU.max, accum_out=Dst[b][:, t:t + 1]).then_inc(S["dmax_step"], 1)

            def keep_dmax(h, b):
                e.wait_ge(S["dmax_step"], NT * (h + 1))
                e.tensor_copy(Dm[:, :, bass.ds(h, 1)].rearrange("p t o -> p (t o)"), Dst[b]).then_inc(S["dmax_kept"], 1)

            e.wait_ge(S["db0_in"], 16)
            dmax(0)
            with e.Fori(1, HEADS // 2) as p:
                e.wait_ge(S["db1_in"], 16 * p)
                keep_dmax(2 * p - 2, 0)
                dmax(1)
                e.wait_ge(S["db0_in"], 16 * p + 16)
                keep_dmax(2 * p - 1, 1)
                dmax(0)
            e.wait_ge(S["db1_in"], 16 * (HEADS // 2))
            keep_dmax(HEADS - 2, 0)
            dmax(1)
            keep_dmax(HEADS - 1, 1)
            e.wait_ge(S["dmax_kept"], HEADS)
            link(e.scalar_tensor_tensor(out=Dm, in0=Dm, scalar=0.5 * FAR, in1=Dm, op0=ALU.is_gt, op1=ALU.mult))
            link(e.tensor_tensor(out=c1, in0=Dm, in1=es, op=ALU.add))
            link(e.scalar_tensor_tensor(out=c2, in0=c1, scalar=ALPHA, in1=c1, op0=ALU.mult, op1=ALU.max))
            link(e.tensor_tensor(out=abc[:, :, 0:8], in0=es, in1=c2, op=ALU.subtract))
            link(e.scalar_tensor_tensor(out=abc[:, :, 8:16], in0=es, scalar=ALPHA, in1=c2, op0=ALU.mult, op1=ALU.subtract))
            link(ts(ed8, ed, 1.0 - ALPHA, None, ALU.mult))
            ts(ed2, ed, ALPHA, None, ALU.mult).then_inc(S["ab_ready"], 1)
            end_stage(e, 10)

            def invert(pair):
                e.wait_ge(S["head_kept"], 4 * (pair + 1))
                e.reciprocal(sums, sums).then_inc(S["inverses"], 1)

            def divide(pair):
                e.wait_ge(S["inverses"], pair + 1)
                e.tensor_tensor(out=heads2, in0=heads2, in1=sums, op=ALU.mult).then_inc(S["ev_b"], 1)
                e.wait_ge(S["ev_b"], pair + 1)
                if not isinstance(pair, int) or pair > 0:
                    e.wait_ge(S["enc_ready"], pair)
                ts(neg, heads2, 0.0, None, ALU.min).then_inc(S["ev_c"], 1)

            def elu(pair):
                e.wait_ge(S["ev_exp"], pair + 1)
                dst = encT[:, bass.ds(pair, 1), 0:N].rearrange("p o n -> p (o n)")
                e.scalar_tensor_tensor(out=dst, in0=neg, scalar=-1.0, in1=heads2, op0=ALU.add, op1=ALU.max).then_inc(S["enc_ready"], 1)

            def head(h, b, p):
                e.wait_ge(S[f"ab{b}_in"], 32 * (p + 1))
                for k in range(NT):
                    ring_free(e, S["p_exp"], h, k)
                    e.scalar_tensor_tensor(out=TP[k % 4], in0=AB[b][0], scalar=ed8[:, k, bass.ds(h, 1)], in1=AB[b][1],
                                           op0=ALU.add, op1=ALU.max).then_inc(S["t_own" if k in BY_VECTOR else "t_ready"], 1)
                    if k - 1 in BY_VECTOR:
                        n = BY_VECTOR.index(k - 1) + 1
                        e.wait_ge(S["t_own"], h * len(BY_VECTOR) + n)
                        T = TP[(k - 1) % 4]
                        e.tensor_tensor(out=T, in0=T, in1=maskT[:, k - 1, 0:N], op=ALU.add).then_inc(S["t_masked_own"], 1)
                    if not isinstance(h, int) and (b, k) in FINISH:
                        FINISH[b, k](p - 1)

            FINISH = {(0, 6): invert, (0, 9): divide, (1, 1): elu}
            head(0, 0, 0)
            head(1, 1, 0)
            with e.Fori(1, HEADS // 2) as p:
                head(2 * p, 0, p)
                head(2 * p + 1, 1, p)
            for finish_pair in (invert, divide, elu):
                finish_pair(HEADS // 2 - 1)

            e.wait_ge(S["mlp_in"], 96)

            def finish(t, b, p):
                e.wait_ge(S["y4_done"], t + 1)
                two_back(e, S["out_ready"], t)
                e.tensor_tensor(out=XA[b], in0=bank(6 + b), in1=b4b, op=ALU.add).then_inc(S["out_a"], 1)
                e.wait_ge(S["out_a"], t + 1)
                e.tensor_tensor(out=F[0][:, t, :], in0=XA[b], in1=F[0][:, t, :], op=ALU.add).then_inc(S["out_ready"], 1)
            tiles(finish)(e)

        @block.tensor
        def _(e):
            def product(acc, lhs, rhs, last_open=False):
                for k in range(NT):
                    last = e.matmul(acc, lhs[:, k, :], rhs[:, k, :], start=(k == 0), stop=(k == NT - 1 and not last_open))
                return last

            def adjacency_product(name, rhs, base_bank, loads_before, free, with_self):
                def body(t, b, p):
                    e.wait_ge(S[f"at{b}_in"], 16 * (loads_before[b] + p + 1))
                    two_back(e, S[free], t)
                    last = product(bank(base_bank + b), STk[b], rhs, with_self)
                    if with_self:
                        last = e.matmul(bank(base_bank + b), ident, rhs[:, t, :], start=False, stop=True)
                    last.then_inc(S[f"{name}_product"], 1)
                return body

            e.wait_ge(S["const_id0"], 3)
            e.wait_ge(S["const_ready"], 2)
            e.wait_ge(S["wsum_ready"], 1)
            e.matmul(bank(0, 1), ones, small[:, 0:1], start=True, stop=True).then_inc(S["wtot_done"], 1)
            e.wait_ge(S["wsq_ready"], 1)
            e.matmul(bank(1, 1), ones, small[:, 2:3], start=True, stop=True).then_inc(S["wtot2_done"], 1)
            e.wait_ge(S["attn_w_in"], 48)
            for c in range(DC):
                last = e.matmul(bank(2)[:, c * ATTN:(c + 1) * ATTN], w1t[:, c * P:(c + 1) * P], w2, start=True, stop=True)
            last.then_inc(S["w12_done"], 1)
            end_stage(e, 0)

            e.wait_ge(S["l0_half"], NT)

            def l0(t, b, p):
                e.wait_ge(S["l0_staged"], t + 1)
                two_back(e, S["l0_scaled"], t)
                product(bank(b), STk[b], F[1]).then_inc(S["l0_product"], 1)
            tiles(l0)(e)
            end_stage(e, 1)
            tiles(adjacency_product("p1", F[2], 0, (0, 0), "p1_added", False))(e)
            end_stage(e, 2)

            def support(t, b, p):
                e.wait_ge(S["xi_ready"], t + 1)
                two_back(e, S["xi_copied"], t)
                for c in range(DC):
                    last = e.transpose(bank(2 + b, 256).bitcast(BF16)[:, c * P:(c + 1) * P], XI[b][:, c * P:(c + 1) * P], identb)
                last.then_inc(S["xi_turned"], 1)
                e.wait_ge(S["xi_copied"], t + 1)
                two_back(e, S["sup_a"], t)
                for c in range(DC):
                    last = e.matmul(bank(b), XIT[b][:, c * P:(c + 1) * P], wq[:, c, :], start=(c == 0), stop=(c == DC - 1))
                last.then_inc(S["sup_done"], 1)
            tiles(support)(e)
            end_stage(e, 3)

            def quantised_product(t, b, p):
                e.wait_ge(S["a_low"], t + 1)
                two_back(e, S["p2_added"], t)
                for i in range(3):
                    part = A_PARTS[i][b].rearrange("p (k n) -> p k n", n=P)
                    for k in range(NT):
                        last = e.matmul(bank(b), part[:, k, :], q16[:, k, :], start=(i + k == 0), stop=(i == 2 and k == NT - 1))
                last.then_inc(S["p2_product"], 1)
            tiles(quantised_product)(e)
            end_stage(e, 4)

            e.wait_ge(S["u_in"], 32)

            def project(acc, turned, weights):
                for c in range(DC):
                    last = e.matmul(acc, turned[:, c, :], weights[:, c, :], start=(c == 0), stop=(c == DC - 1))
                return last

            def turn(acc, tile):
                for c in range(DC):
                    last = e.transpose(acc[:, c * P:(c + 1) * P], tile[:, c * P:(c + 1) * P], ident)
                return last

            def h3(t, b, p):
                e.wait_ge(S["h3_ready"], t + 1)
                two_back(e, S["h3_copied"], t)
                turn(bank(2 + b), XA[b]).then_inc(S["h3_turned"], 1)
                e.wait_ge(S["h3_copied"], t + 1)
                two_back(e, S["g0_kept"], t)
                project(bank(4 * b), HTc[b], U[:, 0]).then_inc(S["g0_done"], 1)
                two_back(e, S["g1_kept"], t)
                project(bank(1 + 4 * b), HTc[b], U[:, 1]).then_inc(S["g1_done"], 1)
                two_back(e, S["qk_kept"], t)
                project(bank(6 + b, P), WQK, HTc[b]).then_inc(S["qk_done"], 1)
            tiles(h3)(e)
            end_stage(e, 5)

            def logits(s):
                def body(t, b, p):
                    e.wait_ge(S["q_staged"], NT * s + t + 1)
                    two_back(e, S["exp_done"], t, NT * s)
                    for a, z in CHUNKS:
                        last = e.matmul(ps[:, b * 1536 + a:b * 1536 + z], QS[b][ATTN:, :], QKT[ATTN:, a:z], start=True, stop=True)
                    last.then_inc(S["logits"], 1)
                return body

            def turn_pt(n, b):
                e.wait_ge(S["keep_ready"], n + 1)
                if not isinstance(n, int) or n >= 1:
                    e.wait_ge(S["pt_copied"], n)
                for k in range(NT):
                    last = e.transpose(ps[:, k * P:(k + 1) * P], PT[b][:, k * P:(k + 1) * P], ident)
                last.then_inc(S["pt_turned"], 1)

            def attention(s, t, b, turn_next):
                n = NT * s + t
                e.wait_ge(S["pt_copied"], n + 1)
                if not isinstance(t, int) or t >= 1:
                    e.wait_ge(S["xa_ready" if s else "qk2_kept"], n)
                product(bank(6), STk[b], (F[1], F[3])[s]).then_inc(S["att_done"], 1)
                if turn_next:
                    turn_pt(n + 1, 1 - b)
                if s == 0:
                    e.wait_ge(S["xa_ready"], t + 1)
                    turn(bank(7), XA[0]).then_inc(S["xa_turned"], 1)
                    e.wait_ge(S["xa_copied"], t + 1)
                    e.matmul(bank(6), ident, F[1][:, t, :], start=True, stop=False)
                    for c in range(DC):
                        last = e.matmul(bank(6), HTc[0][:, c, :], U[:, 0][:, c, :], start=False, stop=(c == DC - 1))
                    last.then_inc(S["xu_done"], 1)
                    project(bank(7), HTc[0], U[:, 1]).then_inc(S["g2_done"], 1)
                    e.wait_ge(S["xu_kept"], t + 1)
                    project(bank(6, P), WQK, HTc[0]).then_inc(S["qk2_done"], 1)

            def group_attention(s, a, z):
                turn_pt(NT * s + a, a % 2)
                attention(s, a, a % 2, True)
                pairs = (z - a - 2) // 2
                if pairs:
                    with e.Fori(0, pairs) as i:
                        attention(s, 2 * i + (a + 1), (a + 1) % 2, True)
                        attention(s, 2 * i + (a + 2), a % 2, True)
                for t in range(a + 1 + 2 * pairs, z):
                    attention(s, t, t % 2, t < z - 1)

            for s in range(2):
                tiles(logits(s))(e)
                tiles(adjacency_product(("p3", "p4")[s], (F[3], F[2])[s], 6, ((12, 10), (18, 15))[s], ("p3_scaled", "p4_scaled")[s], True))(e)
                if s == 0:
                    e.wait_ge(S["u_in"], 64)
                for a, _, z in GROUPS[s]:
                    group_attention(s, a, z)
                end_stage(e, 6 + s)
            end_stage(e, 8)
            e.wait_ge(S["wcat_in"], 48)

            def wh(t, b, p):
                e.wait_ge(S["h4_ready"], t + 1)
                two_back(e, S["h4_copied"], t)
                turn(bank(2 + b), XA[b]).then_inc(S["h4_turned"], 1)
                e.wait_ge(S["h4_copied"], t + 1)
                two_back(e, S["wh_kept"], t)
                project(bank(b), HTc[b], Wcat).then_inc(S["wh_done"], 1)
            tiles(wh)(e)
            e.wait_ge(S["scores_kept"], 2 * NT)
            for t in range(NT):
                last = e.transpose(ps[0:8, 4 * 512 + t * P:4 * 512 + (t + 1) * P], ed[:, t, :], ident)
            last.then_inc(S["ed_turned"], 1)
            end_stage(e, 9)
            e.wait_ge(S["ab_ready"], 1)
            for t in range(NT):
                last = e.transpose(ps[0:16, t * P:(t + 1) * P], abc[:, t, :], ident)
            last.then_inc(S["ab_turned"], 1)
            end_stage(e, 10)

            def head(h, b):
                e.wait_ge(S["wh_staged"], h + 1)
                if not isinstance(h, int):
                    e.wait_ge(S["head_kept"], 2 * (h - 1))
                for k in range(NT):
                    e.wait_ge(S["p_exp"], h * NT + (k + 1))
                    for a, z in CHUNKS:
                        last = e.matmul(ps[:, b * 1536 + a:b * 1536 + z], WS[b][:, k, :], PP[k % 4][:, a:z], start=(k == 0), stop=(k == NT - 1))
                    last.then_inc(S["p_used"], 1)
            head(0, 0)
            head(1, 1)
            with e.Fori(1, HEADS // 2) as p:
                head(2 * p, 0)
                head(2 * p + 1, 1)

            e.wait_ge(S["mlp_in"], 96)
            WIDE = [(0, 512), (512, 1024), (1024, NP)]
            e.wait_ge(S["head_kept"], 2 * HEADS)
            e.wait_ge(S["enc_ready"], DC - 1)
            for c in range(DC - 1):
                for m in range(2):
                    for a, z in WIDE:
                        e.matmul(ps[:, m * 1536 + a:m * 1536 + z], m1[:, c, m * P:(m + 1) * P], encT[:, c, a:z], start=(c == 0), stop=False)
            e.wait_ge(S["enc_ready"], DC)
            for m in range(2):
                for a, z in WIDE:
                    last = e.matmul(ps[:, m * 1536 + a:m * 1536 + z], m1[:, DC - 1, m * P:(m + 1) * P], encT[:, DC - 1, a:z], start=False, stop=True)
                last.then_inc(S["o1_done"], 1)
            e.wait_ge(S["o1_kept"], 2)
            for a, z in WIDE:
                for c in range(2):
                    last = e.matmul(ps[:, a:z], m2[:, c, :], o1T[:, c, a:z], start=(c == 0), stop=(c == 1))
            last.then_inc(S["o2_done"], 1)
            e.wait_ge(S["o2_kept"], 1)
            for m in range(2):
                off = (1 - m) * 1536
                for a, z in WIDE:
                    last = e.matmul(ps[:, off + a:off + z], m3[:, m * P:(m + 1) * P], o2T[:, a:z], start=True, stop=True)
                last.then_inc(S["o3_done"], 1)
            e.wait_ge(S["o3_kept"], 2)
            for t in range(NT):
                if t >= 2:
                    e.wait_ge(S["out_a"], t - 1)
                for c in range(2):
                    last = e.matmul(bank(6 + t % 2), o3T[:, c, t * P:(t + 1) * P], m4[:, c, :], start=(c == 0), stop=(c == 1))
                last.then_inc(S["y4_done"], 1)


def kernel(**inputs):
    import numpy as np
    import concourse.bacc as bacc
    from concourse import mybir as mb
    from concourse.bass_utils import run_bass_kernel_spmd as run

    g = {k: np.asarray(v) for k, v in inputs.items()}
    adj = np.pad(g["adj"], ((0, NP - N), (0, NP - N)))
    adjT = np.ascontiguousarray(adj.T)
    broad = lambda v: np.ascontiguousarray(np.broadcast_to(v.reshape(1, -1), (P, v.size)))
    scalars = np.stack([g["L1_gnn_adj_scaling_factor"], g["L1_gnn_wgt_alpha"], g["L1_gnn_act_alpha"],
                        g["L1_gnn_act_alpha2"], g["L1_gnn_act_alpha2"]])
    arrays = {
        "x": np.pad(g["x"], ((0, NP - N), (0, 0))),
        "adj_rows": adj,
        "adjT_rows": adjT,
        "adjT_blocks": np.ascontiguousarray(adjT.reshape(NT, P, NT, P).transpose(2, 1, 0, 3)).reshape(NT, P, NP),
        "scalars": broad(scalars),
        "L1_gnn_weight": g["L1_gnn_weight"],
        "W1T": np.ascontiguousarray(g["L2_gnn_W1"].T),
        "L2_gnn_W2": g["L2_gnn_W2"], "L2_gnn_W3": g["L2_gnn_W3"],
        "L2_gnn_U1_0": g["L2_gnn_U1_0"], "L2_gnn_U1_1": g["L2_gnn_U1_1"],
        "L2_gnn_U2_0": g["L2_gnn_U2_0"], "L2_gnn_U2_1": g["L2_gnn_U2_1"],
        "gamma_b": broad(g["L2_gnn_gamma"]), "beta_b": broad(g["L2_gnn_beta"]),
        "Wcat": np.ascontiguousarray(g["L3_gnn_W"].transpose(1, 0, 2)).reshape(D, HEADS * HD),
        "a1_b": broad(g["L3_gnn_a1"]), "a2_b": broad(g["L3_gnn_a2"]),
        "M1": np.ascontiguousarray(g["L3_gnn_W1"].T), "M2": np.ascontiguousarray(g["L3_gnn_W2"].T),
        "M3": np.ascontiguousarray(g["L3_gnn_W3"].T), "M4": np.ascontiguousarray(g["L3_gnn_W4"].T),
        "b4_b": broad(g["L3_gnn_b4"]),
        "bcols": np.ascontiguousarray(np.concatenate([g["L3_gnn_b1"].reshape(2, P), g["L3_gnn_b2"].reshape(1, P),
                                                      g["L3_gnn_b3"].reshape(2, P)]).T),
    }
    nc = bacc.Bacc("TRN2", target_bir_lowering=False, num_devices=1)
    ins = {n: nc.dram_tensor(n, a.shape, mb.dt.from_np(a.dtype), kind="ExternalInput").ap() for n, a in arrays.items()}
    out = nc.dram_tensor("out", [N, D], F32, kind="ExternalOutput").ap()
    spill = nc.dram_tensor("x_spill", [NP, D], F32, kind="Internal").ap()
    rows = nc.dram_tensor("score_rows", [24, NP], F32, kind="Internal").ap()
    build(nc, ins, out, spill, rows)
    r = run(nc, [arrays], core_ids=[0])
    return r.results[0]["out"]
```
